# Optimizing a Trainium2 kernel written in Bass

```python
import numpy as np
import jax
import jax.numpy as jnp

def _softmax(x, axis=-1):
    return jax.nn.softmax(x, axis=axis)

def _gelu(x):
    return jax.nn.gelu(x, approximate=True)

def _silu(x):
    return jax.nn.silu(x)

def _sigmoid(x):
    return jax.nn.sigmoid(x)

def _layernorm(x, axis=-1, eps=1e-05):
    m = jnp.mean(x, axis=axis, keepdims=True)
    v = jnp.var(x, axis=axis, keepdims=True)
    return (x - m) / jnp.sqrt(v + eps)

def _scatter_add(tgt, idx, src, axis=0):
    return tgt.at[idx].add(src)

def _segment_sum(src, seg, n):
    return jax.ops.segment_sum(src, seg, n)
kernel_name = 'mk_gnn_preln_d4_gnn_r32_bfa8a0'

def setup_inputs(seed: int=0):
    np.random.seed(seed)
    _w = jnp.asarray

    def _rec_inputs():
        import jax
        import jax.numpy as jnp
        _gk = jax.random.key(seed)
        x = -0.0003713 + 1 * jax.random.normal(jax.random.fold_in(_gk, 1), (3125, 128), jnp.float32)
        _s = jax.random.randint(jax.random.fold_in(_gk, 2), (25000,), 0, 3125, jnp.int32)
        _d = jax.random.randint(jax.random.fold_in(_gk, 3), (25000,), 0, 3125, jnp.int32)
        _loop = jnp.arange(3125, dtype=jnp.int32)
        src = jnp.concatenate([_s, _d, _loop])
        dst = jnp.concatenate([_d, _s, _loop])
        _o = jnp.argsort(dst, stable=True)
        src = src[_o]
        dst = dst[_o]
        edge_weight = jax.random.uniform(jax.random.fold_in(_gk, 13), (53125,), jnp.float32, 0.0, 0.999999)
        return (x, src, dst, edge_weight)
    x, src, dst, edge_weight = _rec_inputs()

    def _L0_gnn_setup():
        import jax, jax.numpy as jnp
        import numpy as np
        BN_EPS = 1e-05

        def _sage_conv(x, edge_index, edge_weight, Wl, bl, Wr):
            N = x.shape[0]
            src, dst = (edge_index[0], edge_index[1])
            msg = x[src] * edge_weight[:, None]
            agg = jax.ops.segment_sum(msg, dst, num_segments=N)
            cnt = jax.ops.segment_sum(jnp.ones_like(edge_weight), dst, num_segments=N)
            agg = agg / jnp.maximum(cnt, 1.0)[:, None]
            return agg @ Wl.T + bl + x @ Wr.T

        def _batchnorm(x, gamma, beta):
            mean = x.mean(axis=0)
            var = x.var(axis=0)
            return (x - mean) * jax.lax.rsqrt(var + BN_EPS) * gamma + beta
        key = jax.random.key(seed)
        ks = jax.random.split(key, 8)
        N, E, C = (3125, 50000, 128)
        x = jax.random.normal(ks[0], (N, C), dtype=jnp.float32)
        edge_index = jax.random.randint(ks[1], (2, E), 0, N, dtype=jnp.int64)
        edge_weight = jax.random.uniform(ks[2], (E,), dtype=jnp.float32)
        s = 0.05
        return {'x': x, 'edge_index': edge_index, 'edge_weight': edge_weight, 'W1l': jax.random.normal(ks[3], (C, C), dtype=jnp.float32) * s, 'b1l': jnp.zeros((C,), dtype=jnp.float32), 'W1r': jax.random.normal(ks[4], (C, C), dtype=jnp.float32) * s, 'bn_gamma': jnp.ones((C,), dtype=jnp.float32), 'bn_beta': jnp.zeros((C,), dtype=jnp.float32), 'W2l': jax.random.normal(ks[5], (C, C), dtype=jnp.float32) * s, 'b2l': jnp.zeros((C,), dtype=jnp.float32), 'W2r': jax.random.normal(ks[6], (C, C), dtype=jnp.float32) * s}
    _L0_gnn_all = _L0_gnn_setup()
    _L0_gnn_in = {k: v for k, v in _L0_gnn_all.items() if k in ('W1l', 'b1l', 'W1r', 'bn_gamma', 'bn_beta', 'W2l', 'b2l', 'W2r')}
    del _L0_gnn_all

    def _L1_gnn_setup():
        import jax, jax.numpy as jnp
        import numpy as np
        N_NODES = 3125
        N_EDGES = 50000
        D_IN = 128
        D_OUT = 128
        key = jax.random.key(seed)
        k1, k2, k3, k4, k5, k6 = jax.random.split(key, 6)
        x = jax.random.normal(k1, (N_NODES, D_IN), dtype=jnp.float32)
        scale = 1.0 / np.sqrt(D_IN)
        W = jax.random.normal(k2, (D_IN, D_OUT), dtype=jnp.float32) * scale
        b = jax.random.normal(k3, (D_OUT,), dtype=jnp.float32) * scale
        edge_val = jax.random.uniform(k4, (N_EDGES,), dtype=jnp.float32)
        edge_row = jax.random.randint(k5, (N_EDGES,), 0, N_NODES, dtype=jnp.int64)
        edge_col = jax.random.randint(k6, (N_EDGES,), 0, N_NODES, dtype=jnp.int64)
        return {'x': x, 'W': W, 'b': b, 'edge_val': edge_val, 'edge_row': edge_row, 'edge_col': edge_col}
    _L1_gnn_all = _L1_gnn_setup()
    _L1_gnn_in = {k: v for k, v in _L1_gnn_all.items() if k in ('W', 'b')}
    del _L1_gnn_all

    def _L2_gnn_setup():
        import jax, jax.numpy as jnp
        import numpy as np
        N = 3125
        E = 50000
        L = 128
        H = 128
        O = 128

        def _gcn_conv(x, W, b, src, dst, norm, n_nodes):
            h = x @ W
            msg = h[src] * norm[:, None]
            out = jax.ops.segment_sum(msg, dst, num_segments=n_nodes)
            return out + b

        def _lstm_step(z, W_ih, W_hh, b_ih, b_hh):
            gates = z @ W_ih.T + jnp.zeros((1, H), z.dtype) @ W_hh.T + b_ih + b_hh
            i, f, g, o = jnp.split(gates, 4, axis=-1)
            c = jax.nn.sigmoid(i) * jnp.tanh(g)
            return jax.nn.sigmoid(o) * jnp.tanh(c)
        key = jax.random.key(seed)
        ks = jax.random.split(key, 16)
        s = 1.0 / np.sqrt(H)
        inp = {'z': jax.random.normal(ks[0], (N, L), dtype=jnp.float32), 'edge_index': jax.random.randint(ks[1], (2, E), 0, N, dtype=jnp.int64), 'W_ih': jax.random.uniform(ks[2], (4 * H, L), jnp.float32, -s, s), 'W_hh': jax.random.uniform(ks[3], (4 * H, H), jnp.float32, -s, s), 'b_ih': jax.random.uniform(ks[4], (4 * H,), jnp.float32, -s, s), 'b_hh': jax.random.uniform(ks[5], (4 * H,), jnp.float32, -s, s), 'W1': jax.random.uniform(ks[6], (H, H), jnp.float32, -s, s), 'b1': jnp.zeros((H,), jnp.float32), 'W2': jax.random.uniform(ks[7], (H, H), jnp.float32, -s, s), 'b2': jnp.zeros((H,), jnp.float32), 'W3': jax.random.uniform(ks[8], (O, H), jnp.float32, -s, s), 'b3': jax.random.uniform(ks[9], (O,), jnp.float32, -s, s)}
        return inp
    _L2_gnn_all = _L2_gnn_setup()
    _L2_gnn_in = {k: v for k, v in _L2_gnn_all.items() if k in ('W_ih', 'W_hh', 'b_ih', 'b_hh', 'W1', 'b1', 'W2', 'b2', 'W3', 'b3')}
    del _L2_gnn_all

    def _L3_gnn_setup():
        import jax, jax.numpy as jnp
        import numpy as np
        N_NODES = 3125
        N_EDGES = 50000
        D = 128
        K = 2
        ALPHA = 0.5

        def _appnp(x, edge_index):
            n = x.shape[0]
            loops = jnp.arange(n, dtype=edge_index.dtype)
            src = jnp.concatenate([edge_index[0], loops])
            dst = jnp.concatenate([edge_index[1], loops])
            ew = jnp.ones_like(src, dtype=x.dtype)
            deg = jax.ops.segment_sum(ew, dst, num_segments=n)
            dinv = jnp.where(deg > 0, jax.lax.rsqrt(deg), 0.0)
            norm = dinv[src] * ew * dinv[dst]
            h = x
            for _ in range(K):
                msg = norm[:, None] * x[src]
                agg = jax.ops.segment_sum(msg, dst, num_segments=n)
                x = (1.0 - ALPHA) * agg + ALPHA * h
            return x
        key = jax.random.key(seed)
        ks = jax.random.split(key, 5)
        x = jax.random.normal(ks[0], (N_NODES, D), dtype=jnp.float32)
        edge_index = jax.random.randint(ks[1], (2, N_EDGES), 0, N_NODES, dtype=jnp.int32)
        s = 1.0 / np.sqrt(D)
        w1 = jax.random.uniform(ks[2], (D, D), jnp.float32, -s, s)
        b1 = jnp.zeros((D,), jnp.float32)
        w2 = jax.random.uniform(ks[3], (D, D), jnp.float32, -s, s)
        b2 = jnp.zeros((D,), jnp.float32)
        return {'x': x, 'edge_index': edge_index, 'w1': w1, 'b1': b1, 'w2': w2, 'b2': b2}
    _L3_gnn_all = _L3_gnn_setup()
    _L3_gnn_in = {k: v for k, v in _L3_gnn_all.items() if k in ('w1', 'b1', 'w2', 'b2')}
    del _L3_gnn_all
    return {'x': x, 'src': src, 'dst': dst, 'edge_weight': edge_weight, 'L0_gnn_W1l': _L0_gnn_in['W1l'], 'L0_gnn_b1l': _L0_gnn_in['b1l'], 'L0_gnn_W1r': _L0_gnn_in['W1r'], 'L0_gnn_bn_gamma': _L0_gnn_in['bn_gamma'], 'L0_gnn_bn_beta': _L0_gnn_in['bn_beta'], 'L0_gnn_W2l': _L0_gnn_in['W2l'], 'L0_gnn_b2l': _L0_gnn_in['b2l'], 'L0_gnn_W2r': _L0_gnn_in['W2r'], 'L1_gnn_W': _L1_gnn_in['W'], 'L1_gnn_b': _L1_gnn_in['b'], 'L2_gnn_W_ih': _L2_gnn_in['W_ih'], 'L2_gnn_W_hh': _L2_gnn_in['W_hh'], 'L2_gnn_b_ih': _L2_gnn_in['b_ih'], 'L2_gnn_b_hh': _L2_gnn_in['b_hh'], 'L2_gnn_W1': _L2_gnn_in['W1'], 'L2_gnn_b1': _L2_gnn_in['b1'], 'L2_gnn_W2': _L2_gnn_in['W2'], 'L2_gnn_b2': _L2_gnn_in['b2'], 'L2_gnn_W3': _L2_gnn_in['W3'], 'L2_gnn_b3': _L2_gnn_in['b3'], 'L3_gnn_w1': _L3_gnn_in['w1'], 'L3_gnn_b1': _L3_gnn_in['b1'], 'L3_gnn_w2': _L3_gnn_in['w2'], 'L3_gnn_b2': _L3_gnn_in['b2']}

def reference(x, src, dst, edge_weight, L0_gnn_W1l, L0_gnn_b1l, L0_gnn_W1r, L0_gnn_bn_gamma, L0_gnn_bn_beta, L0_gnn_W2l, L0_gnn_b2l, L0_gnn_W2r, L1_gnn_W, L1_gnn_b, L2_gnn_W_ih, L2_gnn_W_hh, L2_gnn_b_ih, L2_gnn_b_hh, L2_gnn_W1, L2_gnn_b1, L2_gnn_W2, L2_gnn_b2, L2_gnn_W3, L2_gnn_b3, L3_gnn_w1, L3_gnn_b1, L3_gnn_w2, L3_gnn_b2):
    import jax
    import jax.numpy as jnp

    def _L0_gnn_ref(x, edge_index, edge_weight, W1l, b1l, W1r, bn_gamma, bn_beta, W2l, b2l, W2r):
        import jax, jax.numpy as jnp
        import numpy as np
        BN_EPS = 1e-05

        def _sage_conv(x, edge_index, edge_weight, Wl, bl, Wr):
            N = x.shape[0]
            src, dst = (edge_index[0], edge_index[1])
            msg = x[src] * edge_weight[:, None]
            agg = jax.ops.segment_sum(msg, dst, num_segments=N)
            cnt = jax.ops.segment_sum(jnp.ones_like(edge_weight), dst, num_segments=N)
            agg = agg / jnp.maximum(cnt, 1.0)[:, None]
            return agg @ Wl.T + bl + x @ Wr.T

        def _batchnorm(x, gamma, beta):
            mean = x.mean(axis=0)
            var = x.var(axis=0)
            return (x - mean) * jax.lax.rsqrt(var + BN_EPS) * gamma + beta
        h = _sage_conv(x, edge_index, edge_weight, W1l, b1l, W1r)
        h = _batchnorm(h, bn_gamma, bn_beta)
        h = jax.nn.relu(h)
        out = _sage_conv(h, edge_index, edge_weight, W2l, b2l, W2r)
        return out

    def _L1_gnn_ref(x, W, b, edge_val, edge_row, edge_col):
        import jax, jax.numpy as jnp
        import numpy as np
        N_NODES = 3125
        N_EDGES = 50000
        D_IN = 128
        D_OUT = 128
        support = x @ W + b
        gathered = support[edge_col] * edge_val[:, None]
        out = jax.ops.segment_sum(gathered, edge_row, num_segments=x.shape[0])
        return out

    def _L2_gnn_ref(z, edge_index, W_ih, W_hh, b_ih, b_hh, W1, b1, W2, b2, W3, b3):
        import jax, jax.numpy as jnp
        import numpy as np
        N = 3125
        E = 50000
        L = 128
        H = 128
        O = 128

        def _gcn_conv(x, W, b, src, dst, norm, n_nodes):
            h = x @ W
            msg = h[src] * norm[:, None]
            out = jax.ops.segment_sum(msg, dst, num_segments=n_nodes)
            return out + b

        def _lstm_step(z, W_ih, W_hh, b_ih, b_hh):
            gates = z @ W_ih.T + jnp.zeros((1, H), z.dtype) @ W_hh.T + b_ih + b_hh
            i, f, g, o = jnp.split(gates, 4, axis=-1)
            c = jax.nn.sigmoid(i) * jnp.tanh(g)
            return jax.nn.sigmoid(o) * jnp.tanh(c)
        n = z.shape[0]
        loop = jnp.arange(n, dtype=edge_index.dtype)
        src = jnp.concatenate([edge_index[0], loop])
        dst = jnp.concatenate([edge_index[1], loop])
        deg = jax.ops.segment_sum(jnp.ones_like(dst, dtype=z.dtype), dst, num_segments=n)
        dinv = jnp.where(deg > 0, jax.lax.rsqrt(deg), 0.0)
        norm = dinv[src] * dinv[dst]
        h = _lstm_step(z, W_ih, W_hh, b_ih, b_hh)
        x = jax.nn.relu(_gcn_conv(h, W1, b1, src, dst, norm, n))
        x = _gcn_conv(x, W2, b2, src, dst, norm, n)
        return jax.nn.relu(x @ W3.T + b3)

    def _L3_gnn_ref(x, edge_index, w1, b1, w2, b2):
        import jax, jax.numpy as jnp
        import numpy as np
        N_NODES = 3125
        N_EDGES = 50000
        D = 128
        K = 2
        ALPHA = 0.5

        def _appnp(x, edge_index):
            n = x.shape[0]
            loops = jnp.arange(n, dtype=edge_index.dtype)
            src = jnp.concatenate([edge_index[0], loops])
            dst = jnp.concatenate([edge_index[1], loops])
            ew = jnp.ones_like(src, dtype=x.dtype)
            deg = jax.ops.segment_sum(ew, dst, num_segments=n)
            dinv = jnp.where(deg > 0, jax.lax.rsqrt(deg), 0.0)
            norm = dinv[src] * ew * dinv[dst]
            h = x
            for _ in range(K):
                msg = norm[:, None] * x[src]
                agg = jax.ops.segment_sum(msg, dst, num_segments=n)
                x = (1.0 - ALPHA) * agg + ALPHA * h
            return x
        x = jax.nn.relu(_appnp(x, edge_index))
        x = x @ w1.T + b1
        x = x @ w2.T + b2
        return x
    edge_index = jnp.stack([src, dst])
    h = jnp.maximum(_layernorm(x, axis=-1), 0.0)
    x = x + _L0_gnn_ref(h, edge_index, edge_weight, L0_gnn_W1l, L0_gnn_b1l, L0_gnn_W1r, L0_gnn_bn_gamma, L0_gnn_bn_beta, L0_gnn_W2l, L0_gnn_b2l, L0_gnn_W2r)
    h = jnp.maximum(_layernorm(x, axis=-1), 0.0)
    x = x + _L1_gnn_ref(h, L1_gnn_W, L1_gnn_b, edge_weight, src, dst)
    h = jnp.maximum(_layernorm(x, axis=-1), 0.0)
    x = x + _L2_gnn_ref(h, edge_index, L2_gnn_W_ih, L2_gnn_W_hh, L2_gnn_b_ih, L2_gnn_b_hh, L2_gnn_W1, L2_gnn_b1, L2_gnn_W2, L2_gnn_b2, L2_gnn_W3, L2_gnn_b3)
    h = jnp.maximum(_layernorm(x, axis=-1), 0.0)
    x = x + _L3_gnn_ref(h, edge_index, L3_gnn_w1, L3_gnn_b1, L3_gnn_w2, L3_gnn_b2)
    return x

_drawn_inputs = setup_inputs


def setup_inputs(seed=0):
    import zlib

    import numpy as np

    out = dict(_drawn_inputs(seed))
    spreads = {'L0_gnn_b1l': (0.0, 2.0),
     'L0_gnn_bn_gamma': (1.0, 0.2),
     'L0_gnn_bn_beta': (0.0, 0.1),
     'L0_gnn_b2l': (0.0, 0.1),
     'L2_gnn_b1': (0.0, 0.8),
     'L2_gnn_b2': (0.0, 0.8),
     'L3_gnn_b1': (0.0, 0.533),
     'L3_gnn_b2': (0.0, 0.346)}
    factors = {'L2_gnn_W_ih': 8.0,
     'L2_gnn_b_ih': 8.0,
     'L2_gnn_b_hh': 8.0,
     'L2_gnn_W1': 8.0,
     'L2_gnn_W2': 8.0,
     'L2_gnn_W3': 7.271,
     'L2_gnn_b3': 6.927,
     'L0_gnn_W1l': 4.022}
    for name, (base, spread) in spreads.items():
        noise = np.random.default_rng([zlib.crc32(name.encode()), seed]).standard_normal(out[name].shape)
        drawn = base * np.exp(spread * noise) if base else spread * noise
        out[name] = jnp.asarray(drawn.astype(out[name].dtype))
    for name, factor in factors.items():
        out[name] = (out[name] * factor).astype(out[name].dtype)
    return out
```

```python
from contextlib import ExitStack

import concourse.bass as bass
from concourse import mybir

F32 = mybir.dt.float32
BF16 = mybir.dt.bfloat16
I32 = mybir.dt.int32
ALU = mybir.AluOpType
ACT = mybir.ActivationFunctionType
ds = bass.ds
P = 128
V = 8
ROW = 256
STEP = 32
BANK = 512


def gnn_blocks(nc, x, src, dst, edge_weight, weights, weight_at, biases, bias_at, columns, out):
    N, D = x.shape
    E, = src.shape
    NT = -(-N // P)
    NR = N - P * (NT - 1)
    NW = -(-N // (2 * V)) * 2
    NC = NW * V
    LC = NC - P * (NT - 1)
    CODE = V * NT
    G = 4
    NPT = P // (2 * V)
    NPL = LC // (2 * V)
    NCH = -(-E // P)
    NCB = -(-NCH // 8)
    LASTROW = (E - ROW) // STEP + 1
    NROWS = LASTROW + 1
    NG = -(-NT // 4)
    BANKS = [(c, min(BANK, NC - c)) for c in range(0, NC, BANK)]
    HALF = BANK * (len(BANKS) // 2)
    HALVES = [(0, HALF), (HALF, NC - HALF)]
    STREAM = max(HALF, NC - HALF)
    RESTS = [(c, min(2 * BANK, NC - c)) for c in range(0, NC, 2 * BANK)]
    assert len(RESTS) % 2 == 0
    EPS = 1e-5
    assert D == P and NT % 6 == 1 and NW <= G * P and NCH <= BANK and NR <= LC < P and LC % (2 * V) == 0
    SETUP = 14000
    assert 7 * BANK >= NC and 2 * CODE <= BANK and LC == P // 2

    edge_rows = nc.dram_tensor("edge_rows", (NROWS, 3 * ROW), I32).ap()
    AT = nc.dram_tensor("AT", (NT, P, NC), F32).ap()
    A = nc.dram_tensor("A", (NT, P, NT * P), F32).ap()
    count_rest = nc.dram_tensor("count_rest", (NT, P, NC), BF16).ap()

    with ExitStack() as ctx:
        arena = ctx.enter_context(nc.sbuf_tensor("arena", [P, 53208], F32))
        PS = ctx.enter_context(nc.psum_tensor("PS", [P, 8 * BANK], F32))
        at = [0]

        def take(words):
            at[0] += words
            assert at[0] <= 53208, at[0]
            return arena[:, at[0] - words:at[0]]

        scratch0 = at[0]
        C = take(max(NT * NC // 2, SETUP))[:, 0:NT * NC // 2].bitcast(BF16)
        setup_end = at[0]
        ident = take(P)
        iota = take(-(-max(CODE, P) // 2)).bitcast(BF16)
        identb = take(P // 2).bitcast(BF16)
        ones = take(1)
        onesb = take(1).bitcast(BF16)
        count = take(NT)
        rcount = take(NT)
        dinv = take(NT)
        half_dinv = take(NT)
        flag = take(1)
        region = at[0]

        W5 = 2 * NW
        t_code, t_src = [take(W5) for _ in range(2)]
        t_w = take(3 * W5 // 2).bitcast(BF16).rearrange("p (k h v) -> p h k v", k=3, h=2)
        PLACE = 2 * 4 * P + 2 * CODE
        places = [take(PLACE // 2).bitcast(BF16) for _ in range(4)]
        hots = [m[:, 0:2 * P] for m in places]
        hot = [[m[:, s * P:(s + 1) * P] for s in (0, 1)] for m in places]
        hots_w = [m[:, 2 * P:8 * P] for m in places]
        hot_w = [[[m[:, (2 + 3 * s + k) * P:(3 + 3 * s + k) * P] for k in range(3)] for s in (0, 1)] for m in places]
        code_hot = [[m[:, 8 * P + s * CODE:8 * P + (s + 1) * CODE] for s in (0, 1)] for m in places]
        piece = [take(BANK) for _ in range(2)]
        staged = [take(NT * P) for _ in range(2)]
        rest_stage = take(NT * V).bitcast(BF16)
        zerosb = take(max(CODE, P // 2)).bitcast(BF16)
        degree_row = take(P)

        at[0] = scratch0
        gathered = take(G * 3 * ROW).bitcast(I32)
        firsts_i = take(BANK).bitcast(I32)
        firsts = take(BANK)
        onesrow = take(P)
        firsts_all = take(BANK)
        below = take(BANK)
        iota_w = take(P).bitcast(I32)
        theta_i = take(G).bitcast(I32)
        theta = take(G)
        theta_nt = take(G)
        chunks_below = take(G)
        row0 = take(G)
        row_i = take(G).bitcast(I32)
        base0 = take(G)
        fine = take(G)
        start = take(G)
        start_i = take(G).bitcast(I32)
        last_or = take(G)
        row1 = take(G)
        row1_i = take(G).bitcast(I32)
        dstf = take(G * ROW)
        tile_i = take(G * ROW).bitcast(I32)
        tilef = take(G * ROW)
        low_i = take(G * ROW).bitcast(I32)
        lowf = take(G * ROW)
        codef = take(G * ROW)
        inside = take(G * ROW)
        inside2 = take(G * ROW)
        hits = take(1)
        total = take(1)
        assert at[0] <= setup_end
        at[0] = region
        NCP = 8 * NCB
        l_code, l_src, l_dst = [take(NCP) for _ in range(3)]
        l_w = take(3 * NCP // 2).bitcast(BF16).rearrange("p (k c) -> p c k", k=3)
        assert at[0] <= region + 2 * W5 + 3 * W5 // 2
        list_i = staged[0][:, 0:2 * NCP].bitcast(I32)
        list_w = staged[0][:, 2 * NCP:3 * NCP]
        list_t = staged[0][:, 3 * NCP:4 * NCP].bitcast(I32)
        w_left = staged[1][:, 0:W5]

        at[0] = region
        X = take(NT * P)
        H = take(NT * P)
        big = take(max(3 * STREAM, 3 * NT * P // 2, NC))
        stream = [big[:, i * STREAM:(i + 1) * STREAM] for i in range(3)]
        bn_in = big[:, 0:NC]
        parts = big[:, 0:3 * NT * P // 2].bitcast(BF16)
        over_parts = big[:, 3 * NT * P // 2 - NC:3 * NT * P // 2]
        assert 3 * NT * P // 2 - NC >= NT * P // 2
        wslot = take(3 * P)
        bslot = take(3 * P)
        work = take(12 * P)
        mv = take(2 * NT)
        rstd = take(NT)
        nmr = take(NT)
        gamma, beta, bn_scale, bn_shift, b1col = [take(1) for _ in range(5)]
        bn_mv = take(2)
        ag = [work[:, i * P:(i + 1) * P] for i in (0, 1)]
        hb = [work[:, i * P:(i + 1) * P] for i in (2, 3)]
        hT = [work[:, i * P:(i + 1) * P] for i in (4, 5)]
        tmp = [work[:, i * P:(i + 1) * P] for i in (6, 7)]
        stat6 = work[:, 8 * P:8 * P + 6 * NT]
        gates_io = [work[:, 8 * P:10 * P], work[:, 10 * P:12 * P]]
        gates_g = ag
        stationary = [work[:, i * P:(i + 1) * P] for i in range(3)]
        rest_in = [work[:, i * BANK:(i + 1) * BANK].bitcast(BF16) for i in range(2)]
        whh = big[:, 0:3 * P]
        bihh = big[:, 3 * P:9 * P]
        zeros = big[:, 9 * P:10 * P]
        w = [wslot[:, i * P:(i + 1) * P] for i in range(3)]
        b = [bslot[:, i * P:(i + 1) * P] for i in range(3)]

        agg = PS[:, 0:7 * BANK]
        misc = [PS[:, k * BANK:k * BANK + P] for k in range(8)]
        gates_out = [PS[:, k * BANK:k * BANK + 3 * P] for k in (4, 5)]
        gate_prod_out = PS[:, 6 * BANK:6 * BANK + 3 * P]

        def sem(name):
            return ctx.enter_context(nc.semaphore(name))

        def tile(buf, t, n=P):
            return buf[:, ds(t * P, n)] if not isinstance(t, int) else buf[:, t * P:t * P + n]

        def part(k, t):
            return cols(parts, (3 * t + k) * P, P)

        def col(buf, c):
            return buf[:, ds(c, 1)] if not isinstance(c, int) else buf[:, c:c + 1]

        def cols(buf, c, n):
            return buf[:, ds(c, n)] if not isinstance(c, int) else buf[:, c:c + n]

        class Mark:
            def __init__(self, s, base):
                self.sem, self.base = s, base

        stages = {}

        def stage(name, step=NT):
            if name not in stages:
                stages[name] = [sem(name), 2]
            s, base = stages[name]
            stages[name][1] += step
            return Mark(s, base)

        def finished(eng, m, t):
            eng.wait_ge(m.sem, m.base + t + 1)

        def two_back(eng, m, t):
            eng.wait_ge(m.sem, m.base + t - 1)

        counts = {}

        def mark(name, step):
            if name not in counts:
                counts[name] = [sem(name), 0]
            s, base = counts[name]
            counts[name][1] += step
            return Mark(s, base)

        def tiles(eng, body):
            with eng.Fori(0, NT // 2) as i:
                body(2 * i, 0, P)
                body(2 * i + 1, 1, P)
            body(NT - 1, 0, LC)

        edges_in = sem("edges_in")
        firsts_in = sem("firsts_in")
        pool_const = sem("pool_const")
        dve_chain = sem("dve_chain")
        all_chain = sem("all_chain")
        firsts_ready = sem("firsts_ready")
        firsts_spread = sem("firsts_spread")
        rows_ready = sem("rows_ready")
        gather0 = sem("gather0")
        gather1 = sem("gather1")
        codes_ready = sem("codes_ready")
        tables_turned = sem("tables_turned")
        hits_ready = sem("hits_ready")
        hits_summed = sem("hits_summed")
        flag_ready = sem("flag_ready")
        tables_ready = sem("tables_ready")
        list_in = sem("list_in")
        list_ready = sem("list_ready")
        hots_ready = sem("hots_ready")
        scaled_ready = sem("scaled_ready")
        slots_used = sem("slots_used")
        row_ready = sem("row_ready")
        row_out = sem("row_out")
        pairs_out = stage("pairs_out").sem
        rest_out = sem("rest_out")
        rest_saved = sem("rest_saved")
        rest_free = sem("rest_free")
        shifted = sem("shifted")
        stage_saved = [sem("stage_saved0"), sem("stage_saved1")]
        tile_turned = stage("tile_turned").sem
        turned = stage("groups_turned").sem
        turned_out = sem("turned_out")
        piece_saved = [sem("piece_saved0"), sem("piece_saved1")]
        counted = sem("counted")
        build_over = sem("build_over")
        act_over = sem("act_over")
        root_ready = sem("root_ready")
        degrees_ready = sem("degrees_ready")

        def pairs_before(t):
            return t * NPT

        def pairs_in(t):
            return NPL if isinstance(t, int) and t == NT - 1 else NPT

        def build_tiles(eng, body):
            for t in range(3):
                body(t, t % 2)
            with eng.Fori(1, (NT - 3) // 2) as i:
                body(2 * i + 1, 1)
                body(2 * i + 2, 0)
            body(NT - 2, 1)
            body(NT - 1, 0)

        def pair_loop(eng, t, first, body):
            q0 = pairs_before(t)
            with eng.Fori(0, (pairs_in(t) - first) // 2) as i:
                body(q0 + first + 2 * i, 0)
                body(q0 + first + 2 * i + 1, 1)

        def pairs_and_groups(t, pair, group):
            pairs, before = pairs_in(t), not isinstance(t, int) or t >= 1
            for k in range(pairs):
                pair(pairs_before(t) + k, k)
                if before and 0 < k <= NG:
                    group(t - 1, k - 1)
            for g in range(pairs - 1, NG):
                if before:
                    group(t - 1, g)

        def list_batches(eng, body):
            with eng.Fori(0, NW) as win:
                with eng.Fori(0, NCB) as i:
                    for r in range(4):
                        body((4 * NCB) * win + 4 * i + r, r, 8 * i + 2 * r)

        def irregular_flag(eng):
            eng.wait_ge(flag_ready, 1)
            return eng.value_load(flag.bitcast(I32)[0:1, 0:1], min_val=0, max_val=1)

        x_in = sem("x_in")
        wload = {k: sem("w_" + k) for k in ("p0", "e0", "p1", "e1", "p2", "p3", "bias3", "e3", "e4", "e6a", "e6b", "small")}

        class Pass:
            def __init__(self, streamed):
                self.done = mark("agg_done", 1)
                self.out = mark("agg_out", len(BANKS))
                if streamed:
                    self.loaded = [mark(f"unit_loaded{i}", 16 * len(range(i, 2 * NT, 3))) for i in range(3)]
                    self.units = mark("units_used", 2 * NT)
                    self.stat = mark("stationary_ready", NT)
                else:
                    self.rest_loaded = [mark(f"rest_loaded{i}", 16 * NT * len(RESTS) // 2) for i in range(2)]
                    self.rest_used = mark("rest_used", len(RESTS) * NT)

        agg0, agg1, agg2 = Pass(True), Pass(True), Pass(True)
        agg3, agg4, agg5, agg6 = [Pass(False) for _ in range(4)]

        def norm_marks():
            return [mark("norm_" + k, 1) for k in ("var", "root", "ready")]

        n0, n1, n2, n4 = norm_marks(), norm_marks(), norm_marks(), norm_marks()
        p0 = [stage(k) for k in ("relu", "turned", "hT", "prod", "out", "kept")]
        e0 = [stage(k) for k in ("copied", "prod", "sum", "turned", "act_out")]
        bn_var, bn_root, bn_ready = sem("bn_var"), sem("bn_root"), sem("bn_ready")
        p1 = [stage(k) for k in ("relu", "prod", "out")]
        p1_x = sem("p1_x")
        h_cleared = sem("h_cleared")
        e1 = [stage(k) for k in ("copied", "prod", "out")]
        p2 = [stage(k) for k in ("relu", "turned", "hT", "prod", "out")]
        e2 = [stage(k) for k in ("copied", "turned", "out")]
        p3 = [stage(k) for k in ("relu", "turned", "hT", "gates", "biased", "acts", "cell", "tanh", "out")]
        gate_prod, gate_bias, gate_ready = sem("gate_prod"), sem("gate_bias"), sem("gate_ready")
        e3 = [stage(k) for k in ("copied", "prod", "out")]
        e4 = [stage(k) for k in ("copied", "prod", "sum", "turned", "act_hT", "prod3", "out")]
        p4 = [stage(k) for k in ("relu", "out")]
        e5 = [stage(k) for k in ("copied", "turned", "out")]
        e6 = [stage(k) for k in ("copied", "turned", "sum", "turned2", "act_hT", "prod3", "tT", "prod2", "out")]
        out_saved = sem("out_saved")

        def evacuate(eng, copy, a, dest, first):
            agg_end(eng, a)
            for c, m in BANKS[first::2]:
                copy(dest[:, c:c + m], agg[:, c:c + m]).then_inc(a.out.sem, 1)

        def agg_end(eng, a):
            eng.wait_ge(a.done.sem, a.done.base + 1)

        block = ctx.enter_context(nc.Block())

        @block.sync
        def _(sp):
            for s, _ in stages.values():
                sp.sem_inc(s, 2)
            sp.sem_inc(slots_used, 4)
            sp.sem_inc(shifted, 1)
            sp.sem_inc(rest_free, 1)
            sp.sem_inc(agg0.units.sem, 6)
            sp.sem_inc(agg3.rest_used.sem, 2)
            for k, v in enumerate((src, dst, edge_weight.bitcast(I32))):
                sp.dma_start(edge_rows[0:LASTROW, k * ROW:(k + 1) * ROW],
                             bass.AP(v.tensor, 0, [[STEP, LASTROW], [1, ROW]])).then_inc(edges_in, 16)
                sp.dma_start(edge_rows[LASTROW:NROWS, k * ROW:(k + 1) * ROW],
                             bass.AP(v.tensor, E - ROW, [[ROW, 1], [1, ROW]])).then_inc(edges_in, 16)
            sp.dma_start(firsts_i[0:1, 0:NCH], bass.AP(dst.tensor, 0, [[1, 1], [P, NCH]]), allow_slow_non_contiguous=True).then_inc(firsts_in, 16)

            irregular = irregular_flag(sp)
            with sp.If(irregular != 0):
                n = NCH if E % P == 0 else NCH - 1
                dests = (list_i[:, NCP:2 * NCP], list_i[:, 0:NCP], list_w)
                sp.wait_ge(tables_ready, 1)
                for v, d in zip((src, dst, edge_weight), dests):
                    sp.dma_start(d[:, 0:n], bass.AP(v.tensor, 0, [[1, P], [P, n]]),
                                 allow_slow_non_contiguous=True).then_inc(list_in, 16)
                    if E % P:
                        sp.dma_start(d[0:E % P, n:n + 1], bass.AP(v.tensor, n * P, [[1, E % P], [1, 1]])).then_inc(list_in, 16)

            def save_rest(q, _):
                sp.wait_ge(rest_out, q + 1)
                sp.dma_start(count_rest[:, :, ds(q * 2 * V, 2 * V)].rearrange("a p d -> p a d"),
                             rest_stage.rearrange("p (a d) -> p a d", a=NT)).then_inc(rest_saved, 16)
                sp.wait_ge(rest_saved, 16 * (q + 1))
                sp.sem_inc(rest_free, 1)

            def save_group(t, g):
                n = LC if isinstance(t, int) and t == NT - 1 else P
                a_rows = A[ds(t, 1), 0:n, :] if not isinstance(t, int) else A[t:t + 1, 0:n, :]
                m = min(BANK, NT * P - g * BANK)
                sp.wait_ge(turned_out, NG * t + g + 1)
                sp.dma_start(a_rows[:, :, g * BANK:g * BANK + m].rearrange("a p s -> (a p) s"),
                             piece[g % 2][0:n, 0:m]).then_inc(piece_saved[g % 2], 16)

            def save_tile(t, p, rest):
                pairs_and_groups(t, save_rest if rest else lambda q, k: None, save_group)
                n = LC if isinstance(t, int) and t == NT - 1 else P
                sp.wait_ge(pairs_out, 2 + pairs_before(t) + pairs_in(t))
                at_cols = AT[:, :, ds(t * P, n)] if not isinstance(t, int) else AT[:, :, t * P:t * P + n]
                sp.dma_start(at_cols.rearrange("a p d -> p a d"),
                             staged[p].rearrange("p (a d) -> p a d", a=NT)[:, :, 0:n]).then_inc(stage_saved[p], 16)

            def save_last():
                for g in range(NG):
                    save_group(NT - 1, g)

            with sp.If(irregular != 0):
                build_tiles(sp, lambda t, p: save_tile(t, p, True))
                save_last()
                sp.wait_ge(shifted, NW + NT + 1)
            with sp.Else():
                build_tiles(sp, lambda t, p: save_tile(t, p, False))
                save_last()
            sp.wait_ge(stage_saved[0], 16 * (NT // 2 + 1))
            sp.wait_ge(stage_saved[1], 16 * (NT // 2))
            sp.wait_ge(piece_saved[0], 16 * NT * ((NG + 1) // 2))
            sp.wait_ge(piece_saved[1], 16 * NT * (NG // 2))
            sp.wait_ge(counted, 1)
            sp.wait_ge(act_over, 1)
            sp.sem_inc(build_over, 1)

            def load_x(s):
                sp.dma_start(X[:, 0:(NT - 1) * P].rearrange("p (t d) -> p t d", t=NT - 1),
                             x[0:(NT - 1) * P, :].rearrange("(t p) d -> p t d", p=P)).then_inc(s, 16)
                sp.dma_start(X[0:NR, (NT - 1) * P:NT * P], x[(NT - 1) * P:N, :]).then_inc(s, 16)

            def load_w(slot, names, s):
                i = weight_at[names[0]]
                sp.dma_start(wslot[:, slot * P:(slot + len(names)) * P], weights[:, i * P:(i + len(names)) * P]).then_inc(s, 16)

            def load_b(slot, name, s):
                i = bias_at[name]
                sp.dma_start(b[slot], bass.AP(biases.tensor, i * P, [[0, P], [1, P]])).then_inc(s, 16)

            sp.wait_ge(h_cleared, 1)
            load_x(x_in)
            load_w(0, ["W1r"], wload["p0"])
            load_b(0, "b1l", wload["p0"])
            load_w(1, ["W1l"], wload["e0"])
            load_w(2, ["W2r"], wload["p1"])
            load_b(1, "b2l", wload["p1"])
            load_b(2, "L1b", wload["p2"])
            for k, d in enumerate((gamma, beta, b1col)):
                sp.dma_start(d, columns[:, k:k + 1], allow_slow_non_contiguous=True).then_inc(wload["small"], 16)

            def stream_matrix(a, M):
                def unit(u, n, t):
                    c, m = HALVES[u % 2]
                    sp.wait_ge(a.units.sem, a.units.base + n + 4)
                    k = P
                    if isinstance(t, int) and t == NT - 1 and M is A:
                        k = LC
                    rows = M[ds(t, 1), 0:k, c:c + m] if not isinstance(t, int) else M[t:t + 1, 0:k, c:c + m]
                    sp.dma_start(stream[u % 3][0:k, 0:m], rows.rearrange("a p s -> (a p) s")).then_inc(a.loaded[u % 3].sem, 16)
                with sp.Fori(0, NT // 3) as i:
                    for u in range(6):
                        unit(u, 6 * i + u, 3 * i + u // 2)
                for u in range(2):
                    unit(u, 2 * (NT - 1) + u, NT - 1)

            stream_matrix(agg0, AT)
            finished(sp, e0[2], NT - 1)
            load_x(p1_x)
            load_w(0, ["W2l"], wload["e1"])
            load_w(1, ["L1W"], wload["p2"])
            finished(sp, p1[0], NT - 1)
            stream_matrix(agg1, AT)
            finished(sp, e1[2], NT - 1)
            stream_matrix(agg2, A)
            finished(sp, p2[4], NT - 1)
            load_w(0, ["Wih_i", "Wih_o", "Wih_g"], wload["p3"])
            agg_end(sp, agg2)
            i = weight_at["Whh_i"]
            sp.dma_start(whh, weights[:, i * P:(i + 3) * P]).then_inc(wload["bias3"], 16)
            i = bias_at["bih_i"]
            sp.dma_start(bihh, bass.AP(biases.tensor, i * P, [[0, P], [1, 6 * P]])).then_inc(wload["bias3"], 16)
            finished(sp, p3[8], NT - 1)
            load_w(0, ["W1"], wload["e3"])
            load_b(0, "b1", wload["e3"])
            load_w(1, ["W2", "W3"], wload["e4"])
            load_b(1, "b2", wload["e4"])
            load_b(2, "b3", wload["e4"])

            def stream_rest(a, before):
                with sp.If(irregular != 0):
                    for s, t in before:
                        finished(sp, s, t)

                    def unit(h, t):
                        c, m = RESTS[h]
                        sp.wait_ge(a.rest_used.sem, a.rest_used.base + len(RESTS) * t + h + 1)
                        sp.dma_start(rest_in[h % 2][:, 0:m], count_rest[ds(t, 1), :, c:c + m]
                                     .rearrange("a p s -> (a p) s")).then_inc(a.rest_loaded[h % 2].sem, 16)
                    with sp.Fori(0, NT) as t:
                        for h in range(len(RESTS)):
                            unit(h, t)

            stream_rest(agg3, [(p3[8], NT - 1)])
            stream_rest(agg4, [(e3[2], NT - 1)])
            stream_rest(agg5, [(p4[1], NT - 1)])
            finished(sp, e4[6], NT - 1)
            load_w(0, ["w1", "w2"], wload["e6a"])
            load_b(0, "w2b", wload["e6b"])
            stream_rest(agg6, [(e5[2], NT - 1)])

            def save_out(t, p, n):
                finished(sp, e6[8], t)
                if n == P:
                    sp.dma_start(out[ds(t * P, P), :], tile(X, t)).then_inc(out_saved, 16)
                else:
                    sp.dma_start(out[(NT - 1) * P:N, :], X[0:NR, (NT - 1) * P:NT * P]).then_inc(out_saved, 16)
            tiles(sp, save_out)
            sp.wait_ge(out_saved, 16 * NT)

        @block.gpsimd
        def _(pool):
            nc.gpsimd.iota(iota[:, 0:max(CODE, P)], [[1, max(CODE, P)]], base=0, channel_multiplier=0,
                           allow_small_or_imprecise_dtypes=True).then_inc(pool_const, 1)
            nc.gpsimd.iota(theta_i, [[V * P, G]], base=0, channel_multiplier=V).then_inc(pool_const, 1)
            nc.gpsimd.iota(iota_w, [[1, P]], base=0, channel_multiplier=-1).then_inc(pool_const, 1)
            nc.gpsimd.memset(ones, 1.0).then_inc(pool_const, 1)
            nc.gpsimd.memset(onesb, 1.0).then_inc(pool_const, 1)
            nc.gpsimd.memset(onesrow, 1.0).then_inc(pool_const, 1)
            nc.gpsimd.memset(count, 0.0).then_inc(pool_const, 1)
            pool.wait_ge(edges_in, 96)
            for s, rows, done in ((1, row_i, gather0), (2, row1_i, gather1)):
                pool.wait_ge(rows_ready, s)
                for g in range(G):
                    nc.gpsimd.indirect_dma_start(
                        out=gathered[:, g * 3 * ROW:(g + 1) * 3 * ROW], out_offset=None, in_=edge_rows,
                        in_offset=bass.IndirectOffsetOnAxis(ap=rows[:, g:g + 1], axis=0)).then_inc(done, 16)
            def scale(n, place, w):
                pool.wait_ge(hots_ready, n + 1)
                each = hots[place].rearrange("p (s e) -> p s e", s=2)[:, :, None, :].to_broadcast([P, 2, 3, P])
                nc.gpsimd.tensor_tensor(hots_w[place].rearrange("p (s k e) -> p s k e", s=2, k=3), each,
                                        w.to_broadcast([P, 2, 3, P]), ALU.mult).then_inc(scaled_ready, 1)

            irregular = irregular_flag(pool)
            pool.wait_ge(tables_ready, 1)
            with pool.If(irregular != 0):
                pool.wait_ge(list_ready, 1)
                list_batches(pool, lambda n, r, c: scale(n, r, l_w[:, ds(c, 2), :][:, :, :, None]))
            with pool.Else():
                def pair_scaled(q, j):
                    for v in range(2):
                        scale(2 * q + v, 2 * j + v, t_w[:, :, :, ds(2 * q + v, 1)])
                build_tiles(pool, lambda t, p: pair_loop(pool, t, 0, pair_scaled))
            pool.wait_ge(build_over, 1)
            nc.gpsimd.memset(X[:, (NT - 1) * P:NT * P], 0.0).then_inc(h_cleared, 1)

            def keep(t, p, n):
                finished(pool, p0[0], t)
                nc.gpsimd.tensor_copy(tile(H, t), hb[p]).then_inc(p0[5].sem, 1)
            tiles(pool, keep)

            def feed(a, before):
                finished(pool, before, NT - 1)

                def one(t, j):
                    pool.wait_ge(a.units.sem, a.units.base + 2 * t + 2)
                    nc.gpsimd.tensor_copy(stationary[j], tile(H, t)).then_inc(a.stat.sem, 1)
                with pool.Fori(0, NT // 3) as i:
                    for j in range(3):
                        one(3 * i + j, j)
                one(NT - 1, 0)
            finished(pool, p0[5], NT - 1)
            feed(agg0, p0[4])
            finished(pool, e0[2], NT - 1)
            nc.gpsimd.memset(H[:, (NT - 1) * P:NT * P], 0.0).then_inc(h_cleared, 1)
            feed(agg1, p1[2])
            feed(agg2, p2[4])

        @block.scalar
        def _(act):
            irregular = irregular_flag(act)

            def evacuate_pair(slots, t, p, q, j, place):
                act.wait_ge(slots_used, 4 + slots * (q + 1))
                src_w = PS[:, 2 * j * BANK:2 * (j + 1) * BANK].rearrange("p (v c) -> p v c", v=2)
                d = staged[p].rearrange("p (a d) -> p a d", a=NT)[:, :, place:place + 2 * V]
                nc.scalar.copy(d.rearrange("p a (v d) -> p v a d", v=2),
                               src_w[:, :, 0:CODE].rearrange("p v (d a) -> p v a d", d=V))
                c = C.rearrange("p (a d) -> p a d", a=NT)[:, :, ds(q * 2 * V, 2 * V)]
                nc.scalar.copy(c.rearrange("p a (v d) -> p v a d", v=2),
                               src_w[:, :, CODE:2 * CODE].rearrange("p v (d a) -> p v a d", d=V)).then_inc(pairs_out, 1)

            def group_out(t, g, with_counts):
                n = LC if isinstance(t, int) and t == NT - 1 else P
                if g == 0 and with_counts:
                    act.wait_ge(row_ready, t + 1)
                    nc.scalar.copy(degree_row[0:1, 0:n], PS[0:1, 7 * BANK:7 * BANK + n]).then_inc(row_out, 1)
                m = min(BANK, NT * P - g * BANK)
                before = (NG + 1) // 2 * t + g // 2 if g % 2 == 0 else NG // 2 * t + g // 2
                act.wait_ge(turned, 3 + NG * t + g)
                if not isinstance(t, int) or before > 0:
                    act.wait_ge(piece_saved[g % 2], 16 * before)
                nc.scalar.copy(piece[g % 2][0:n, 0:m], PS[0:n, (4 + g % 2) * BANK:(4 + g % 2) * BANK + m])\
                    .then_inc(turned_out, 1)

            def build_tile(per_pair, t, p, with_counts):
                def pair_out(q, k):
                    if k == 0 and (not isinstance(t, int) or t >= 2):
                        act.wait_ge(stage_saved[p], (t - p) * 8)
                        act.wait_ge(tile_turned, 2 + t - 1)
                    evacuate_pair(per_pair, t, p, q, k % 2, k * 2 * V)
                pairs_and_groups(t, pair_out, lambda t, g: group_out(t, g, with_counts))

            with act.If(irregular != 0):
                act.wait_ge(list_ready, 1)
                build_tiles(act, lambda t, p: build_tile(2 * (4 * NCB + 1), t, p, False))
                for g in range(NG):
                    group_out(NT - 1, g, False)
            with act.Else():
                build_tiles(act, lambda t, p: build_tile(2, t, p, True))
                for g in range(NG):
                    group_out(NT - 1, g, True)
            act.wait_ge(counted, 1)
            act.wait_ge(pool_const, 7)
            nc.scalar.copy(count[:, 0:NT - 1], PS[:, 6 * BANK:6 * BANK + NT - 1])
            nc.scalar.copy(count[0:LC, NT - 1:NT], PS[0:LC, 6 * BANK + NT - 1:6 * BANK + NT]).then_inc(act_over, 1)
            act.wait_ge(act_over, 1)
            act.wait_ge(build_over, 1)
            nc.scalar.activation(dinv, count, ACT.Sqrt, bias=1.0, scale=1.0).then_inc(root_ready, 1)

            def root(s, d):
                finished(act, s[0], 0)
                nc.scalar.activation(d, d, ACT.Sqrt).then_inc(s[1].sem, 1)

            def relu_norm(t, dest, done):
                nc.scalar.activation(dest, tile(X, t), ACT.Relu, bias=col(nmr, t), scale=col(rstd, t)).then_inc(done.sem, 1)

            def copy_agg(s, a, used, source=H):
                evacuate(act, nc.scalar.copy, a, source, 0)
                finished(act, a.out, len(BANKS) - 1)

                def one(t, p, n):
                    two_back(act, used, t)
                    nc.scalar.copy(ag[p][:, 0:n], cols(source, t * P, n)).then_inc(s.sem, 1)
                return one

            root(n0, rstd)
            finished(act, n0[2], 0)

            def f(t, p, n):
                two_back(act, p0[1], t)
                two_back(act, p0[5], t)
                relu_norm(t, hb[p], p0[0])
            tiles(act, f)

            one = copy_agg(e0[0], agg0, e0[1])

            def turn(t, p, n, turned, out):
                finished(act, turned, t)
                m = n if n == P else NR
                nc.scalar.copy(cols(bn_in, t * P, m), misc[2 + p][:, 0:m]).then_inc(out.sem, 1)

            def f(t, p, n):
                one(t, p, n)
                turn(t, p, n, e0[3], e0[4])
            tiles(act, f)
            act.wait_ge(bn_var, 1)
            nc.scalar.activation(bn_scale, bn_scale, ACT.Sqrt).then_inc(bn_root, 1)
            act.wait_ge(bn_ready, 1)

            def f(t, p, n):
                two_back(act, p1[1], t)
                m = n if n == P else NR
                nc.scalar.activation(hT[p][:, 0:m], cols(bn_in, t * P, m), ACT.Relu, bias=bn_shift, scale=bn_scale)\
                    .then_inc(p1[0].sem, 1)
            tiles(act, f)
            tiles(act, copy_agg(e1[0], agg1, e1[1]))
            root(n1, rstd)
            finished(act, n1[2], 0)

            def f(t, p, n):
                two_back(act, p2[1], t)
                relu_norm(t, hb[p], p2[0])
            tiles(act, f)
            tiles(act, copy_agg(e2[0], agg2, e2[1]))
            root(n2, rstd)
            finished(act, n2[2], 0)

            def f(t, p, n):
                two_back(act, p3[1], t)
                relu_norm(t, hb[p], p3[0])
                finished(act, p3[4], t)
                nc.scalar.activation(gates_io[p], gates_io[p], ACT.Sigmoid)
                nc.scalar.activation(gates_g[p], gates_g[p], ACT.Tanh).then_inc(p3[5].sem, 1)
                finished(act, p3[6], t)
                nc.scalar.activation(tmp[p], tmp[p], ACT.Tanh).then_inc(p3[7].sem, 1)
            tiles(act, f)
            tiles(act, copy_agg(e3[0], agg3, e3[1]))

            one4 = copy_agg(e4[0], agg4, e4[1])

            def f(t, p, n):
                one4(t, p, n)
                finished(act, e4[3], t)
                nc.scalar.copy(hT[p][:, 0:n], misc[2 + p][:, 0:n]).then_inc(e4[4].sem, 1)
            tiles(act, f)
            root(n4, rstd)
            finished(act, n4[2], 0)

            def f(t, p, n):
                relu_norm(t, tile(H, t), p4[0])
            tiles(act, f)
            tiles(act, copy_agg(e5[0], agg5, e5[1], over_parts))

            one6 = copy_agg(e6[0], agg6, e6[1], over_parts)

            def f(t, p, n):
                one6(t, p, n)
                finished(act, e6[3], t)
                nc.scalar.copy(hT[p][:, 0:n], misc[2 + p][:, 0:n]).then_inc(e6[4].sem, 1)
                finished(act, e6[5], t)
                act.wait_ge(wload["small"], 48)
                nc.scalar.activation(tmp[p][:, 0:n], misc[p][:, 0:n], ACT.Identity, bias=b1col, scale=1.0).then_inc(e6[6].sem, 1)
            tiles(act, f)

        @block.vector
        def _(dve):
            def chain(s):
                done = [0]

                def step(ins):
                    done[0] += 1
                    ins.then_inc(s, 1)
                    dve.wait_ge(s, done[0])
                return step
            link = chain(dve_chain)

            def links(per_tile):
                m = mark("tile_links", per_tile * NT)
                return m.sem, lambda t, k: dve.wait_ge(m.sem, m.base + per_tile * t + k)

            dve.wait_ge(pool_const, 7)
            link(nc.vector.tensor_scalar(ident, iota_w, 0.0, None, ALU.is_equal))
            link(nc.vector.tensor_copy(identb, ident))
            link(nc.vector.tensor_copy(theta, theta_i))
            link(nc.vector.tensor_scalar(theta_nt, theta, float(NT), None, ALU.mult))
            dve.wait_ge(firsts_in, 16)
            nc.vector.tensor_copy(firsts[0:1, 0:NCH], firsts_i[0:1, 0:NCH]).then_inc(firsts_ready, 1)
            dve.wait_ge(firsts_spread, 1)
            link(nc.vector.tensor_copy(firsts_all[:, 0:NCH], PS[:, 7 * BANK:7 * BANK + NCH]))
            for g in range(G):
                link(nc.vector.tensor_scalar(below[:, 0:NCH], firsts_all[:, 0:NCH], theta[:, g:g + 1], 0.0,
                                             ALU.is_lt, ALU.add, accum_out=chunks_below[:, g:g + 1]))
            link(nc.vector.tensor_scalar(row0, chunks_below, float(P // STEP), -float(P // STEP), ALU.mult, ALU.add))
            link(nc.vector.tensor_scalar(row0, row0, 0.0, float(LASTROW), ALU.max, ALU.min))
            nc.vector.tensor_copy(row_i, row0).then_inc(rows_ready, 1)
            link(nc.vector.tensor_scalar(base0, row0, float(STEP), float(E - ROW), ALU.mult, ALU.min))
            dve.wait_ge(gather0, 16 * G)
            gv = gathered.rearrange("p (g k r) -> p g k r", g=G, k=3)
            d3 = dstf.rearrange("p (g r) -> p g r", g=G)
            link(nc.vector.tensor_copy(d3, gv[:, :, 1, :]))
            for g in range(G):
                link(nc.vector.tensor_scalar(below[:, 0:ROW], dstf[:, g * ROW:(g + 1) * ROW], theta[:, g:g + 1], 0.0,
                                             ALU.is_lt, ALU.add, accum_out=fine[:, g:g + 1]))
            link(nc.vector.tensor_tensor(start, base0, fine, ALU.add))
            link(nc.vector.tensor_copy(start_i, start))
            link(nc.vector.tensor_scalar(start_i, start_i, STEP.bit_length() - 1, None, ALU.arith_shift_right))
            link(nc.vector.tensor_copy(row1, start_i))
            link(nc.vector.tensor_scalar(last_or, start, float(E - ROW), float(LASTROW), ALU.is_ge, ALU.mult))
            link(nc.vector.tensor_tensor(row1, row1, last_or, ALU.max))
            link(nc.vector.tensor_scalar(row1, row1, float(LASTROW), None, ALU.min))
            nc.vector.tensor_copy(row1_i, row1).then_inc(rows_ready, 1)
            dve.wait_ge(gather1, 16 * G)
            t3, l3 = tile_i.rearrange("p (g r) -> p g r", g=G), low_i.rearrange("p (g r) -> p g r", g=G)
            link(nc.vector.tensor_copy(d3, gv[:, :, 1, :]))
            link(nc.vector.tensor_scalar(t3, gv[:, :, 0, :], 7, None, ALU.arith_shift_right))
            link(nc.vector.tensor_scalar(l3, gv[:, :, 0, :], P - 1, None, ALU.bitwise_and))
            link(nc.vector.tensor_copy(tilef, tile_i))
            link(nc.vector.tensor_copy(lowf, low_i))
            link(nc.vector.scalar_tensor_tensor(out=codef, in0=dstf, scalar=float(NT), in1=tilef, op0=ALU.mult, op1=ALU.add))
            for g in range(G):
                link(nc.vector.tensor_scalar(codef[:, g * ROW:(g + 1) * ROW], codef[:, g * ROW:(g + 1) * ROW],
                                             theta_nt[:, g:g + 1], None, ALU.subtract))
            link(nc.vector.tensor_scalar(inside, codef, 0.0, None, ALU.is_ge))
            link(nc.vector.scalar_tensor_tensor(out=inside2, in0=codef, scalar=float(CODE), in1=inside, op0=ALU.is_lt, op1=ALU.mult))
            nc.vector.reduce_sum(hits, inside2, mybir.AxisListType.X).then_inc(codes_ready, 1)
            dve.wait_ge(hits_summed, 1)
            nc.vector.tensor_scalar(flag.bitcast(I32)[0:1, :], PS[0:1, 6 * BANK:6 * BANK + 1], float(E), None, ALU.not_equal)\
                .then_inc(flag_ready, 1)
            dve.wait_ge(tables_turned, 1)
            for q, tab in enumerate((t_code, t_src, w_left)):
                for k in range(2):
                    link(nc.vector.tensor_copy(tab[:, k * NW:(k + 1) * NW], PS[:, (2 * q + k) * BANK:(2 * q + k) * BANK + NW]))

            def split_weights(link, parts, left):
                for k, part in enumerate(parts):
                    link(nc.vector.tensor_copy(part, left))
                    if k < 2:
                        link(nc.vector.tensor_tensor(left, left, part, ALU.subtract))
            left = w_left.rearrange("p (h v) -> p h v", h=2)
            split_weights(link, [t_w[:, :, k] for k in range(3)], left)

            def place_hots(place, n, code, low):
                dve.wait_ge(slots_used, n + 1)
                for s in range(2):
                    nc.vector.tensor_scalar(hot[place][s], iota[:, 0:P], low[s], None, ALU.is_equal)
                    last = nc.vector.tensor_scalar(code_hot[place][s], iota[:, 0:CODE], code[s], None, ALU.is_equal)
                return last.then_inc(hots_ready, 1)

            def pair_hots(q, j):
                for v in range(2):
                    place_hots(2 * j + v, 2 * q + v, *[[col(tab, s * NW + 2 * q + v) for s in (0, 1)] for tab in (t_code, t_src)])

            irregular = irregular_flag(dve)
            with dve.If(irregular != 0):
                lks = chain(all_chain)
                lks(nc.vector.memset(zerosb, 0.0))
                lks(nc.vector.memset(list_i, -1))
                lks(nc.vector.memset(list_w, 0.0))
                nc.vector.memset(hits, 0.0).then_inc(tables_ready, 1)
                dve.wait_ge(list_in, 16 * 3 * (2 if E % P else 1))
                lks(nc.vector.tensor_copy(l_dst, list_i[:, 0:NCP]))
                lks(nc.vector.tensor_scalar(list_t, list_i[:, NCP:2 * NCP], 7, None, ALU.arith_shift_right))
                lks(nc.vector.tensor_copy(l_src, list_t))
                lks(nc.vector.scalar_tensor_tensor(out=l_code, in0=l_dst, scalar=float(NT), in1=l_src, op0=ALU.mult, op1=ALU.add))
                lks(nc.vector.tensor_scalar(list_t, list_i[:, NCP:2 * NCP], P - 1, None, ALU.bitwise_and))
                lks(nc.vector.tensor_copy(l_src, list_t))
                split_weights(lks, [l_w[:, :, k] for k in range(3)], list_w)
                nc.vector.memset(rest_stage, 0.0).then_inc(list_ready, 1)

                def pair_of_all(q, j):
                    for v in range(2):
                        win = 2 * q + v
                        with dve.Fori(0, NCB) as i:
                            dve.wait_ge(shifted, win + 1)
                            for r in range(4):
                                place_hots(r, (4 * NCB) * win + 4 * i + r + win,
                                           *[[col(tab, 8 * i + 2 * r + s) for s in (0, 1)] for tab in (l_code, l_src)])
                        dve.wait_ge(hots_ready, 4 * NCB * (win + 1))
                        nc.vector.tensor_scalar(l_code, l_code, float(CODE), None, ALU.subtract).then_inc(shifted, 1)
                    dve.wait_ge(pairs_out, 2 + q + 1)
                    dve.wait_ge(rest_free, q + 1)
                    r = rest_stage.rearrange("p (a v d) -> p v a d", a=NT, v=2)
                    full = PS[:, 2 * j * BANK:2 * (j + 1) * BANK].rearrange("p (v c) -> p v c", v=2)[:, :, CODE:2 * CODE]
                    kept = C.rearrange("p (a d) -> p a d", a=NT)[:, :, ds(q * 2 * V, 2 * V)]
                    for v in range(2):
                        last = nc.vector.tensor_tensor(r[:, v], full[:, v].rearrange("p (d a) -> p a d", d=V),
                                                       kept[:, :, v * V:(v + 1) * V], ALU.subtract)
                    last.then_inc(rest_out, 1)
                build_tiles(dve, lambda t, p: pair_loop(dve, t, 0, pair_of_all))
                with dve.Fori(0, NT) as t:
                    with dve.Fori(0, NCB) as i:
                        dve.wait_ge(shifted, NW + t + 1)
                        for r in range(4):
                            dve.wait_ge(slots_used, (NW + t) * (4 * NCB + 1) + 4 * i + r + 1)
                            for s in range(2):
                                last = nc.vector.tensor_scalar(hot[r][s], iota[:, 0:P], col(l_dst, 8 * i + 2 * r + s), None, ALU.is_equal)
                            last.then_inc(hots_ready, 1)
                    dve.wait_ge(hots_ready, 4 * NCB * (NW + t + 1))
                    nc.vector.tensor_scalar(l_dst, l_dst, float(P), None, ALU.subtract).then_inc(shifted, 1)
            with dve.Else():
                nc.vector.memset(zerosb, 0.0).then_inc(tables_ready, 1)
                build_tiles(dve, lambda t, p: pair_loop(dve, t, 0, pair_hots))

            dve.wait_ge(root_ready, 1)

            lk = link
            lk(nc.vector.tensor_scalar(rcount, count, 1.0, None, ALU.max))
            lk(nc.vector.reciprocal(rcount, rcount))
            lk(nc.vector.reciprocal(dinv, dinv))
            lk(nc.vector.tensor_scalar(half_dinv, dinv, 0.5, None, ALU.mult))

            def norm_params(s):
                st = stat6.rearrange("p (t k) -> p t k", k=6)
                mean, var = mv[:, 0:NT], mv[:, NT:2 * NT]
                link(nc.vector.tensor_tensor(nmr, st[:, :, 1], st[:, :, 4], ALU.subtract))
                link(nc.vector.tensor_tensor(mean, st[:, :, 1], st[:, :, 4], ALU.add))
                link(nc.vector.tensor_tensor(var, st[:, :, 2], st[:, :, 5], ALU.add))
                link(nc.vector.scalar_tensor_tensor(out=nmr, in0=nmr, scalar=0.25, in1=nmr, op0=ALU.mult, op1=ALU.mult))
                link(nc.vector.scalar_tensor_tensor(out=var, in0=var, scalar=1.0 / D, in1=nmr, op0=ALU.mult, op1=ALU.add))
                nc.vector.tensor_scalar(rstd, var, EPS, None, ALU.add).then_inc(s[0].sem, 1)
                finished(dve, s[1], 0)
                link(nc.vector.reciprocal(rstd, rstd))
                nc.vector.scalar_tensor_tensor(out=nmr, in0=mean, scalar=-0.5, in1=rstd, op0=ALU.mult, op1=ALU.mult)\
                    .then_inc(s[2].sem, 1)

            def tile_stats(t):
                return nc.vector.bn_stats(cols(stat6, 6 * t, 6), tile(X, t))

            s0, linked0 = links(1)
            dve.wait_ge(x_in, 32)
            with dve.Fori(0, NT) as t:
                tile_stats(t).then_inc(s0, 1)
            linked0(NT - 1, 1)
            norm_params(n0)
            dve.wait_ge(wload["p0"], 32)

            def f(t, p, n):
                finished(dve, p0[1], t)
                two_back(dve, p0[3], t)
                nc.vector.tensor_copy(hT[p], misc[p]).then_inc(p0[2].sem, 1)
                finished(dve, p0[3], t)
                nc.vector.tensor_tensor(tile(X, t), misc[2 + p], b[0], ALU.add).then_inc(p0[4].sem, 1)
            tiles(dve, f)

            evacuate(dve, nc.vector.tensor_copy, agg0, H, 1)

            def f(t, p, n):
                finished(dve, e0[1], t)
                two_back(dve, e0[3], t)
                nc.vector.scalar_tensor_tensor(out=hb[p][0:n], in0=misc[p][0:n], scalar=col(rcount, t)[0:n],
                                               in1=tile(X, t)[0:n], op0=ALU.mult, op1=ALU.add).then_inc(e0[2].sem, 1)
            tiles(dve, f)
            finished(dve, e0[4], NT - 1)
            lk = link
            pieces = [(c, min(BANK, N - c)) for c in range(0, N, BANK)]
            for i, (c, m) in enumerate(pieces):
                ins = nc.vector.bn_stats(stat6[:, 6 * i:6 * i + 6], bn_in[:, c:c + m])
            lk(ins)
            lk(nc.vector.bn_aggr(bn_mv, stat6[:, 0:6 * len(pieces)]))
            nc.vector.tensor_scalar(bn_scale, bn_mv[:, 1:2], EPS, None, ALU.add).then_inc(bn_var, 1)
            dve.wait_ge(bn_root, 1)
            dve.wait_ge(wload["small"], 48)
            lk(nc.vector.reciprocal(bn_scale, bn_scale))
            lk(nc.vector.tensor_tensor(bn_scale, bn_scale, gamma, ALU.mult))
            lk(nc.vector.tensor_tensor(bn_shift, bn_mv[:, 0:1], bn_scale, ALU.mult))
            nc.vector.tensor_tensor(bn_shift, beta, bn_shift, ALU.subtract).then_inc(bn_ready, 1)
            dve.wait_ge(p1_x, 32)
            dve.wait_ge(wload["p1"], 32)
            dve.wait_ge(h_cleared, 2)

            s, linked = links(1)

            def f(t, p, n, s=s, linked=linked):
                m = n if n == P else NR
                finished(dve, p1[1], t)
                nc.vector.tensor_copy(tile(H, t)[0:m], misc[p][0:m])
                nc.vector.tensor_tensor(tile(X, t)[0:m], misc[2 + p][0:m], tile(X, t)[0:m], ALU.add).then_inc(s, 1)
                linked(t, 1)
                nc.vector.tensor_tensor(tile(X, t), tile(X, t), b[1], ALU.add).then_inc(p1[2].sem, 1)
            tiles(dve, f)

            s, linked = links(1)

            evacuate(dve, nc.vector.tensor_copy, agg1, H, 1)

            def f(t, p, n, s=s, linked=linked):
                finished(dve, e1[1], t)
                nc.vector.scalar_tensor_tensor(out=tile(X, t)[0:n], in0=misc[p][0:n], scalar=col(rcount, t)[0:n],
                                               in1=tile(X, t)[0:n], op0=ALU.mult, op1=ALU.add).then_inc(s, 1)
                linked(t, 1)
                tile_stats(t).then_inc(e1[2].sem, 1)
            tiles(dve, f)
            finished(dve, e1[2], NT - 1)
            norm_params(n1)
            dve.wait_ge(wload["p2"], 32)

            def f(t, p, n):
                finished(dve, p2[1], t)
                two_back(dve, p2[3], t)
                nc.vector.tensor_copy(hT[p], misc[p]).then_inc(p2[2].sem, 1)
                finished(dve, p2[3], t)
                nc.vector.tensor_tensor(tile(H, t), misc[2 + p], b[2], ALU.add).then_inc(p2[4].sem, 1)
            tiles(dve, f)

            s, linked = links(1)

            evacuate(dve, nc.vector.tensor_copy, agg2, H, 1)

            def f(t, p, n, s=s, linked=linked):
                finished(dve, e2[1], t)
                nc.vector.tensor_tensor(tile(X, t)[0:n], misc[p][0:n], tile(X, t)[0:n], ALU.add).then_inc(s, 1)
                linked(t, 1)
                tile_stats(t).then_inc(e2[2].sem, 1)
            tiles(dve, f)
            finished(dve, e2[2], NT - 1)
            norm_params(n2)
            lk = link
            agg_end(dve, agg2)
            nc.vector.memset(zeros, 0.0).then_inc(gate_bias, 1)
            dve.wait_ge(wload["bias3"], 32)
            nc.vector.tensor_tensor(bslot, bihh[:, 0:3 * P], bihh[:, 3 * P:6 * P], ALU.add).then_inc(gate_bias, 1)
            dve.wait_ge(gate_bias, 2)
            dve.wait_ge(gate_prod, 1)
            nc.vector.tensor_tensor(bslot, bslot, gate_prod_out, ALU.add).then_inc(gate_ready, 1)
            dve.wait_ge(gate_ready, 1)

            def split(u, t, s, linked, k):
                nc.vector.tensor_copy(part(0, t), u).then_inc(s, 1)
                linked(t, k)
                nc.vector.tensor_tensor(u, u, part(0, t), ALU.subtract).then_inc(s, 1)
                linked(t, k + 1)
                nc.vector.tensor_copy(part(1, t), u).then_inc(s, 1)
                linked(t, k + 2)
                return nc.vector.tensor_tensor(part(2, t), u, part(1, t), ALU.subtract)

            s3, linked3 = links(4)

            def f(t, p, n):
                finished(dve, p3[1], t)
                two_back(dve, p3[3], t)
                nc.vector.tensor_copy(hT[p], misc[p]).then_inc(p3[2].sem, 1)
                finished(dve, p3[3], t)
                g = gates_out[p]
                nc.vector.tensor_tensor(gates_io[p], g[:, 0:2 * P], bslot[:, 0:2 * P], ALU.add)
                nc.vector.tensor_tensor(gates_g[p], g[:, 2 * P:3 * P], bslot[:, 2 * P:3 * P], ALU.add).then_inc(p3[4].sem, 1)
                finished(dve, p3[5], t)
                nc.vector.tensor_tensor(tmp[p], gates_io[p][:, 0:P], gates_g[p], ALU.mult).then_inc(p3[6].sem, 1)
                finished(dve, p3[7], t)
                nc.vector.scalar_tensor_tensor(out=tmp[p], in0=tmp[p], scalar=col(dinv, t), in1=gates_io[p][:, P:2 * P],
                                               op0=ALU.mult, op1=ALU.mult).then_inc(s3, 1)
                linked3(t, 1)
                split(tmp[p], t, s3, linked3, 2).then_inc(p3[8].sem, 1)
            tiles(dve, f)

            dve.wait_ge(wload["e3"], 32)

            s, linked = links(6)

            evacuate(dve, nc.vector.tensor_copy, agg3, H, 1)

            def f(t, p, n, s=s, linked=linked):
                finished(dve, e3[1], t)
                nc.vector.tensor_scalar(tmp[p][0:n], misc[p][0:n], col(dinv, t)[0:n], None, ALU.mult).then_inc(s, 1)
                linked(t, 1)
                nc.vector.tensor_tensor(tmp[p], tmp[p], b[0], ALU.add).then_inc(s, 1)
                linked(t, 2)
                nc.vector.tensor_scalar(tmp[p], tmp[p], 0.0, col(dinv, t), ALU.max, ALU.mult).then_inc(s, 1)
                linked(t, 3)
                split(tmp[p], t, s, linked, 4).then_inc(e3[2].sem, 1)
            tiles(dve, f)

            dve.wait_ge(wload["e4"], 48)

            s, linked = links(4)

            evacuate(dve, nc.vector.tensor_copy, agg4, H, 1)

            def f(t, p, n, s=s, linked=linked):
                finished(dve, e4[1], t)
                two_back(dve, e4[3], t)
                nc.vector.tensor_scalar(hb[p][0:n], misc[p][0:n], col(dinv, t)[0:n], None, ALU.mult).then_inc(s, 1)
                linked(t, 1)
                nc.vector.tensor_tensor(hb[p][0:n], hb[p][0:n], b[1][0:n], ALU.add).then_inc(e4[2].sem, 1)
                finished(dve, e4[5], t)
                nc.vector.tensor_tensor(tmp[p][0:n], misc[p][0:n], b[2][0:n], ALU.add).then_inc(s, 1)
                linked(t, 2)
                nc.vector.tensor_scalar(tmp[p][0:n], tmp[p][0:n], 0.0, None, ALU.max).then_inc(s, 1)
                linked(t, 3)
                nc.vector.tensor_tensor(tile(X, t)[0:n], tile(X, t)[0:n], tmp[p][0:n], ALU.add).then_inc(s, 1)
                linked(t, 4)
                tile_stats(t).then_inc(e4[6].sem, 1)
            tiles(dve, f)
            finished(dve, e4[6], NT - 1)
            norm_params(n4)

            s, linked = links(4)

            def f(t, p, n, s=s, linked=linked):
                finished(dve, p4[0], t)
                nc.vector.tensor_scalar(tmp[p], tile(H, t), col(dinv, t), None, ALU.mult).then_inc(s, 1)
                linked(t, 1)
                split(tmp[p], t, s, linked, 2).then_inc(p4[1].sem, 1)
            tiles(dve, f)

            s, linked = links(5)

            evacuate(dve, nc.vector.tensor_copy, agg5, over_parts, 1)

            def f(t, p, n, s=s, linked=linked):
                finished(dve, e5[1], t)
                nc.vector.scalar_tensor_tensor(out=tmp[p][0:n], in0=misc[p][0:n], scalar=col(dinv, t)[0:n], in1=tile(H, t)[0:n],
                                               op0=ALU.mult, op1=ALU.add).then_inc(s, 1)
                linked(t, 1)
                nc.vector.tensor_scalar(tmp[p], tmp[p], col(half_dinv, t), None, ALU.mult).then_inc(s, 1)
                linked(t, 2)
                split(tmp[p], t, s, linked, 3).then_inc(e5[2].sem, 1)
            tiles(dve, f)

            dve.wait_ge(wload["e6b"], 16)

            s, linked = links(2)

            evacuate(dve, nc.vector.tensor_copy, agg6, over_parts, 1)

            def f(t, p, n, s=s, linked=linked):
                finished(dve, e6[1], t)
                two_back(dve, e6[3], t)
                nc.vector.scalar_tensor_tensor(out=hb[p][0:n], in0=misc[p][0:n], scalar=col(dinv, t)[0:n], in1=tile(H, t)[0:n],
                                               op0=ALU.mult, op1=ALU.add).then_inc(s, 1)
                linked(t, 1)
                nc.vector.tensor_scalar(hb[p][0:n], hb[p][0:n], 0.5, 0.0, ALU.mult, ALU.max).then_inc(e6[2].sem, 1)
                finished(dve, e6[7], t)
                nc.vector.tensor_tensor(tile(X, t)[0:n], misc[2 + p][0:n], tile(X, t)[0:n], ALU.add).then_inc(s, 1)
                linked(t, 2)
                nc.vector.tensor_tensor(tile(X, t)[0:n], tile(X, t)[0:n], b[0][0:n], ALU.add).then_inc(e6[8].sem, 1)
            tiles(dve, f)

        @block.tensor
        def _(pe):
            mm = nc.tensor.matmul
            pe.wait_ge(firsts_ready, 1)
            mm(PS[:, 7 * BANK:7 * BANK + NCH], onesrow[0:1, :], firsts[0:1, 0:NCH], start=True, stop=True).then_inc(firsts_spread, 1)
            pe.wait_ge(codes_ready, 1)
            mm(PS[:, 6 * BANK:6 * BANK + 1], onesrow, hits, start=True, stop=True).then_inc(hits_summed, 1)
            wg = gathered.bitcast(F32)
            for g in range(G):
                for k in range(2):
                    for q, s in enumerate((codef, lowf, wg)):
                        c = g * ROW + k * P if q < 2 else g * 3 * ROW + 2 * ROW + k * P
                        last = nc.tensor.transpose(PS[:, (2 * q + k) * BANK + g * P:(2 * q + k) * BANK + (g + 1) * P],
                                                   s[:, c:c + P], ident)
            last.then_inc(tables_turned, 1)
            irregular = irregular_flag(pe)
            pe.wait_ge(tables_ready, 1)

            def bank_of(j, v):
                return PS[:, (2 * j + v) * BANK:(2 * j + v) * BANK + 2 * CODE]

            def add_place(place, n, out, alone):
                pe.wait_ge(hots_ready, n + 1)
                for s in range(2):
                    mm(out[:, CODE:2 * CODE], hot[place][s], code_hot[place][s], start=alone and s == 0,
                       stop=alone and s == 1)
                pe.wait_ge(scaled_ready, n + 1)
                for s in range(2):
                    for k in range(3):
                        last = mm(out[:, 0:CODE], hot_w[place][s][k], code_hot[place][s], start=False,
                                  stop=alone and s == 1 and k == 2, skip_group_check=True)
                return last.then_inc(slots_used, 1)

            def pair(q, j):
                pe.wait_ge(pairs_out, q + 1)
                for v in range(2):
                    add_place(2 * j + v, 2 * q + v, bank_of(j, v), True)

            def pair_all(q, j):
                pe.wait_ge(pairs_out, q + 1)
                for v in range(2):
                    mm(bank_of(j, v), zerosb[:, 0:P], zerosb[:, 0:2 * CODE], start=True, stop=False)
                    base = (2 * q + v) * NCB * 4
                    with pe.Fori(0, NCB) as i:
                        for r in range(4):
                            add_place(r, base + 4 * i + r, bank_of(j, v), False)
                    mm(bank_of(j, v), zerosb[:, 0:P], zerosb[:, 0:2 * CODE], start=False, stop=True).then_inc(slots_used, 1)
                pe.wait_ge(rest_out, q + 1)

            def turn_group(t, p, g, with_counts):
                n = LC if isinstance(t, int) and t == NT - 1 else P
                if g == 0:
                    pe.wait_ge(pairs_out, 2 + pairs_before(t) + pairs_in(t))
                    if with_counts:
                        for a in range(NT):
                            last = mm(PS[0:1, 7 * BANK:7 * BANK + n], onesb[:, 0:1], cols(C, a * NC + t * P, n),
                                      start=(a == 0), stop=(a == NT - 1))
                        last.then_inc(row_ready, 1)
                before = NG * t + max(g - 1, 0)
                if not isinstance(t, int) or before > 0:
                    pe.wait_ge(turned_out, before)
                for a in range(4 * g, min(4 * g + 4, NT)):
                    last = nc.tensor.transpose(PS[0:n, (4 + g % 2) * BANK + (a % 4) * P:(4 + g % 2) * BANK + (a % 4 + 1) * P],
                                               staged[p][:, a * P:a * P + n], ident)
                last.then_inc(turned, 1)
                if g == NG - 1 and with_counts:
                    pe.wait_ge(row_out, t + 1)
                    mm(col(PS, 6 * BANK + t)[0:n], degree_row[0:1, 0:n], ones[0:1, 0:1], start=True, stop=True)\
                        .then_inc(tile_turned, 1)
                elif g == NG - 1:
                    mm(PS[:, 7 * BANK:7 * BANK + 1], zerosb[:, 0:P], zerosb[:, 0:1], start=True, stop=True).then_inc(tile_turned, 1)

            def build_tile(t, p, pair_body, with_counts):
                pairs_and_groups(t, lambda q, k: pair_body(q, k % 2), lambda t, g: turn_group(t, 1 - p, g, with_counts))

            with pe.If(irregular != 0):
                build_tiles(pe, lambda t, p: build_tile(t, p, pair_all, False))
                for g in range(NG):
                    turn_group(NT - 1, 0, g, False)
                with pe.Fori(0, NT) as t:
                    mm(col(PS, 6 * BANK + t), zerosb[:, 0:P], zerosb[:, 0:1], start=True, stop=False)
                    with pe.Fori(0, NCB) as i:
                        for r in range(4):
                            pe.wait_ge(hots_ready, (NW + t) * NCB * 4 + 4 * i + r + 1)
                            for s in range(2):
                                last = mm(col(PS, 6 * BANK + t), hot[r][s], onesb[:, 0:1], start=False, stop=False)
                            last.then_inc(slots_used, 1)
                    mm(col(PS, 6 * BANK + t), zerosb[:, 0:P], zerosb[:, 0:1], start=False, stop=True).then_inc(slots_used, 1)
                mm(PS[:, 7 * BANK:7 * BANK + 1], zerosb[:, 0:P], zerosb[:, 0:1], start=True, stop=True).then_inc(counted, 1)
            with pe.Else():
                build_tiles(pe, lambda t, p: build_tile(t, p, pair, True))
                for g in range(NG):
                    turn_group(NT - 1, 0, g, True)
                mm(PS[:, 7 * BANK:7 * BANK + 1], ident, ones, start=True, stop=True).then_inc(counted, 1)

            def run_fp32(a, k_last, before):
                for s in before:
                    finished(pe, s, NT - 1)

                def one(t, turn, j, start, stop, k):
                    finished(pe, a.stat, t)
                    for h, (c, m) in enumerate(HALVES):
                        u = 2 * j + h
                        pe.wait_ge(a.loaded[u % 3].sem, a.loaded[u % 3].base + 16 * (2 * turn + u // 3 + 1))
                        for c1 in range(0, m, BANK):
                            w_ = min(BANK, m - c1)
                            last = mm(agg[:, c + c1:c + c1 + w_], stationary[j][0:k], stream[u % 3][0:k, c1:c1 + w_],
                                      start=start, stop=stop)
                        last.then_inc(a.units.sem, 1)
                for j in range(3):
                    one(j, 0, j, j == 0, False, P)
                with pe.Fori(1, NT // 3) as i:
                    for j in range(3):
                        one(3 * i + j, i, j, False, False, P)
                one(NT - 1, NT // 3, 0, False, True, k_last)
                mm(misc[7][:, 0:1], ident, ones, start=True, stop=True).then_inc(a.done.sem, 1)

            def run_counts(a, before):
                for s in before:
                    finished(pe, s, NT - 1)

                def one(t, start):
                    for k in range(3):
                        for c, m in BANKS:
                            mm(agg[:, c:c + m], part(k, t), cols(C, t * NC + c, m), start=start and k == 0, stop=False)
                one(0, True)
                with pe.Fori(1, NT) as t:
                    one(t, False)
                with pe.If(irregular != 0):
                    with pe.Fori(0, NT) as t:
                        for h, (c, m) in enumerate(RESTS):
                            got = a.rest_loaded[h % 2]
                            pe.wait_ge(got.sem, got.base + 16 * (len(RESTS) // 2 * t + h // 2 + 1))
                            for k in range(3):
                                for c1 in range(0, m, BANK):
                                    w_ = min(BANK, m - c1)
                                    last = mm(agg[:, c + c1:c + c1 + w_], part(k, t), rest_in[h % 2][:, c1:c1 + w_],
                                              start=False, stop=False)
                            last.then_inc(a.rest_used.sem, 1)
                for t in range(NT):
                    n = LC if t == NT - 1 else P
                    for k in range(3):
                        last = mm(agg[:, t * P:t * P + n], part(k, t), identb[:, 0:n], start=False,
                                  stop=k == 2 and (t % 4 == 3 or t == NT - 1))
                last.then_inc(a.done.sem, 1)

            def product(t, p, n, operand, operand_done, weight, dest, done, free):
                finished(pe, operand_done, t)
                two_back(pe, free, t)
                mm(misc[dest + p][0:n], operand[p][:, 0:n], weight, start=True, stop=True).then_inc(done.sem, 1)

            def turn(t, p, n, operand, operand_done, dest, done, free):
                finished(pe, operand_done, t)
                two_back(pe, free, t)
                nc.tensor.transpose(misc[dest + p][:, 0:n], operand[p][0:n, :], ident[0:n, 0:n]).then_inc(done.sem, 1)

            def turn_back(t, p, n, operand, operand_done, dest, done, free):
                finished(pe, operand_done, t)
                two_back(pe, free, t)
                nc.tensor.transpose(misc[dest + p][0:n, :], operand[p][:, 0:n], ident).then_inc(done.sem, 1)

            pe.wait_ge(wload["p0"], 32)

            def f(t, p, n):
                turn(t, p, P, hb, p0[0], 0, p0[1], p0[2])
                product(t, p, P, hT, p0[2], w[0], 2, p0[3], p0[4])
            tiles(pe, f)
            run_fp32(agg0, P, [p0[4]])
            pe.wait_ge(wload["e0"], 16)

            def f(t, p, n):
                product(t, p, n, ag, e0[0], w[1], 0, e0[1], e0[2])
                turn(t, p, n, hb, e0[2], 2, e0[3], e0[4])
            tiles(pe, f)
            pe.wait_ge(wload["p1"], 32)

            def f(t, p, n):
                m = n if n == P else NR
                finished(pe, p1[0], t)
                two_back(pe, p1[2], t)
                nc.tensor.transpose(misc[p][0:m, :], hT[p][:, 0:m], ident)
                mm(misc[2 + p][0:m], hT[p][:, 0:m], w[2], start=True, stop=True).then_inc(p1[1].sem, 1)
            tiles(pe, f)
            run_fp32(agg1, P, [p1[2]])
            pe.wait_ge(wload["e1"], 16)
            tiles(pe, lambda t, p, n: product(t, p, n, ag, e1[0], w[0], 0, e1[1], e1[2]))
            pe.wait_ge(wload["p2"], 32)

            def f(t, p, n):
                turn(t, p, P, hb, p2[0], 0, p2[1], p2[2])
                product(t, p, P, hT, p2[2], w[1], 2, p2[3], p2[4])
            tiles(pe, f)
            run_fp32(agg2, LC, [p2[4]])
            tiles(pe, lambda t, p, n: turn_back(t, p, n, ag, e2[0], 0, e2[1], e2[2]))
            pe.wait_ge(gate_bias, 2)
            mm(gate_prod_out, zeros, whh, start=True, stop=True).then_inc(gate_prod, 1)
            pe.wait_ge(wload["p3"], 16)

            def f(t, p, n):
                turn(t, p, P, hb, p3[0], 0, p3[1], p3[2])
                finished(pe, p3[2], t)
                two_back(pe, p3[4], t)
                mm(gates_out[p], hT[p], wslot, start=True, stop=True).then_inc(p3[3].sem, 1)
            tiles(pe, f)
            run_counts(agg3, [p3[8]])
            pe.wait_ge(wload["e3"], 32)
            tiles(pe, lambda t, p, n: product(t, p, n, ag, e3[0], w[0], 0, e3[1], e3[2]))
            run_counts(agg4, [e3[2]])
            pe.wait_ge(wload["e4"], 48)

            def f(t, p, n):
                product(t, p, n, ag, e4[0], w[1], 0, e4[1], e4[6])
                turn(t, p, n, hb, e4[2], 2, e4[3], e4[4])
                finished(pe, e4[4], t)
                mm(misc[p][0:n], hT[p][:, 0:n], w[2], start=True, stop=True).then_inc(e4[5].sem, 1)
            tiles(pe, f)
            run_counts(agg5, [p4[1]])
            tiles(pe, lambda t, p, n: turn_back(t, p, n, ag, e5[0], 0, e5[1], e5[2]))
            run_counts(agg6, [e5[2]])
            pe.wait_ge(wload["e6a"], 16)

            def f(t, p, n):
                turn_back(t, p, n, ag, e6[0], 0, e6[1], e6[6])
                turn(t, p, n, hb, e6[2], 2, e6[3], e6[8])
                finished(pe, e6[4], t)
                mm(misc[p][:, 0:n], w[0], hT[p][:, 0:n], start=True, stop=True).then_inc(e6[5].sem, 1)
                finished(pe, e6[6], t)
                mm(misc[2 + p][0:n], tmp[p][:, 0:n], w[1], start=True, stop=True).then_inc(e6[7].sem, 1)
            tiles(pe, f)


_W = ["W1r", "W1l", "W2r", "W2l", "L1W", "Wih_i", "Wih_o", "Wih_g", "Whh_i", "Whh_o", "Whh_g", "W1", "W2", "W3", "w1", "w2"]
_B = ["b1l", "b2l", "L1b", "bih_i", "bih_o", "bih_g", "bhh_i", "bhh_o", "bhh_g", "b1", "b2", "b3", "w2b"]


def kernel(x, src, dst, edge_weight, L0_gnn_W1l, L0_gnn_b1l, L0_gnn_W1r, L0_gnn_bn_gamma, L0_gnn_bn_beta, L0_gnn_W2l,
           L0_gnn_b2l, L0_gnn_W2r, L1_gnn_W, L1_gnn_b, L2_gnn_W_ih, L2_gnn_W_hh, L2_gnn_b_ih, L2_gnn_b_hh, L2_gnn_W1,
           L2_gnn_b1, L2_gnn_W2, L2_gnn_b2, L2_gnn_W3, L2_gnn_b3, L3_gnn_w1, L3_gnn_b1, L3_gnn_w2, L3_gnn_b2):
    import numpy as _np
    import concourse.bacc as _bacc
    from concourse.bass_utils import run_bass_kernel_spmd as _run

    D = x.shape[1]

    def gate(a, k):
        return _np.asarray(a)[k * D:(k + 1) * D]

    by_name = {"W1r": _np.asarray(L0_gnn_W1r).T, "W1l": _np.asarray(L0_gnn_W1l).T, "W2r": _np.asarray(L0_gnn_W2r).T,
               "W2l": _np.asarray(L0_gnn_W2l).T, "L1W": _np.asarray(L1_gnn_W), "W1": _np.asarray(L2_gnn_W1),
               "W2": _np.asarray(L2_gnn_W2), "W3": _np.asarray(L2_gnn_W3).T, "w1": _np.asarray(L3_gnn_w1).T,
               "w2": _np.asarray(L3_gnn_w2).T}
    rows = {"b1l": L0_gnn_b1l, "b2l": L0_gnn_b2l, "L1b": L1_gnn_b, "b1": L2_gnn_b1, "b2": L2_gnn_b2, "b3": L2_gnn_b3,
            "w2b": L3_gnn_b2}
    for name, k in (("i", 0), ("g", 2), ("o", 3)):
        by_name["Wih_" + name] = gate(L2_gnn_W_ih, k).T
        by_name["Whh_" + name] = gate(L2_gnn_W_hh, k).T
        rows["bih_" + name] = gate(L2_gnn_b_ih, k)
        rows["bhh_" + name] = gate(L2_gnn_b_hh, k)
    arrays = {
        "in_x": _np.ascontiguousarray(x),
        "in_src": _np.ascontiguousarray(src),
        "in_dst": _np.ascontiguousarray(dst),
        "in_edge_weight": _np.ascontiguousarray(edge_weight),
        "in_weights": _np.ascontiguousarray(_np.concatenate([by_name[n] for n in _W], axis=1)),
        "in_biases": _np.ascontiguousarray(_np.stack([_np.asarray(rows[n]) for n in _B])),
        "in_columns": _np.ascontiguousarray(_np.stack([_np.asarray(a) for a in (L0_gnn_bn_gamma, L0_gnn_bn_beta, L3_gnn_b1)], axis=1)),
    }
    nc = _bacc.Bacc("TRN2", target_bir_lowering=False, num_devices=1)
    t = {k: nc.dram_tensor(k, a.shape, mybir.dt.from_np(a.dtype), kind="ExternalInput").ap() for k, a in arrays.items()}
    out = nc.dram_tensor("out", x.shape, F32, kind="ExternalOutput").ap()
    gnn_blocks(nc, t["in_x"], t["in_src"], t["in_dst"], t["in_edge_weight"], t["in_weights"],
               {n: i for i, n in enumerate(_W)}, t["in_biases"], {n: i for i, n in enumerate(_B)}, t["in_columns"], out)
    r = _run(nc, [arrays], core_ids=[0])
    return r.results[0]["out"]
```

```python
from contextlib import ExitStack

import concourse.bass as bass
from concourse import mybir

F32 = mybir.dt.float32
BF16 = mybir.dt.bfloat16
I32 = mybir.dt.int32
ALU = mybir.AluOpType
ACT = mybir.ActivationFunctionType
ds = bass.ds
P = 128
V = 8
ROW = 256
STEP = 32
BANK = 512


def gnn_blocks(nc, x, src, dst, edge_weight, weights, weight_at, biases, bias_at, columns, out):
    N, D = x.shape
    E, = src.shape
    NT = -(-N // P)
    NR = N - P * (NT - 1)
    NW = -(-N // (2 * V)) * 2
    NC = NW * V
    LC = NC - P * (NT - 1)
    CODE = V * NT
    G = 4
    NPT = P // (2 * V)
    NPL = LC // (2 * V)
    NCH = -(-E // P)
    NCB = -(-NCH // 8)
    LASTROW = (E - ROW) // STEP + 1
    NROWS = LASTROW + 1
    NG = -(-NT // 4)
    BANKS = [(c, min(BANK, NC - c)) for c in range(0, NC, BANK)]
    HALF = BANK * (len(BANKS) // 2)
    HALVES = [(0, HALF), (HALF, NC - HALF)]
    STREAM = max(HALF, NC - HALF)
    RESTS = [(c, min(2 * BANK, NC - c)) for c in range(0, NC, 2 * BANK)]
    assert len(RESTS) % 2 == 0
    EPS = 1e-5
    assert D == P and NT % 6 == 1 and NW <= G * P and NCH <= BANK and NR <= LC < P and LC % (2 * V) == 0
    SETUP = 14000
    assert 7 * BANK >= NC and 2 * CODE <= BANK and LC == P // 2

    edge_rows = nc.dram_tensor("edge_rows", (NROWS, 3 * ROW), I32).ap()
    AT = nc.dram_tensor("AT", (NT, P, NC), F32).ap()
    A = nc.dram_tensor("A", (NT, P, NT * P), F32).ap()
    count_rest = nc.dram_tensor("count_rest", (NT, P, NC), BF16).ap()

    with ExitStack() as ctx:
        arena = ctx.enter_context(nc.sbuf_tensor("arena", [P, 53208], F32))
        PS = ctx.enter_context(nc.psum_tensor("PS", [P, 8 * BANK], F32))
        at = [0]

        def take(words):
            at[0] += words
            assert at[0] <= 53208, at[0]
            return arena[:, at[0] - words:at[0]]

        scratch0 = at[0]
        C = take(max(NT * NC // 2, SETUP))[:, 0:NT * NC // 2].bitcast(BF16)
        setup_end = at[0]
        ident = take(P)
        iota = take(-(-max(CODE, P) // 2)).bitcast(BF16)
        identb = take(P // 2).bitcast(BF16)
        ones = take(1)
        onesb = take(1).bitcast(BF16)
        count = take(NT)
        rcount = take(NT)
        dinv = take(NT)
        half_dinv = take(NT)
        flag = take(1)
        region = at[0]

        W5 = 2 * NW
        t_code, t_src = [take(W5) for _ in range(2)]
        t_w = take(3 * W5 // 2).bitcast(BF16).rearrange("p (k h v) -> p h k v", k=3, h=2)
        PLACE = 2 * 4 * P + 2 * CODE
        places = [take(PLACE // 2).bitcast(BF16) for _ in range(4)]
        hots = [m[:, 0:2 * P] for m in places]
        hot = [[m[:, s * P:(s + 1) * P] for s in (0, 1)] for m in places]
        hots_w = [m[:, 2 * P:8 * P] for m in places]
        hot_w = [[[m[:, (2 + 3 * s + k) * P:(3 + 3 * s + k) * P] for k in range(3)] for s in (0, 1)] for m in places]
        code_hot = [[m[:, 8 * P + s * CODE:8 * P + (s + 1) * CODE] for s in (0, 1)] for m in places]
        piece = [take(BANK) for _ in range(2)]
        staged = [take(NT * P) for _ in range(2)]
        rest_stage = take(NT * V).bitcast(BF16)
        zerosb = take(max(CODE, P // 2)).bitcast(BF16)
        degree_row = take(P)

        at[0] = scratch0
        gathered = take(G * 3 * ROW).bitcast(I32)
        firsts_i = take(BANK).bitcast(I32)
        firsts = take(BANK)
        onesrow = take(P)
        firsts_all = take(BANK)
        below = take(BANK)
        iota_w = take(P).bitcast(I32)
        theta_i = take(G).bitcast(I32)
        theta = take(G)
        theta_nt = take(G)
        chunks_below = take(G)
        row0 = take(G)
        row_i = take(G).bitcast(I32)
        base0 = take(G)
        fine = take(G)
        start = take(G)
        start_i = take(G).bitcast(I32)
        last_or = take(G)
        row1 = take(G)
        row1_i = take(G).bitcast(I32)
        dstf = take(G * ROW)
        tile_i = take(G * ROW).bitcast(I32)
        tilef = take(G * ROW)
        low_i = take(G * ROW).bitcast(I32)
        lowf = take(G * ROW)
        codef = take(G * ROW)
        inside = take(G * ROW)
        inside2 = take(G * ROW)
        hits = take(1)
        total = take(1)
        assert at[0] <= setup_end
        at[0] = region
        NCP = 8 * NCB
        l_code, l_src, l_dst = [take(NCP) for _ in range(3)]
        l_w = take(3 * NCP // 2).bitcast(BF16).rearrange("p (k c) -> p c k", k=3)
        assert at[0] <= region + 2 * W5 + 3 * W5 // 2
        list_i = staged[0][:, 0:2 * NCP].bitcast(I32)
        list_w = staged[0][:, 2 * NCP:3 * NCP]
        list_t = staged[0][:, 3 * NCP:4 * NCP].bitcast(I32)
        w_left = staged[1][:, 0:W5]

        at[0] = region
        X = take(NT * P)
        H = take(NT * P)
        big = take(max(3 * STREAM, 3 * NT * P // 2, NC))
        stream = [big[:, i * STREAM:(i + 1) * STREAM] for i in range(3)]
        bn_in = big[:, 0:NC]
        parts = big[:, 0:3 * NT * P // 2].bitcast(BF16)
        over_parts = big[:, 3 * NT * P // 2 - NC:3 * NT * P // 2]
        assert 3 * NT * P // 2 - NC >= NT * P // 2
        wslot = take(3 * P)
        bslot = take(3 * P)
        work = take(12 * P)
        mv = take(2 * NT)
        rstd = take(NT)
        nmr = take(NT)
        gamma, beta, bn_scale, bn_shift, b1col = [take(1) for _ in range(5)]
        bn_mv = take(2)
        ag = [work[:, i * P:(i + 1) * P] for i in (0, 1)]
        hb = [work[:, i * P:(i + 1) * P] for i in (2, 3)]
        hT = [work[:, i * P:(i + 1) * P] for i in (4, 5)]
        tmp = [work[:, i * P:(i + 1) * P] for i in (6, 7)]
        stat6 = work[:, 8 * P:8 * P + 6 * NT]
        gates_io = [work[:, 8 * P:10 * P], work[:, 10 * P:12 * P]]
        gates_g = ag
        stationary = [work[:, i * P:(i + 1) * P] for i in range(3)]
        rest_in = [work[:, i * BANK:(i + 1) * BANK].bitcast(BF16) for i in range(2)]
        whh = big[:, 0:3 * P]
        bihh = big[:, 3 * P:9 * P]
        zeros = big[:, 9 * P:10 * P]
        w = [wslot[:, i * P:(i + 1) * P] for i in range(3)]
        b = [bslot[:, i * P:(i + 1) * P] for i in range(3)]

        agg = PS[:, 0:7 * BANK]
        misc = [PS[:, k * BANK:k * BANK + P] for k in range(8)]
        gates_out = [PS[:, k * BANK:k * BANK + 3 * P] for k in (4, 5)]
        gate_prod_out = PS[:, 6 * BANK:6 * BANK + 3 * P]

        def sem(name):
            return ctx.enter_context(nc.semaphore(name))

        def tile(buf, t, n=P):
            return buf[:, ds(t * P, n)] if not isinstance(t, int) else buf[:, t * P:t * P + n]

        def part(k, t):
            return cols(parts, (3 * t + k) * P, P)

        def col(buf, c):
            return buf[:, ds(c, 1)] if not isinstance(c, int) else buf[:, c:c + 1]

        def cols(buf, c, n):
            return buf[:, ds(c, n)] if not isinstance(c, int) else buf[:, c:c + n]

        class Mark:
            def __init__(self, s, base):
                self.sem, self.base = s, base

        stages = {}

        def stage(name, step=NT):
            if name not in stages:
                stages[name] = [sem(name), 2]
            s, base = stages[name]
            stages[name][1] += step
            return Mark(s, base)

        def finished(eng, m, t):
            eng.wait_ge(m.sem, m.base + t + 1)

        def two_back(eng, m, t):
            eng.wait_ge(m.sem, m.base + t - 1)

        counts = {}

        def mark(name, step):
            if name not in counts:
                counts[name] = [sem(name), 0]
            s, base = counts[name]
            counts[name][1] += step
            return Mark(s, base)

        def tiles(eng, body):
            with eng.Fori(0, NT // 2) as i:
                body(2 * i, 0, P)
                body(2 * i + 1, 1, P)
            body(NT - 1, 0, LC)

        def tile_pairs(eng, body):
            with eng.Fori(0, NT // 2) as i:
                body([(2 * i, 0, P), (2 * i + 1, 1, P)])
            body([(NT - 1, 0, LC)])

        def skewed(eng, *parts):
            most = max(lag for lag, _ in parts)

            def step(s):
                for lag, body in parts:
                    if 0 <= s - lag < NT:
                        body(s - lag, (s - lag) % 2, LC if s - lag == NT - 1 else P)
            head = -(-most // 2) * 2
            for s in range(head):
                step(s)
            with eng.Fori(head // 2, NT // 2) as i:
                for j in range(2):
                    for lag, body in parts:
                        body(2 * i + (j - lag), (j - lag) % 2, P)
            for s in range(NT - 1, NT + most):
                step(s)

        edges_in = sem("edges_in")
        firsts_in = sem("firsts_in")
        pool_const = sem("pool_const")
        dve_chain = sem("dve_chain")
        all_chain = sem("all_chain")
        firsts_ready = sem("firsts_ready")
        firsts_spread = sem("firsts_spread")
        rows_ready = sem("rows_ready")
        gather0 = sem("gather0")
        gather1 = sem("gather1")
        codes_ready = sem("codes_ready")
        tables_turned = sem("tables_turned")
        hits_ready = sem("hits_ready")
        hits_summed = sem("hits_summed")
        flag_ready = sem("flag_ready")
        tables_ready = sem("tables_ready")
        list_in = sem("list_in")
        list_ready = sem("list_ready")
        hots_ready = sem("hots_ready")
        scaled_ready = sem("scaled_ready")
        slots_used = sem("slots_used")
        row_ready = sem("row_ready")
        row_out = sem("row_out")
        pairs_out = stage("pairs_out").sem
        rest_out = sem("rest_out")
        rest_saved = sem("rest_saved")
        rest_free = sem("rest_free")
        shifted = sem("shifted")
        stage_saved = [sem("stage_saved0"), sem("stage_saved1")]
        tile_turned = stage("tile_turned").sem
        turned = stage("groups_turned").sem
        turned_out = sem("turned_out")
        piece_saved = [sem("piece_saved0"), sem("piece_saved1")]
        counted = sem("counted")
        build_over = sem("build_over")
        act_over = sem("act_over")
        root_ready = sem("root_ready")
        degrees_ready = sem("degrees_ready")

        def pairs_before(t):
            return t * NPT

        def pairs_in(t):
            return NPL if isinstance(t, int) and t == NT - 1 else NPT

        def build_tiles(eng, body):
            for t in range(3):
                body(t, t % 2)
            with eng.Fori(1, (NT - 3) // 2) as i:
                body(2 * i + 1, 1)
                body(2 * i + 2, 0)
            body(NT - 2, 1)
            body(NT - 1, 0)

        def pair_loop(eng, t, first, body):
            q0 = pairs_before(t)
            with eng.Fori(0, (pairs_in(t) - first) // 2) as i:
                body(q0 + first + 2 * i, 0)
                body(q0 + first + 2 * i + 1, 1)

        def pairs_and_groups(t, pair, group):
            pairs, before = pairs_in(t), not isinstance(t, int) or t >= 1
            for k in range(pairs):
                pair(pairs_before(t) + k, k)
                if before and 0 < k <= NG:
                    group(t - 1, k - 1)
            for g in range(pairs - 1, NG):
                if before:
                    group(t - 1, g)

        def list_batches(eng, body):
            with eng.Fori(0, NW) as win:
                with eng.Fori(0, NCB) as i:
                    for r in range(4):
                        body((4 * NCB) * win + 4 * i + r, r, 8 * i + 2 * r)

        def irregular_flag(eng):
            eng.wait_ge(flag_ready, 1)
            return eng.value_load(flag.bitcast(I32)[0:1, 0:1], min_val=0, max_val=1)

        x_in = sem("x_in")
        wload = {k: sem("w_" + k) for k in ("p0", "e0", "p1", "e1", "p2", "p3", "bias3", "e3", "e4", "e6a", "e6b", "small")}

        class Pass:
            def __init__(self, streamed):
                self.done = mark("agg_done", 1)
                self.out = mark("agg_out", len(BANKS))
                if streamed:
                    self.loaded = [mark(f"unit_loaded{i}", 16 * len(range(i, 2 * NT, 3))) for i in range(3)]
                    self.units = mark("units_used", 2 * NT)
                    self.stat = mark("stationary_ready", NT)
                else:
                    self.rest_loaded = [mark(f"rest_loaded{i}", 16 * NT * len(RESTS) // 2) for i in range(2)]
                    self.rest_used = mark("rest_used", len(RESTS) * NT)

        agg0, agg1, agg2 = Pass(True), Pass(True), Pass(True)
        agg3, agg4, agg5, agg6 = [Pass(False) for _ in range(4)]

        def norm_marks():
            return [mark("norm_" + k, 1) for k in ("var", "root", "ready")]

        n0, n1, n2, n4 = norm_marks(), norm_marks(), norm_marks(), norm_marks()
        p0 = [stage(k) for k in ("relu", "turned", "hT", "prod", "out", "kept")]
        e0 = [stage(k) for k in ("copied", "prod", "sum", "turned", "act_out")]
        bn_var, bn_root, bn_ready = sem("bn_var"), sem("bn_root"), sem("bn_ready")
        p1 = [stage(k) for k in ("relu", "prod", "out", "taken")]
        p1_x = sem("p1_x")
        h_cleared = sem("h_cleared")
        e1 = [stage(k) for k in ("copied", "prod", "out", "taken")]
        p2 = [stage(k) for k in ("relu", "turned", "hT", "prod", "out")]
        e2 = [stage(k) for k in ("copied", "turned", "out", "taken")]
        p3 = [stage(k) for k in ("relu", "turned", "hT", "gates", "biased", "acts", "cell", "tanh", "out")]
        gate_prod, gate_bias, gate_ready = sem("gate_prod"), sem("gate_bias"), sem("gate_ready")
        e3 = [stage(k) for k in ("copied", "prod", "out", "taken")]
        e4 = [stage(k) for k in ("copied", "prod", "sum", "turned", "act_hT", "prod3", "out", "taken")]
        p4 = [stage(k) for k in ("relu", "out")]
        e5 = [stage(k) for k in ("copied", "turned", "out", "taken")]
        e6 = [stage(k) for k in ("copied", "turned", "sum", "turned2", "act_hT", "prod3", "tT", "prod2", "out", "taken", "taken2")]
        out_saved = sem("out_saved")

        def evacuate(eng, copy, a, dest, first):
            agg_end(eng, a)
            for c, m in BANKS[first::2]:
                copy(dest[:, c:c + m], agg[:, c:c + m]).then_inc(a.out.sem, 1)

        def agg_end(eng, a):
            eng.wait_ge(a.done.sem, a.done.base + 1)

        block = ctx.enter_context(nc.Block())

        @block.sync
        def _(sp):
            for s, _ in stages.values():
                sp.sem_inc(s, 2)
            sp.sem_inc(slots_used, 4)
            sp.sem_inc(shifted, 1)
            sp.sem_inc(rest_free, 1)
            sp.sem_inc(agg0.units.sem, 6)
            sp.sem_inc(agg3.rest_used.sem, 2)
            for k, v in enumerate((src, dst, edge_weight.bitcast(I32))):
                sp.dma_start(edge_rows[0:LASTROW, k * ROW:(k + 1) * ROW],
                             bass.AP(v.tensor, 0, [[STEP, LASTROW], [1, ROW]])).then_inc(edges_in, 16)
                sp.dma_start(edge_rows[LASTROW:NROWS, k * ROW:(k + 1) * ROW],
                             bass.AP(v.tensor, E - ROW, [[ROW, 1], [1, ROW]])).then_inc(edges_in, 16)
            sp.dma_start(firsts_i[0:1, 0:NCH], bass.AP(dst.tensor, 0, [[1, 1], [P, NCH]]), allow_slow_non_contiguous=True).then_inc(firsts_in, 16)

            irregular = irregular_flag(sp)
            with sp.If(irregular != 0):
                n = NCH if E % P == 0 else NCH - 1
                dests = (list_i[:, NCP:2 * NCP], list_i[:, 0:NCP], list_w)
                sp.wait_ge(tables_ready, 1)
                for v, d in zip((src, dst, edge_weight), dests):
                    sp.dma_start(d[:, 0:n], bass.AP(v.tensor, 0, [[1, P], [P, n]]),
                                 allow_slow_non_contiguous=True).then_inc(list_in, 16)
                    if E % P:
                        sp.dma_start(d[0:E % P, n:n + 1], bass.AP(v.tensor, n * P, [[1, E % P], [1, 1]])).then_inc(list_in, 16)

            def save_rest(q, _):
                sp.wait_ge(rest_out, q + 1)
                sp.dma_start(count_rest[:, :, ds(q * 2 * V, 2 * V)].rearrange("a p d -> p a d"),
                             rest_stage.rearrange("p (a d) -> p a d", a=NT)).then_inc(rest_saved, 16)
                sp.wait_ge(rest_saved, 16 * (q + 1))
                sp.sem_inc(rest_free, 1)

            def save_group(t, g):
                n = LC if isinstance(t, int) and t == NT - 1 else P
                a_rows = A[ds(t, 1), 0:n, :] if not isinstance(t, int) else A[t:t + 1, 0:n, :]
                m = min(BANK, NT * P - g * BANK)
                sp.wait_ge(turned_out, NG * t + g + 1)
                sp.dma_start(a_rows[:, :, g * BANK:g * BANK + m].rearrange("a p s -> (a p) s"),
                             piece[g % 2][0:n, 0:m]).then_inc(piece_saved[g % 2], 16)

            def save_tile(t, p, rest):
                pairs_and_groups(t, save_rest if rest else lambda q, k: None, save_group)
                n = LC if isinstance(t, int) and t == NT - 1 else P
                sp.wait_ge(pairs_out, 2 + pairs_before(t) + pairs_in(t))
                at_cols = AT[:, :, ds(t * P, n)] if not isinstance(t, int) else AT[:, :, t * P:t * P + n]
                sp.dma_start(at_cols.rearrange("a p d -> p a d"),
                             staged[p].rearrange("p (a d) -> p a d", a=NT)[:, :, 0:n]).then_inc(stage_saved[p], 16)

            def save_last():
                for g in range(NG):
                    save_group(NT - 1, g)

            with sp.If(irregular != 0):
                build_tiles(sp, lambda t, p: save_tile(t, p, True))
                save_last()
                sp.wait_ge(shifted, NW + NT + 1)
            with sp.Else():
                build_tiles(sp, lambda t, p: save_tile(t, p, False))
                save_last()
            sp.wait_ge(stage_saved[0], 16 * (NT // 2 + 1))
            sp.wait_ge(stage_saved[1], 16 * (NT // 2))
            sp.wait_ge(piece_saved[0], 16 * NT * ((NG + 1) // 2))
            sp.wait_ge(piece_saved[1], 16 * NT * (NG // 2))
            sp.wait_ge(counted, 1)
            sp.wait_ge(act_over, 1)
            sp.sem_inc(build_over, 1)

            def load_x(s):
                sp.dma_start(X[:, 0:(NT - 1) * P].rearrange("p (t d) -> p t d", t=NT - 1),
                             x[0:(NT - 1) * P, :].rearrange("(t p) d -> p t d", p=P)).then_inc(s, 16)
                sp.dma_start(X[0:NR, (NT - 1) * P:NT * P], x[(NT - 1) * P:N, :]).then_inc(s, 16)

            def load_w(slot, names, s):
                i = weight_at[names[0]]
                sp.dma_start(wslot[:, slot * P:(slot + len(names)) * P], weights[:, i * P:(i + len(names)) * P]).then_inc(s, 16)

            def load_b(slot, name, s):
                i = bias_at[name]
                sp.dma_start(b[slot], bass.AP(biases.tensor, i * P, [[0, P], [1, P]])).then_inc(s, 16)

            sp.wait_ge(h_cleared, 1)
            load_x(x_in)
            load_w(0, ["W1r"], wload["p0"])
            load_b(0, "b1l", wload["p0"])
            load_w(1, ["W1l"], wload["e0"])
            load_w(2, ["W2r"], wload["p1"])
            load_b(1, "b2l", wload["p1"])
            load_b(2, "L1b", wload["p2"])
            for k, d in enumerate((gamma, beta, b1col)):
                sp.dma_start(d, columns[:, k:k + 1], allow_slow_non_contiguous=True).then_inc(wload["small"], 16)

            def stream_matrix(a, M):
                def unit(u, n, t):
                    c, m = HALVES[u % 2]
                    sp.wait_ge(a.units.sem, a.units.base + n + 4)
                    k = P
                    if isinstance(t, int) and t == NT - 1 and M is A:
                        k = LC
                    rows = M[ds(t, 1), 0:k, c:c + m] if not isinstance(t, int) else M[t:t + 1, 0:k, c:c + m]
                    sp.dma_start(stream[u % 3][0:k, 0:m], rows.rearrange("a p s -> (a p) s")).then_inc(a.loaded[u % 3].sem, 16)
                with sp.Fori(0, NT // 3) as i:
                    for u in range(6):
                        unit(u, 6 * i + u, 3 * i + u // 2)
                for u in range(2):
                    unit(u, 2 * (NT - 1) + u, NT - 1)

            stream_matrix(agg0, AT)
            finished(sp, e0[2], NT - 1)
            load_x(p1_x)
            load_w(0, ["W2l"], wload["e1"])
            load_w(1, ["L1W"], wload["p2"])
            finished(sp, p1[0], NT - 1)
            stream_matrix(agg1, AT)
            finished(sp, e1[2], NT - 1)
            stream_matrix(agg2, A)
            finished(sp, p2[4], NT - 1)
            load_w(0, ["Wih_i", "Wih_o", "Wih_g"], wload["p3"])
            agg_end(sp, agg2)
            i = weight_at["Whh_i"]
            sp.dma_start(whh, weights[:, i * P:(i + 3) * P]).then_inc(wload["bias3"], 16)
            i = bias_at["bih_i"]
            sp.dma_start(bihh, bass.AP(biases.tensor, i * P, [[0, P], [1, 6 * P]])).then_inc(wload["bias3"], 16)
            finished(sp, p3[8], NT - 1)
            load_w(0, ["W1"], wload["e3"])
            load_b(0, "b1", wload["e3"])
            load_w(1, ["W2", "W3"], wload["e4"])
            load_b(1, "b2", wload["e4"])
            load_b(2, "b3", wload["e4"])

            def stream_rest(a, before):
                with sp.If(irregular != 0):
                    for s, t in before:
                        finished(sp, s, t)

                    def unit(h, t):
                        c, m = RESTS[h]
                        sp.wait_ge(a.rest_used.sem, a.rest_used.base + len(RESTS) * t + h + 1)
                        sp.dma_start(rest_in[h % 2][:, 0:m], count_rest[ds(t, 1), :, c:c + m]
                                     .rearrange("a p s -> (a p) s")).then_inc(a.rest_loaded[h % 2].sem, 16)
                    with sp.Fori(0, NT) as t:
                        for h in range(len(RESTS)):
                            unit(h, t)

            stream_rest(agg3, [(p3[8], NT - 1)])
            stream_rest(agg4, [(e3[2], NT - 1)])
            stream_rest(agg5, [(p4[1], NT - 1)])
            finished(sp, e4[6], NT - 1)
            load_w(0, ["w1", "w2"], wload["e6a"])
            load_b(0, "w2b", wload["e6b"])
            stream_rest(agg6, [(e5[2], NT - 1)])

            def save_out(t, p, n):
                finished(sp, e6[8], t)
                if n == P:
                    sp.dma_start(out[ds(t * P, P), :], tile(X, t)).then_inc(out_saved, 16)
                else:
                    sp.dma_start(out[(NT - 1) * P:N, :], X[0:NR, (NT - 1) * P:NT * P]).then_inc(out_saved, 16)
            tiles(sp, save_out)
            sp.wait_ge(out_saved, 16 * NT)

        @block.gpsimd
        def _(pool):
            nc.gpsimd.iota(iota[:, 0:max(CODE, P)], [[1, max(CODE, P)]], base=0, channel_multiplier=0,
                           allow_small_or_imprecise_dtypes=True).then_inc(pool_const, 1)
            nc.gpsimd.iota(theta_i, [[V * P, G]], base=0, channel_multiplier=V).then_inc(pool_const, 1)
            nc.gpsimd.iota(iota_w, [[1, P]], base=0, channel_multiplier=-1).then_inc(pool_const, 1)
            nc.gpsimd.memset(ones, 1.0).then_inc(pool_const, 1)
            nc.gpsimd.memset(onesb, 1.0).then_inc(pool_const, 1)
            nc.gpsimd.memset(onesrow, 1.0).then_inc(pool_const, 1)
            nc.gpsimd.memset(count, 0.0).then_inc(pool_const, 1)
            pool.wait_ge(edges_in, 96)
            for s, rows, done in ((1, row_i, gather0), (2, row1_i, gather1)):
                pool.wait_ge(rows_ready, s)
                for g in range(G):
                    nc.gpsimd.indirect_dma_start(
                        out=gathered[:, g * 3 * ROW:(g + 1) * 3 * ROW], out_offset=None, in_=edge_rows,
                        in_offset=bass.IndirectOffsetOnAxis(ap=rows[:, g:g + 1], axis=0)).then_inc(done, 16)
            def scale(n, place, w):
                pool.wait_ge(hots_ready, n + 1)
                each = hots[place].rearrange("p (s e) -> p s e", s=2)[:, :, None, :].to_broadcast([P, 2, 3, P])
                nc.gpsimd.tensor_tensor(hots_w[place].rearrange("p (s k e) -> p s k e", s=2, k=3), each,
                                        w.to_broadcast([P, 2, 3, P]), ALU.mult).then_inc(scaled_ready, 1)

            irregular = irregular_flag(pool)
            pool.wait_ge(tables_ready, 1)
            with pool.If(irregular != 0):
                pool.wait_ge(list_ready, 1)
                list_batches(pool, lambda n, r, c: scale(n, r, l_w[:, ds(c, 2), :][:, :, :, None]))
            with pool.Else():
                def pair_scaled(q, j):
                    for v in range(2):
                        scale(2 * q + v, 2 * j + v, t_w[:, :, :, ds(2 * q + v, 1)])
                build_tiles(pool, lambda t, p: pair_loop(pool, t, 0, pair_scaled))
            pool.wait_ge(build_over, 1)
            nc.gpsimd.memset(X[:, (NT - 1) * P:NT * P], 0.0).then_inc(h_cleared, 1)

            def keep(t, p, n):
                finished(pool, p0[0], t)
                nc.gpsimd.tensor_copy(tile(H, t), hb[p]).then_inc(p0[5].sem, 1)
            tiles(pool, keep)

            def feed(a, before):
                finished(pool, before, NT - 1)

                def one(t, j):
                    pool.wait_ge(a.units.sem, a.units.base + 2 * t + 2)
                    nc.gpsimd.tensor_copy(stationary[j], tile(H, t)).then_inc(a.stat.sem, 1)
                with pool.Fori(0, NT // 3) as i:
                    for j in range(3):
                        one(3 * i + j, j)
                one(NT - 1, 0)
            finished(pool, p0[5], NT - 1)
            feed(agg0, p0[4])
            finished(pool, e0[2], NT - 1)
            nc.gpsimd.memset(H[:, (NT - 1) * P:NT * P], 0.0).then_inc(h_cleared, 1)
            feed(agg1, p1[2])
            feed(agg2, p2[4])

        @block.scalar
        def _(act):
            irregular = irregular_flag(act)

            def evacuate_pair(slots, t, p, q, j, place):
                act.wait_ge(slots_used, 4 + slots * (q + 1))
                src_w = PS[:, 2 * j * BANK:2 * (j + 1) * BANK].rearrange("p (v c) -> p v c", v=2)
                d = staged[p].rearrange("p (a d) -> p a d", a=NT)[:, :, place:place + 2 * V]
                nc.scalar.copy(d.rearrange("p a (v d) -> p v a d", v=2),
                               src_w[:, :, 0:CODE].rearrange("p v (d a) -> p v a d", d=V))
                c = C.rearrange("p (a d) -> p a d", a=NT)[:, :, ds(q * 2 * V, 2 * V)]
                nc.scalar.copy(c.rearrange("p a (v d) -> p v a d", v=2),
                               src_w[:, :, CODE:2 * CODE].rearrange("p v (d a) -> p v a d", d=V)).then_inc(pairs_out, 1)

            def group_out(t, g, with_counts):
                n = LC if isinstance(t, int) and t == NT - 1 else P
                if g == 0 and with_counts:
                    act.wait_ge(row_ready, t + 1)
                    nc.scalar.copy(degree_row[0:1, 0:n], PS[0:1, 7 * BANK:7 * BANK + n]).then_inc(row_out, 1)
                m = min(BANK, NT * P - g * BANK)
                before = (NG + 1) // 2 * t + g // 2 if g % 2 == 0 else NG // 2 * t + g // 2
                act.wait_ge(turned, 3 + NG * t + g)
                if not isinstance(t, int) or before > 0:
                    act.wait_ge(piece_saved[g % 2], 16 * before)
                nc.scalar.copy(piece[g % 2][0:n, 0:m], PS[0:n, (4 + g % 2) * BANK:(4 + g % 2) * BANK + m])\
                    .then_inc(turned_out, 1)

            def build_tile(per_pair, t, p, with_counts):
                def pair_out(q, k):
                    if k == 0 and (not isinstance(t, int) or t >= 2):
                        act.wait_ge(stage_saved[p], (t - p) * 8)
                        act.wait_ge(tile_turned, 2 + t - 1)
                    evacuate_pair(per_pair, t, p, q, k % 2, k * 2 * V)
                pairs_and_groups(t, pair_out, lambda t, g: group_out(t, g, with_counts))

            with act.If(irregular != 0):
                act.wait_ge(list_ready, 1)
                build_tiles(act, lambda t, p: build_tile(2 * (4 * NCB + 1), t, p, False))
                for g in range(NG):
                    group_out(NT - 1, g, False)
            with act.Else():
                build_tiles(act, lambda t, p: build_tile(2, t, p, True))
                for g in range(NG):
                    group_out(NT - 1, g, True)
            act.wait_ge(counted, 1)
            act.wait_ge(pool_const, 7)
            nc.scalar.copy(count[:, 0:NT - 1], PS[:, 6 * BANK:6 * BANK + NT - 1])
            nc.scalar.copy(count[0:LC, NT - 1:NT], PS[0:LC, 6 * BANK + NT - 1:6 * BANK + NT]).then_inc(act_over, 1)
            act.wait_ge(act_over, 1)
            act.wait_ge(build_over, 1)
            nc.scalar.activation(dinv, count, ACT.Sqrt, bias=1.0, scale=1.0).then_inc(root_ready, 1)

            def root(s, d):
                finished(act, s[0], 0)
                nc.scalar.activation(d, d, ACT.Sqrt).then_inc(s[1].sem, 1)

            def relu_norm(t, dest, done):
                nc.scalar.activation(dest, tile(X, t), ACT.Relu, bias=col(nmr, t), scale=col(rstd, t)).then_inc(done.sem, 1)

            def copy_agg(s, a, used, source=H):
                evacuate(act, nc.scalar.copy, a, source, 0)
                finished(act, a.out, len(BANKS) - 1)

                def one(t, p, n):
                    two_back(act, used, t)
                    nc.scalar.copy(ag[p][:, 0:n], cols(source, t * P, n)).then_inc(s.sem, 1)
                return one

            root(n0, rstd)
            finished(act, n0[2], 0)

            def f(t, p, n):
                two_back(act, p0[1], t)
                two_back(act, p0[5], t)
                relu_norm(t, hb[p], p0[0])
            tiles(act, f)

            one = copy_agg(e0[0], agg0, e0[1])

            def turn(t, p, n):
                finished(act, e0[3], t)
                m = n if n == P else NR
                nc.scalar.copy(cols(bn_in, t * P, m), misc[2 + p][:, 0:m]).then_inc(e0[4].sem, 1)
            skewed(act, (0, one), (2, turn))
            act.wait_ge(bn_var, 1)
            nc.scalar.activation(bn_scale, bn_scale, ACT.Sqrt).then_inc(bn_root, 1)
            act.wait_ge(bn_ready, 1)

            def f(t, p, n):
                two_back(act, p1[1], t)
                m = n if n == P else NR
                nc.scalar.activation(hT[p][:, 0:m], cols(bn_in, t * P, m), ACT.Relu, bias=bn_shift, scale=bn_scale)\
                    .then_inc(p1[0].sem, 1)
            tiles(act, f)
            tiles(act, copy_agg(e1[0], agg1, e1[1]))
            root(n1, rstd)
            finished(act, n1[2], 0)

            def f(t, p, n):
                two_back(act, p2[1], t)
                relu_norm(t, hb[p], p2[0])
            tiles(act, f)
            tiles(act, copy_agg(e2[0], agg2, e2[1]))
            root(n2, rstd)
            finished(act, n2[2], 0)

            def h(t, p, n):
                two_back(act, p3[1], t)
                relu_norm(t, hb[p], p3[0])

            def gates(t, p, n):
                finished(act, p3[4], t)
                nc.scalar.activation(gates_io[p], gates_io[p], ACT.Sigmoid)
                nc.scalar.activation(gates_g[p], gates_g[p], ACT.Tanh).then_inc(p3[5].sem, 1)

            def of_cell(t, p, n):
                finished(act, p3[6], t)
                nc.scalar.activation(tmp[p], tmp[p], ACT.Tanh).then_inc(p3[7].sem, 1)
            skewed(act, (0, h), (2, gates), (3, of_cell))
            tiles(act, copy_agg(e3[0], agg3, e3[1]))

            one4 = copy_agg(e4[0], agg4, e4[1])

            def turned_back(t, p, n):
                finished(act, e4[3], t)
                two_back(act, e4[5], t)
                nc.scalar.copy(hT[p][:, 0:n], misc[2 + p][:, 0:n]).then_inc(e4[4].sem, 1)
            skewed(act, (0, one4), (2, turned_back))
            root(n4, rstd)
            finished(act, n4[2], 0)

            def f(t, p, n):
                relu_norm(t, tile(H, t), p4[0])
            tiles(act, f)
            tiles(act, copy_agg(e5[0], agg5, e5[1], over_parts))

            one6 = copy_agg(e6[0], agg6, e6[1], over_parts)

            act.wait_ge(wload["small"], 48)

            def hidden_T(t, p, n):
                finished(act, e6[3], t)
                two_back(act, e6[5], t)
                nc.scalar.copy(hT[p][:, 0:n], misc[2 + p][:, 0:n]).then_inc(e6[4].sem, 1)

            def middle_T(t, p, n):
                finished(act, e6[5], t)
                two_back(act, e6[7], t)
                nc.scalar.activation(tmp[p][:, 0:n], misc[4 + p][:, 0:n], ACT.Identity, bias=b1col, scale=1.0).then_inc(e6[6].sem, 1)
            skewed(act, (0, one6), (2, hidden_T), (4, middle_T))

        @block.vector
        def _(dve):
            def chain(s):
                done = [0]

                def step(ins):
                    done[0] += 1
                    ins.then_inc(s, 1)
                    dve.wait_ge(s, done[0])
                return step
            link = chain(dve_chain)

            def links(per_tile):
                m = mark("tile_links", per_tile * NT)
                return m.sem, lambda t, k: dve.wait_ge(m.sem, m.base + per_tile * t + k)

            def pair_links(per_tile):
                m = mark("tile_links", per_tile * NT)
                return m.sem, lambda pair, i, k: dve.wait_ge(m.sem, m.base + per_tile * pair[0][0] + (k - 1) * len(pair) + i + 1)

            dve.wait_ge(pool_const, 7)
            link(nc.vector.tensor_scalar(ident, iota_w, 0.0, None, ALU.is_equal))
            link(nc.vector.tensor_copy(identb, ident))
            link(nc.vector.tensor_copy(theta, theta_i))
            link(nc.vector.tensor_scalar(theta_nt, theta, float(NT), None, ALU.mult))
            dve.wait_ge(firsts_in, 16)
            nc.vector.tensor_copy(firsts[0:1, 0:NCH], firsts_i[0:1, 0:NCH]).then_inc(firsts_ready, 1)
            dve.wait_ge(firsts_spread, 1)
            link(nc.vector.tensor_copy(firsts_all[:, 0:NCH], PS[:, 7 * BANK:7 * BANK + NCH]))
            for g in range(G):
                link(nc.vector.tensor_scalar(below[:, 0:NCH], firsts_all[:, 0:NCH], theta[:, g:g + 1], 0.0,
                                             ALU.is_lt, ALU.add, accum_out=chunks_below[:, g:g + 1]))
            link(nc.vector.tensor_scalar(row0, chunks_below, float(P // STEP), -float(P // STEP), ALU.mult, ALU.add))
            link(nc.vector.tensor_scalar(row0, row0, 0.0, float(LASTROW), ALU.max, ALU.min))
            nc.vector.tensor_copy(row_i, row0).then_inc(rows_ready, 1)
            link(nc.vector.tensor_scalar(base0, row0, float(STEP), float(E - ROW), ALU.mult, ALU.min))
            dve.wait_ge(gather0, 16 * G)
            gv = gathered.rearrange("p (g k r) -> p g k r", g=G, k=3)
            d3 = dstf.rearrange("p (g r) -> p g r", g=G)
            link(nc.vector.tensor_copy(d3, gv[:, :, 1, :]))
            for g in range(G):
                link(nc.vector.tensor_scalar(below[:, 0:ROW], dstf[:, g * ROW:(g + 1) * ROW], theta[:, g:g + 1], 0.0,
                                             ALU.is_lt, ALU.add, accum_out=fine[:, g:g + 1]))
            link(nc.vector.tensor_tensor(start, base0, fine, ALU.add))
            link(nc.vector.tensor_copy(start_i, start))
            link(nc.vector.tensor_scalar(start_i, start_i, STEP.bit_length() - 1, None, ALU.arith_shift_right))
            link(nc.vector.tensor_copy(row1, start_i))
            link(nc.vector.tensor_scalar(last_or, start, float(E - ROW), float(LASTROW), ALU.is_ge, ALU.mult))
            link(nc.vector.tensor_tensor(row1, row1, last_or, ALU.max))
            link(nc.vector.tensor_scalar(row1, row1, float(LASTROW), None, ALU.min))
            nc.vector.tensor_copy(row1_i, row1).then_inc(rows_ready, 1)
            dve.wait_ge(gather1, 16 * G)
            t3, l3 = tile_i.rearrange("p (g r) -> p g r", g=G), low_i.rearrange("p (g r) -> p g r", g=G)
            link(nc.vector.tensor_copy(d3, gv[:, :, 1, :]))
            link(nc.vector.tensor_scalar(t3, gv[:, :, 0, :], 7, None, ALU.arith_shift_right))
            link(nc.vector.tensor_scalar(l3, gv[:, :, 0, :], P - 1, None, ALU.bitwise_and))
            link(nc.vector.tensor_copy(tilef, tile_i))
            link(nc.vector.tensor_copy(lowf, low_i))
            link(nc.vector.scalar_tensor_tensor(out=codef, in0=dstf, scalar=float(NT), in1=tilef, op0=ALU.mult, op1=ALU.add))
            for g in range(G):
                link(nc.vector.tensor_scalar(codef[:, g * ROW:(g + 1) * ROW], codef[:, g * ROW:(g + 1) * ROW],
                                             theta_nt[:, g:g + 1], None, ALU.subtract))
            link(nc.vector.tensor_scalar(inside, codef, 0.0, None, ALU.is_ge))
            link(nc.vector.scalar_tensor_tensor(out=inside2, in0=codef, scalar=float(CODE), in1=inside, op0=ALU.is_lt, op1=ALU.mult))
            nc.vector.reduce_sum(hits, inside2, mybir.AxisListType.X).then_inc(codes_ready, 1)
            dve.wait_ge(hits_summed, 1)
            nc.vector.tensor_scalar(flag.bitcast(I32)[0:1, :], PS[0:1, 6 * BANK:6 * BANK + 1], float(E), None, ALU.not_equal)\
                .then_inc(flag_ready, 1)
            dve.wait_ge(tables_turned, 1)
            for q, tab in enumerate((t_code, t_src, w_left)):
                for k in range(2):
                    link(nc.vector.tensor_copy(tab[:, k * NW:(k + 1) * NW], PS[:, (2 * q + k) * BANK:(2 * q + k) * BANK + NW]))

            def split_weights(link, parts, left):
                for k, part in enumerate(parts):
                    link(nc.vector.tensor_copy(part, left))
                    if k < 2:
                        link(nc.vector.tensor_tensor(left, left, part, ALU.subtract))
            left = w_left.rearrange("p (h v) -> p h v", h=2)
            split_weights(link, [t_w[:, :, k] for k in range(3)], left)

            def place_hots(place, n, code, low):
                dve.wait_ge(slots_used, n + 1)
                for s in range(2):
                    nc.vector.tensor_scalar(hot[place][s], iota[:, 0:P], low[s], None, ALU.is_equal)
                    last = nc.vector.tensor_scalar(code_hot[place][s], iota[:, 0:CODE], code[s], None, ALU.is_equal)
                return last.then_inc(hots_ready, 1)

            def pair_hots(q, j):
                for v in range(2):
                    place_hots(2 * j + v, 2 * q + v, *[[col(tab, s * NW + 2 * q + v) for s in (0, 1)] for tab in (t_code, t_src)])

            irregular = irregular_flag(dve)
            with dve.If(irregular != 0):
                lks = chain(all_chain)
                lks(nc.vector.memset(zerosb, 0.0))
                lks(nc.vector.memset(list_i, -1))
                lks(nc.vector.memset(list_w, 0.0))
                nc.vector.memset(hits, 0.0).then_inc(tables_ready, 1)
                dve.wait_ge(list_in, 16 * 3 * (2 if E % P else 1))
                lks(nc.vector.tensor_copy(l_dst, list_i[:, 0:NCP]))
                lks(nc.vector.tensor_scalar(list_t, list_i[:, NCP:2 * NCP], 7, None, ALU.arith_shift_right))
                lks(nc.vector.tensor_copy(l_src, list_t))
                lks(nc.vector.scalar_tensor_tensor(out=l_code, in0=l_dst, scalar=float(NT), in1=l_src, op0=ALU.mult, op1=ALU.add))
                lks(nc.vector.tensor_scalar(list_t, list_i[:, NCP:2 * NCP], P - 1, None, ALU.bitwise_and))
                lks(nc.vector.tensor_copy(l_src, list_t))
                split_weights(lks, [l_w[:, :, k] for k in range(3)], list_w)
                nc.vector.memset(rest_stage, 0.0).then_inc(list_ready, 1)

                def pair_of_all(q, j):
                    for v in range(2):
                        win = 2 * q + v
                        with dve.Fori(0, NCB) as i:
                            dve.wait_ge(shifted, win + 1)
                            for r in range(4):
                                place_hots(r, (4 * NCB) * win + 4 * i + r + win,
                                           *[[col(tab, 8 * i + 2 * r + s) for s in (0, 1)] for tab in (l_code, l_src)])
                        dve.wait_ge(hots_ready, 4 * NCB * (win + 1))
                        nc.vector.tensor_scalar(l_code, l_code, float(CODE), None, ALU.subtract).then_inc(shifted, 1)
                    dve.wait_ge(pairs_out, 2 + q + 1)
                    dve.wait_ge(rest_free, q + 1)
                    r = rest_stage.rearrange("p (a v d) -> p v a d", a=NT, v=2)
                    full = PS[:, 2 * j * BANK:2 * (j + 1) * BANK].rearrange("p (v c) -> p v c", v=2)[:, :, CODE:2 * CODE]
                    kept = C.rearrange("p (a d) -> p a d", a=NT)[:, :, ds(q * 2 * V, 2 * V)]
                    for v in range(2):
                        last = nc.vector.tensor_tensor(r[:, v], full[:, v].rearrange("p (d a) -> p a d", d=V),
                                                       kept[:, :, v * V:(v + 1) * V], ALU.subtract)
                    last.then_inc(rest_out, 1)
                build_tiles(dve, lambda t, p: pair_loop(dve, t, 0, pair_of_all))
                with dve.Fori(0, NT) as t:
                    with dve.Fori(0, NCB) as i:
                        dve.wait_ge(shifted, NW + t + 1)
                        for r in range(4):
                            dve.wait_ge(slots_used, (NW + t) * (4 * NCB + 1) + 4 * i + r + 1)
                            for s in range(2):
                                last = nc.vector.tensor_scalar(hot[r][s], iota[:, 0:P], col(l_dst, 8 * i + 2 * r + s), None, ALU.is_equal)
                            last.then_inc(hots_ready, 1)
                    dve.wait_ge(hots_ready, 4 * NCB * (NW + t + 1))
                    nc.vector.tensor_scalar(l_dst, l_dst, float(P), None, ALU.subtract).then_inc(shifted, 1)
            with dve.Else():
                nc.vector.memset(zerosb, 0.0).then_inc(tables_ready, 1)
                build_tiles(dve, lambda t, p: pair_loop(dve, t, 0, pair_hots))

            dve.wait_ge(root_ready, 1)

            lk = link
            lk(nc.vector.tensor_scalar(rcount, count, 1.0, None, ALU.max))
            lk(nc.vector.reciprocal(rcount, rcount))
            lk(nc.vector.reciprocal(dinv, dinv))
            lk(nc.vector.tensor_scalar(half_dinv, dinv, 0.5, None, ALU.mult))

            def norm_params(s):
                st = stat6.rearrange("p (t k) -> p t k", k=6)
                mean, var = mv[:, 0:NT], mv[:, NT:2 * NT]
                link(nc.vector.tensor_tensor(nmr, st[:, :, 1], st[:, :, 4], ALU.subtract))
                link(nc.vector.tensor_tensor(mean, st[:, :, 1], st[:, :, 4], ALU.add))
                link(nc.vector.tensor_tensor(var, st[:, :, 2], st[:, :, 5], ALU.add))
                link(nc.vector.scalar_tensor_tensor(out=nmr, in0=nmr, scalar=0.25, in1=nmr, op0=ALU.mult, op1=ALU.mult))
                link(nc.vector.scalar_tensor_tensor(out=var, in0=var, scalar=1.0 / D, in1=nmr, op0=ALU.mult, op1=ALU.add))
                nc.vector.tensor_scalar(rstd, var, EPS, None, ALU.add).then_inc(s[0].sem, 1)
                finished(dve, s[1], 0)
                link(nc.vector.reciprocal(rstd, rstd))
                nc.vector.scalar_tensor_tensor(out=nmr, in0=mean, scalar=-0.5, in1=rstd, op0=ALU.mult, op1=ALU.mult)\
                    .then_inc(s[2].sem, 1)

            def tile_stats(t):
                return nc.vector.bn_stats(cols(stat6, 6 * t, 6), tile(X, t))

            s0, linked0 = links(1)
            dve.wait_ge(x_in, 32)
            with dve.Fori(0, NT) as t:
                tile_stats(t).then_inc(s0, 1)
            linked0(NT - 1, 1)
            norm_params(n0)
            dve.wait_ge(wload["p0"], 32)

            def hT_of(s):
                def f(t, p, n):
                    finished(dve, s[0], t)
                    two_back(dve, s[2], t)
                    nc.vector.tensor_copy(hT[p], misc[p]).then_inc(s[1].sem, 1)
                return f

            def f(t, p, n):
                finished(dve, p0[3], t)
                nc.vector.tensor_tensor(tile(X, t), misc[2 + p], b[0], ALU.add).then_inc(p0[4].sem, 1)
            skewed(dve, (0, hT_of(p0[1:4])), (1, f))

            evacuate(dve, nc.vector.tensor_copy, agg0, H, 1)

            def f(t, p, n):
                finished(dve, e0[1], t)
                two_back(dve, e0[3], t)
                nc.vector.scalar_tensor_tensor(out=hb[p][0:n], in0=misc[p][0:n], scalar=col(rcount, t)[0:n],
                                               in1=tile(X, t)[0:n], op0=ALU.mult, op1=ALU.add).then_inc(e0[2].sem, 1)
            tiles(dve, f)
            finished(dve, e0[4], NT - 1)
            lk = link
            pieces = [(c, min(BANK, N - c)) for c in range(0, N, BANK)]
            for i, (c, m) in enumerate(pieces):
                ins = nc.vector.bn_stats(stat6[:, 6 * i:6 * i + 6], bn_in[:, c:c + m])
            lk(ins)
            lk(nc.vector.bn_aggr(bn_mv, stat6[:, 0:6 * len(pieces)]))
            nc.vector.tensor_scalar(bn_scale, bn_mv[:, 1:2], EPS, None, ALU.add).then_inc(bn_var, 1)
            dve.wait_ge(bn_root, 1)
            dve.wait_ge(wload["small"], 48)
            lk(nc.vector.reciprocal(bn_scale, bn_scale))
            lk(nc.vector.tensor_tensor(bn_scale, bn_scale, gamma, ALU.mult))
            lk(nc.vector.tensor_tensor(bn_shift, bn_mv[:, 0:1], bn_scale, ALU.mult))
            nc.vector.tensor_tensor(bn_shift, beta, bn_shift, ALU.subtract).then_inc(bn_ready, 1)
            dve.wait_ge(p1_x, 32)
            dve.wait_ge(wload["p1"], 32)
            dve.wait_ge(h_cleared, 2)

            def f(t, p, n):
                m = n if n == P else NR
                finished(dve, p1[1], t)
                nc.vector.tensor_copy(tile(H, t)[0:m], misc[p][0:m])
                nc.vector.tensor_tensor(tile(X, t)[0:m], misc[2 + p][0:m], tile(X, t)[0:m], ALU.add).then_inc(p1[3].sem, 1)

            def biased(t, p, n):
                finished(dve, p1[3], t)
                nc.vector.tensor_tensor(tile(X, t), tile(X, t), b[1], ALU.add).then_inc(p1[2].sem, 1)
            skewed(dve, (0, f), (1, biased))

            evacuate(dve, nc.vector.tensor_copy, agg1, H, 1)

            def stats_of(s):
                def f(t, p, n):
                    finished(dve, s[0], t)
                    tile_stats(t).then_inc(s[1].sem, 1)
                return f

            def f(t, p, n):
                finished(dve, e1[1], t)
                nc.vector.scalar_tensor_tensor(out=tile(X, t)[0:n], in0=misc[p][0:n], scalar=col(rcount, t)[0:n],
                                               in1=tile(X, t)[0:n], op0=ALU.mult, op1=ALU.add).then_inc(e1[3].sem, 1)
            skewed(dve, (0, f), (1, stats_of([e1[3], e1[2]])))
            finished(dve, e1[2], NT - 1)
            norm_params(n1)
            dve.wait_ge(wload["p2"], 32)

            def f(t, p, n):
                finished(dve, p2[3], t)
                nc.vector.tensor_tensor(tile(H, t), misc[2 + p], b[2], ALU.add).then_inc(p2[4].sem, 1)
            skewed(dve, (0, hT_of(p2[1:4])), (1, f))

            evacuate(dve, nc.vector.tensor_copy, agg2, H, 1)

            def f(t, p, n):
                finished(dve, e2[1], t)
                nc.vector.tensor_tensor(tile(X, t)[0:n], misc[p][0:n], tile(X, t)[0:n], ALU.add).then_inc(e2[3].sem, 1)
            skewed(dve, (0, f), (1, stats_of([e2[3], e2[2]])))
            finished(dve, e2[2], NT - 1)
            norm_params(n2)
            lk = link
            agg_end(dve, agg2)
            nc.vector.memset(zeros, 0.0).then_inc(gate_bias, 1)
            dve.wait_ge(wload["bias3"], 32)
            nc.vector.tensor_tensor(bslot, bihh[:, 0:3 * P], bihh[:, 3 * P:6 * P], ALU.add).then_inc(gate_bias, 1)
            dve.wait_ge(gate_bias, 2)
            dve.wait_ge(gate_prod, 1)
            nc.vector.tensor_tensor(bslot, bslot, gate_prod_out, ALU.add).then_inc(gate_ready, 1)
            dve.wait_ge(gate_ready, 1)

            def split_high(u, t):
                return nc.vector.tensor_copy(part(0, t), u)

            def split_rest(u, t):
                return nc.vector.tensor_tensor(u, u, part(0, t), ALU.subtract)

            def split_middle(u, t):
                return nc.vector.tensor_copy(part(1, t), u)

            def split_low(u, t):
                return nc.vector.tensor_tensor(part(2, t), u, part(1, t), ALU.subtract)

            s3, linked3 = links(4)

            def gate_io(t, p, n):
                finished(dve, p3[3], t)
                nc.vector.tensor_tensor(gates_io[p], gates_out[p][:, 0:2 * P], bslot[:, 0:2 * P], ALU.add)

            def gate_g(t, p, n):
                nc.vector.tensor_tensor(gates_g[p], gates_out[p][:, 2 * P:3 * P], bslot[:, 2 * P:3 * P], ALU.add)\
                    .then_inc(p3[4].sem, 1)

            def cell(t, p, n):
                finished(dve, p3[5], t)
                two_back(dve, p3[8], t)
                nc.vector.tensor_tensor(tmp[p], gates_io[p][:, 0:P], gates_g[p], ALU.mult).then_inc(p3[6].sem, 1)

            def hidden(t, p, n):
                finished(dve, p3[7], t)
                nc.vector.scalar_tensor_tensor(out=tmp[p], in0=tmp[p], scalar=col(dinv, t), in1=gates_io[p][:, P:2 * P],
                                               op0=ALU.mult, op1=ALU.mult).then_inc(s3, 1)

            def high(t, p, n):
                linked3(t, 1)
                split_high(tmp[p], t).then_inc(s3, 1)

            def rest(t, p, n):
                linked3(t, 2)
                split_rest(tmp[p], t).then_inc(s3, 1)

            def middle(t, p, n):
                linked3(t, 3)
                split_middle(tmp[p], t).then_inc(s3, 1)

            def low(t, p, n):
                linked3(t, 4)
                split_low(tmp[p], t).then_inc(p3[8].sem, 1)
            skewed(dve, (4, hidden), (0, hT_of(p3[1:4])), (4, high), (2, gate_io), (4, rest), (2, gate_g), (4, middle),
                   (3, cell), (4, low))

            def split_pair(pair, s, linked, k, done):
                for i, (t, p, n) in enumerate(pair):
                    linked(pair, i, k)
                    split_high(tmp[p], t).then_inc(s, 1)
                for i, (t, p, n) in enumerate(pair):
                    linked(pair, i, k + 1)
                    split_rest(tmp[p], t).then_inc(s, 1)
                for i, (t, p, n) in enumerate(pair):
                    linked(pair, i, k + 2)
                    split_middle(tmp[p], t).then_inc(s, 1)
                for i, (t, p, n) in enumerate(pair):
                    linked(pair, i, k + 3)
                    split_low(tmp[p], t).then_inc(done.sem, 1)

            dve.wait_ge(wload["e3"], 32)

            s, linked = pair_links(4)

            evacuate(dve, nc.vector.tensor_copy, agg3, H, 1)

            def f(pair, s=s, linked=linked):
                for t, p, n in pair:
                    finished(dve, e3[1], t)
                    two_back(dve, e3[2], t)
                    nc.vector.scalar_tensor_tensor(out=tmp[p][0:n], in0=misc[p][0:n], scalar=col(dinv, t)[0:n], in1=b[0][0:n],
                                                   op0=ALU.mult, op1=ALU.add).then_inc(e3[3].sem, 1)
                for t, p, n in pair:
                    finished(dve, e3[3], t)
                    nc.vector.tensor_scalar(tmp[p], tmp[p], 0.0, col(dinv, t), ALU.max, ALU.mult).then_inc(s, 1)
                split_pair(pair, s, linked, 1, e3[2])
            tile_pairs(dve, f)

            dve.wait_ge(wload["e4"], 48)

            s, linked = links(1)

            evacuate(dve, nc.vector.tensor_copy, agg4, H, 1)

            def f(t, p, n):
                finished(dve, e4[1], t)
                two_back(dve, e4[3], t)
                nc.vector.scalar_tensor_tensor(out=hb[p][0:n], in0=misc[p][0:n], scalar=col(dinv, t)[0:n], in1=b[1][0:n],
                                               op0=ALU.mult, op1=ALU.add).then_inc(e4[2].sem, 1)

            def biased(t, p, n):
                finished(dve, e4[5], t)
                nc.vector.tensor_tensor(tmp[p][0:n], misc[4 + p][0:n], b[2][0:n], ALU.add).then_inc(e4[7].sem, 1)

            def added(t, p, n, s=s):
                finished(dve, e4[7], t)
                nc.vector.scalar_tensor_tensor(out=tile(X, t)[0:n], in0=tmp[p][0:n], scalar=0.0, in1=tile(X, t)[0:n],
                                               op0=ALU.max, op1=ALU.add).then_inc(s, 1)

            def stats(t, p, n, linked=linked):
                linked(t, 1)
                tile_stats(t).then_inc(e4[6].sem, 1)
            skewed(dve, (0, f), (4, added), (3, biased), (4, stats))
            finished(dve, e4[6], NT - 1)
            norm_params(n4)

            s, linked = pair_links(4)

            def f(pair, s=s, linked=linked):
                for t, p, n in pair:
                    finished(dve, p4[0], t)
                    two_back(dve, p4[1], t)
                    nc.vector.tensor_scalar(tmp[p], tile(H, t), col(dinv, t), None, ALU.mult).then_inc(s, 1)
                split_pair(pair, s, linked, 1, p4[1])
            tile_pairs(dve, f)

            s, linked = pair_links(4)

            evacuate(dve, nc.vector.tensor_copy, agg5, over_parts, 1)

            def f(pair, s=s, linked=linked):
                for t, p, n in pair:
                    finished(dve, e5[1], t)
                    two_back(dve, e5[2], t)
                    nc.vector.scalar_tensor_tensor(out=tmp[p][0:n], in0=misc[p][0:n], scalar=col(dinv, t)[0:n],
                                                   in1=tile(H, t)[0:n], op0=ALU.mult, op1=ALU.add).then_inc(e5[3].sem, 1)
                for t, p, n in pair:
                    finished(dve, e5[3], t)
                    nc.vector.tensor_scalar(tmp[p], tmp[p], col(half_dinv, t), None, ALU.mult).then_inc(s, 1)
                split_pair(pair, s, linked, 1, e5[2])
            tile_pairs(dve, f)

            dve.wait_ge(wload["e6b"], 16)

            evacuate(dve, nc.vector.tensor_copy, agg6, over_parts, 1)

            def mixed(t, p, n):
                finished(dve, e6[1], t)
                two_back(dve, e6[3], t)
                nc.vector.scalar_tensor_tensor(out=hb[p][0:n], in0=misc[p][0:n], scalar=col(dinv, t)[0:n], in1=tile(H, t)[0:n],
                                               op0=ALU.mult, op1=ALU.add).then_inc(e6[9].sem, 1)

            def relu_half(t, p, n):
                finished(dve, e6[9], t)
                nc.vector.tensor_scalar(hb[p][0:n], hb[p][0:n], 0.5, 0.0, ALU.mult, ALU.max).then_inc(e6[2].sem, 1)

            def added(t, p, n):
                finished(dve, e6[7], t)
                nc.vector.tensor_tensor(tile(X, t)[0:n], misc[6 + p][0:n], tile(X, t)[0:n], ALU.add).then_inc(e6[10].sem, 1)

            def biased(t, p, n):
                finished(dve, e6[10], t)
                nc.vector.tensor_tensor(tile(X, t)[0:n], tile(X, t)[0:n], b[0][0:n], ALU.add).then_inc(e6[8].sem, 1)
            skewed(dve, (0, mixed), (6, added), (1, relu_half), (7, biased))

        @block.tensor
        def _(pe):
            mm = nc.tensor.matmul
            pe.wait_ge(firsts_ready, 1)
            mm(PS[:, 7 * BANK:7 * BANK + NCH], onesrow[0:1, :], firsts[0:1, 0:NCH], start=True, stop=True).then_inc(firsts_spread, 1)
            pe.wait_ge(codes_ready, 1)
            mm(PS[:, 6 * BANK:6 * BANK + 1], onesrow, hits, start=True, stop=True).then_inc(hits_summed, 1)
            wg = gathered.bitcast(F32)
            for g in range(G):
                for k in range(2):
                    for q, s in enumerate((codef, lowf, wg)):
                        c = g * ROW + k * P if q < 2 else g * 3 * ROW + 2 * ROW + k * P
                        last = nc.tensor.transpose(PS[:, (2 * q + k) * BANK + g * P:(2 * q + k) * BANK + (g + 1) * P],
                                                   s[:, c:c + P], ident)
            last.then_inc(tables_turned, 1)
            irregular = irregular_flag(pe)
            pe.wait_ge(tables_ready, 1)

            def bank_of(j, v):
                return PS[:, (2 * j + v) * BANK:(2 * j + v) * BANK + 2 * CODE]

            def add_place(place, n, out, alone):
                pe.wait_ge(hots_ready, n + 1)
                for s in range(2):
                    mm(out[:, CODE:2 * CODE], hot[place][s], code_hot[place][s], start=alone and s == 0,
                       stop=alone and s == 1)
                pe.wait_ge(scaled_ready, n + 1)
                for s in range(2):
                    for k in range(3):
                        last = mm(out[:, 0:CODE], hot_w[place][s][k], code_hot[place][s], start=False,
                                  stop=alone and s == 1 and k == 2, skip_group_check=True)
                return last.then_inc(slots_used, 1)

            def pair(q, j):
                pe.wait_ge(pairs_out, q + 1)
                for v in range(2):
                    add_place(2 * j + v, 2 * q + v, bank_of(j, v), True)

            def pair_all(q, j):
                pe.wait_ge(pairs_out, q + 1)
                for v in range(2):
                    mm(bank_of(j, v), zerosb[:, 0:P], zerosb[:, 0:2 * CODE], start=True, stop=False)
                    base = (2 * q + v) * NCB * 4
                    with pe.Fori(0, NCB) as i:
                        for r in range(4):
                            add_place(r, base + 4 * i + r, bank_of(j, v), False)
                    mm(bank_of(j, v), zerosb[:, 0:P], zerosb[:, 0:2 * CODE], start=False, stop=True).then_inc(slots_used, 1)
                pe.wait_ge(rest_out, q + 1)

            def turn_group(t, p, g, with_counts):
                n = LC if isinstance(t, int) and t == NT - 1 else P
                if g == 0:
                    pe.wait_ge(pairs_out, 2 + pairs_before(t) + pairs_in(t))
                    if with_counts:
                        for a in range(NT):
                            last = mm(PS[0:1, 7 * BANK:7 * BANK + n], onesb[:, 0:1], cols(C, a * NC + t * P, n),
                                      start=(a == 0), stop=(a == NT - 1))
                        last.then_inc(row_ready, 1)
                before = NG * t + max(g - 1, 0)
                if not isinstance(t, int) or before > 0:
                    pe.wait_ge(turned_out, before)
                for a in range(4 * g, min(4 * g + 4, NT)):
                    last = nc.tensor.transpose(PS[0:n, (4 + g % 2) * BANK + (a % 4) * P:(4 + g % 2) * BANK + (a % 4 + 1) * P],
                                               staged[p][:, a * P:a * P + n], ident)
                last.then_inc(turned, 1)
                if g == NG - 1 and with_counts:
                    pe.wait_ge(row_out, t + 1)
                    mm(col(PS, 6 * BANK + t)[0:n], degree_row[0:1, 0:n], ones[0:1, 0:1], start=True, stop=True)\
                        .then_inc(tile_turned, 1)
                elif g == NG - 1:
                    mm(PS[:, 7 * BANK:7 * BANK + 1], zerosb[:, 0:P], zerosb[:, 0:1], start=True, stop=True).then_inc(tile_turned, 1)

            def build_tile(t, p, pair_body, with_counts):
                pairs_and_groups(t, lambda q, k: pair_body(q, k % 2), lambda t, g: turn_group(t, 1 - p, g, with_counts))

            with pe.If(irregular != 0):
                build_tiles(pe, lambda t, p: build_tile(t, p, pair_all, False))
                for g in range(NG):
                    turn_group(NT - 1, 0, g, False)
                with pe.Fori(0, NT) as t:
                    mm(col(PS, 6 * BANK + t), zerosb[:, 0:P], zerosb[:, 0:1], start=True, stop=False)
                    with pe.Fori(0, NCB) as i:
                        for r in range(4):
                            pe.wait_ge(hots_ready, (NW + t) * NCB * 4 + 4 * i + r + 1)
                            for s in range(2):
                                last = mm(col(PS, 6 * BANK + t), hot[r][s], onesb[:, 0:1], start=False, stop=False)
                            last.then_inc(slots_used, 1)
                    mm(col(PS, 6 * BANK + t), zerosb[:, 0:P], zerosb[:, 0:1], start=False, stop=True).then_inc(slots_used, 1)
                mm(PS[:, 7 * BANK:7 * BANK + 1], zerosb[:, 0:P], zerosb[:, 0:1], start=True, stop=True).then_inc(counted, 1)
            with pe.Else():
                build_tiles(pe, lambda t, p: build_tile(t, p, pair, True))
                for g in range(NG):
                    turn_group(NT - 1, 0, g, True)
                mm(PS[:, 7 * BANK:7 * BANK + 1], ident, ones, start=True, stop=True).then_inc(counted, 1)

            def run_fp32(a, k_last, before):
                for s in before:
                    finished(pe, s, NT - 1)

                def one(t, turn, j, start, stop, k):
                    finished(pe, a.stat, t)
                    for h, (c, m) in enumerate(HALVES):
                        u = 2 * j + h
                        pe.wait_ge(a.loaded[u % 3].sem, a.loaded[u % 3].base + 16 * (2 * turn + u // 3 + 1))
                        for c1 in range(0, m, BANK):
                            w_ = min(BANK, m - c1)
                            last = mm(agg[:, c + c1:c + c1 + w_], stationary[j][0:k], stream[u % 3][0:k, c1:c1 + w_],
                                      start=start, stop=stop)
                        last.then_inc(a.units.sem, 1)
                for j in range(3):
                    one(j, 0, j, j == 0, False, P)
                with pe.Fori(1, NT // 3) as i:
                    for j in range(3):
                        one(3 * i + j, i, j, False, False, P)
                one(NT - 1, NT // 3, 0, False, True, k_last)
                mm(misc[7][:, 0:1], ident, ones, start=True, stop=True).then_inc(a.done.sem, 1)

            def run_counts(a, before):
                for s in before:
                    finished(pe, s, NT - 1)

                def one(t, start):
                    for k in range(3):
                        for c, m in BANKS:
                            mm(agg[:, c:c + m], part(k, t), cols(C, t * NC + c, m), start=start and k == 0, stop=False)
                one(0, True)
                with pe.Fori(1, NT) as t:
                    one(t, False)
                with pe.If(irregular != 0):
                    with pe.Fori(0, NT) as t:
                        for h, (c, m) in enumerate(RESTS):
                            got = a.rest_loaded[h % 2]
                            pe.wait_ge(got.sem, got.base + 16 * (len(RESTS) // 2 * t + h // 2 + 1))
                            for k in range(3):
                                for c1 in range(0, m, BANK):
                                    w_ = min(BANK, m - c1)
                                    last = mm(agg[:, c + c1:c + c1 + w_], part(k, t), rest_in[h % 2][:, c1:c1 + w_],
                                              start=False, stop=False)
                            last.then_inc(a.rest_used.sem, 1)
                for t in range(NT):
                    n = LC if t == NT - 1 else P
                    for k in range(3):
                        last = mm(agg[:, t * P:t * P + n], part(k, t), identb[:, 0:n], start=False,
                                  stop=k == 2 and (t % 4 == 3 or t == NT - 1))
                last.then_inc(a.done.sem, 1)

            def product(t, p, n, operand, operand_done, weight, dest, done, free):
                finished(pe, operand_done, t)
                two_back(pe, free, t)
                mm(misc[dest + p][0:n], operand[p][:, 0:n], weight, start=True, stop=True).then_inc(done.sem, 1)

            def turn(t, p, n, operand, operand_done, dest, done, free):
                finished(pe, operand_done, t)
                two_back(pe, free, t)
                nc.tensor.transpose(misc[dest + p][:, 0:n], operand[p][0:n, :], ident[0:n, 0:n]).then_inc(done.sem, 1)

            def turn_back(t, p, n, operand, operand_done, dest, done, free):
                finished(pe, operand_done, t)
                two_back(pe, free, t)
                nc.tensor.transpose(misc[dest + p][0:n, :], operand[p][:, 0:n], ident).then_inc(done.sem, 1)

            pe.wait_ge(wload["p0"], 32)

            def norm_product(s, weight):
                skewed(pe, (0, lambda t, p, n: turn(t, p, P, hb, s[0], 0, s[1], s[2])),
                       (1, lambda t, p, n: product(t, p, P, hT, s[2], weight, 2, s[3], s[4])))
            norm_product(p0, w[0])
            run_fp32(agg0, P, [p0[4]])
            pe.wait_ge(wload["e0"], 16)

            skewed(pe, (0, lambda t, p, n: product(t, p, n, ag, e0[0], w[1], 0, e0[1], e0[2])),
                   (1, lambda t, p, n: turn(t, p, n, hb, e0[2], 2, e0[3], e0[4])))
            pe.wait_ge(wload["p1"], 32)

            def f(t, p, n):
                m = n if n == P else NR
                finished(pe, p1[0], t)
                two_back(pe, p1[3], t)
                nc.tensor.transpose(misc[p][0:m, :], hT[p][:, 0:m], ident)
                mm(misc[2 + p][0:m], hT[p][:, 0:m], w[2], start=True, stop=True).then_inc(p1[1].sem, 1)
            tiles(pe, f)
            run_fp32(agg1, P, [p1[2]])
            pe.wait_ge(wload["e1"], 16)
            tiles(pe, lambda t, p, n: product(t, p, n, ag, e1[0], w[0], 0, e1[1], e1[3]))
            pe.wait_ge(wload["p2"], 32)

            norm_product(p2, w[1])
            run_fp32(agg2, LC, [p2[4]])
            tiles(pe, lambda t, p, n: turn_back(t, p, n, ag, e2[0], 0, e2[1], e2[3]))
            pe.wait_ge(gate_bias, 2)
            mm(gate_prod_out, zeros, whh, start=True, stop=True).then_inc(gate_prod, 1)
            pe.wait_ge(wload["p3"], 16)

            def f(t, p, n):
                finished(pe, p3[2], t)
                two_back(pe, p3[4], t)
                mm(gates_out[p], hT[p], wslot, start=True, stop=True).then_inc(p3[3].sem, 1)
            skewed(pe, (0, lambda t, p, n: turn(t, p, P, hb, p3[0], 0, p3[1], p3[2])), (1, f))
            run_counts(agg3, [p3[8]])
            pe.wait_ge(wload["e3"], 32)
            tiles(pe, lambda t, p, n: product(t, p, n, ag, e3[0], w[0], 0, e3[1], e3[3]))
            run_counts(agg4, [e3[2]])
            pe.wait_ge(wload["e4"], 48)

            skewed(pe, (0, lambda t, p, n: product(t, p, n, ag, e4[0], w[1], 0, e4[1], e4[2])),
                   (1, lambda t, p, n: turn(t, p, n, hb, e4[2], 2, e4[3], e4[4])),
                   (3, lambda t, p, n: product(t, p, n, hT, e4[4], w[2], 4, e4[5], e4[7])))
            run_counts(agg5, [p4[1]])
            tiles(pe, lambda t, p, n: turn_back(t, p, n, ag, e5[0], 0, e5[1], e5[3]))
            run_counts(agg6, [e5[2]])
            pe.wait_ge(wload["e6a"], 16)

            def middle(t, p, n):
                finished(pe, e6[4], t)
                two_back(pe, e6[6], t)
                mm(misc[4 + p][:, 0:n], w[0], hT[p][:, 0:n], start=True, stop=True).then_inc(e6[5].sem, 1)
            skewed(pe, (0, lambda t, p, n: turn_back(t, p, n, ag, e6[0], 0, e6[1], e6[9])),
                   (1, lambda t, p, n: turn(t, p, n, hb, e6[2], 2, e6[3], e6[4])), (3, middle),
                   (5, lambda t, p, n: product(t, p, n, tmp, e6[6], w[1], 6, e6[7], e6[10])))


_W = ["W1r", "W1l", "W2r", "W2l", "L1W", "Wih_i", "Wih_o", "Wih_g", "Whh_i", "Whh_o", "Whh_g", "W1", "W2", "W3", "w1", "w2"]
_B = ["b1l", "b2l", "L1b", "bih_i", "bih_o", "bih_g", "bhh_i", "bhh_o", "bhh_g", "b1", "b2", "b3", "w2b"]


def kernel(x, src, dst, edge_weight, L0_gnn_W1l, L0_gnn_b1l, L0_gnn_W1r, L0_gnn_bn_gamma, L0_gnn_bn_beta, L0_gnn_W2l,
           L0_gnn_b2l, L0_gnn_W2r, L1_gnn_W, L1_gnn_b, L2_gnn_W_ih, L2_gnn_W_hh, L2_gnn_b_ih, L2_gnn_b_hh, L2_gnn_W1,
           L2_gnn_b1, L2_gnn_W2, L2_gnn_b2, L2_gnn_W3, L2_gnn_b3, L3_gnn_w1, L3_gnn_b1, L3_gnn_w2, L3_gnn_b2):
    import numpy as _np
    import concourse.bacc as _bacc
    from concourse.bass_utils import run_bass_kernel_spmd as _run

    D = x.shape[1]

    def gate(a, k):
        return _np.asarray(a)[k * D:(k + 1) * D]

    by_name = {"W1r": _np.asarray(L0_gnn_W1r).T, "W1l": _np.asarray(L0_gnn_W1l).T, "W2r": _np.asarray(L0_gnn_W2r).T,
               "W2l": _np.asarray(L0_gnn_W2l).T, "L1W": _np.asarray(L1_gnn_W), "W1": _np.asarray(L2_gnn_W1),
               "W2": _np.asarray(L2_gnn_W2), "W3": _np.asarray(L2_gnn_W3).T, "w1": _np.asarray(L3_gnn_w1).T,
               "w2": _np.asarray(L3_gnn_w2).T}
    rows = {"b1l": L0_gnn_b1l, "b2l": L0_gnn_b2l, "L1b": L1_gnn_b, "b1": L2_gnn_b1, "b2": L2_gnn_b2, "b3": L2_gnn_b3,
            "w2b": L3_gnn_b2}
    for name, k in (("i", 0), ("g", 2), ("o", 3)):
        by_name["Wih_" + name] = gate(L2_gnn_W_ih, k).T
        by_name["Whh_" + name] = gate(L2_gnn_W_hh, k).T
        rows["bih_" + name] = gate(L2_gnn_b_ih, k)
        rows["bhh_" + name] = gate(L2_gnn_b_hh, k)
    arrays = {
        "in_x": _np.ascontiguousarray(x),
        "in_src": _np.ascontiguousarray(src),
        "in_dst": _np.ascontiguousarray(dst),
        "in_edge_weight": _np.ascontiguousarray(edge_weight),
        "in_weights": _np.ascontiguousarray(_np.concatenate([by_name[n] for n in _W], axis=1)),
        "in_biases": _np.ascontiguousarray(_np.stack([_np.asarray(rows[n]) for n in _B])),
        "in_columns": _np.ascontiguousarray(_np.stack([_np.asarray(a) for a in (L0_gnn_bn_gamma, L0_gnn_bn_beta, L3_gnn_b1)], axis=1)),
    }
    nc = _bacc.Bacc("TRN2", target_bir_lowering=False, num_devices=1)
    t = {k: nc.dram_tensor(k, a.shape, mybir.dt.from_np(a.dtype), kind="ExternalInput").ap() for k, a in arrays.items()}
    out = nc.dram_tensor("out", x.shape, F32, kind="ExternalOutput").ap()
    gnn_blocks(nc, t["in_x"], t["in_src"], t["in_dst"], t["in_edge_weight"], t["in_weights"],
               {n: i for i, n in enumerate(_W)}, t["in_biases"], {n: i for i, n in enumerate(_B)}, t["in_columns"], out)
    r = _run(nc, [arrays], core_ids=[0])
    return r.results[0]["out"]
```

```python
from contextlib import ExitStack

import concourse.bass as bass
from concourse import mybir

F32 = mybir.dt.float32
BF16 = mybir.dt.bfloat16
I32 = mybir.dt.int32
ALU = mybir.AluOpType
ACT = mybir.ActivationFunctionType
ds = bass.ds
P = 128
V = 8
ROW = 256
STEP = 32
BANK = 512


def gnn_blocks(nc, x, src, dst, edge_weight, weights, weight_at, biases, bias_at, columns, out):
    N, D = x.shape
    E, = src.shape
    NT = -(-N // P)
    NR = N - P * (NT - 1)
    NW = -(-N // (2 * V)) * 2
    NC = NW * V
    LC = NC - P * (NT - 1)
    CODE = V * NT
    G = 4
    NPT = P // (2 * V)
    NPL = LC // (2 * V)
    NCH = -(-E // P)
    NCB = -(-NCH // 8)
    LASTROW = (E - ROW) // STEP + 1
    NROWS = LASTROW + 1
    NG = -(-NT // 4)
    BANKS = [(c, min(BANK, NC - c)) for c in range(0, NC, BANK)]
    HALF = BANK * (len(BANKS) // 2)
    HALVES = [(0, HALF), (HALF, NC - HALF)]
    STREAM = max(HALF, NC - HALF)
    NB = len(BANKS)
    EPS = 1e-5
    assert D == P and NT % 6 == 1 and NW <= G * P and NCH <= BANK and NR <= LC < P and LC % (2 * V) == 0
    SETUP = 14000
    assert 7 * BANK >= NC and 4 * (NB - 1) == NT - 1 and 2 * CODE <= BANK and LC == P // 2

    edge_rows = nc.dram_tensor("edge_rows", (NROWS, 3 * ROW), I32).ap()
    AT = nc.dram_tensor("AT", (NT, P, NC), F32).ap()
    A = nc.dram_tensor("A", (NT, P, NT * P), F32).ap()
    count_rest = nc.dram_tensor("count_rest", (NT, P, NC), BF16).ap()

    with ExitStack() as ctx:
        arena = ctx.enter_context(nc.sbuf_tensor("arena", [P, 53208], F32))
        PS = ctx.enter_context(nc.psum_tensor("PS", [P, 8 * BANK], F32))
        at = [0]

        def take(words):
            at[0] += words
            assert at[0] <= 53208, at[0]
            return arena[:, at[0] - words:at[0]]

        scratch0 = at[0]
        C = take(max(NT * NC // 2, SETUP))[:, 0:NT * NC // 2].bitcast(BF16)
        setup_end = at[0]
        ident = take(P)
        iota = take(-(-max(CODE, P) // 2)).bitcast(BF16)
        identb = take(P // 2).bitcast(BF16)
        ones = take(1)
        onesb = take(1).bitcast(BF16)
        count = take(NT)
        flag = take(1)
        region = at[0]

        W5 = 2 * NW
        t_code, t_src, t_w1 = [take(W5) for _ in range(3)]
        t_w23 = take(W5).bitcast(BF16).rearrange("p (k h v) -> p h k v", k=2, h=2)
        PLACE = 2 * 4 * P + 2 * CODE
        places = [take(PLACE // 2).bitcast(BF16) for _ in range(4)]
        hots = [m[:, 0:2 * P] for m in places]
        hot = [[m[:, s * P:(s + 1) * P] for s in (0, 1)] for m in places]
        hots_w23 = [m[:, 4 * P:8 * P] for m in places]
        hot_w = [[[m[:, c * P:(c + 1) * P] for c in (2 + s, 4 + 2 * s, 5 + 2 * s)] for s in (0, 1)] for m in places]
        code_hot = [[m[:, 8 * P + s * CODE:8 * P + (s + 1) * CODE] for s in (0, 1)] for m in places]
        piece = [take(BANK) for _ in range(2)]
        staged = [take(NT * P) for _ in range(2)]
        staged_end = at[0]
        zeros_or_row = take(max(CODE, P))
        zerosb = zeros_or_row.bitcast(BF16)
        degree_row = zeros_or_row[:, 0:P]

        at[0] = scratch0
        gathered = take(G * 3 * ROW).bitcast(I32)
        firsts_i = take(BANK).bitcast(I32)
        firsts = take(BANK)
        onesrow = take(P)
        firsts_all = take(BANK)
        below = take(BANK)
        iota_w = take(P).bitcast(I32)
        theta_i = take(G).bitcast(I32)
        theta = take(G)
        theta_nt = take(G)
        chunks_below = take(G)
        row0 = take(G)
        row_i = take(G).bitcast(I32)
        base0 = take(G)
        fine = take(G)
        start = take(G)
        start_i = take(G).bitcast(I32)
        last_or = take(G)
        row1 = take(G)
        row1_i = take(G).bitcast(I32)
        dstf = take(G * ROW)
        tile_i = take(G * ROW).bitcast(I32)
        tilef = take(G * ROW)
        low_i = take(G * ROW).bitcast(I32)
        lowf = take(G * ROW)
        codef = take(G * ROW)
        inside = take(G * ROW)
        inside2 = take(G * ROW)
        hits = take(1)
        total = take(1)
        assert at[0] <= setup_end
        at[0] = region
        NCP = 8 * NCB
        l_code, l_src, l_dst, l_w1 = [take(NCP) for _ in range(4)]
        l_w23 = take(NCP).bitcast(BF16).rearrange("p (k c) -> p c k", k=2)
        rest_stage = take(NT * V).bitcast(BF16)
        assert at[0] <= region + 4 * W5
        list_i = staged[0][:, 0:2 * NCP].bitcast(I32)
        list_w = staged[0][:, 2 * NCP:3 * NCP]
        list_t = staged[0][:, 3 * NCP:4 * NCP].bitcast(I32)
        w_left = staged[1][:, 0:W5]

        at[0] = region
        X = take(NT * P)
        H = take(NT * P)
        rcount = take(NT)
        dinv = take(NT)
        half_dinv = take(NT)
        big = take(max(3 * STREAM, 3 * NT * P // 2, NC))
        stream = [big[:, i * STREAM:(i + 1) * STREAM] for i in range(3)]
        bn_in = big[:, 0:NC]
        parts = big[:, 0:3 * NT * P // 2].bitcast(BF16)
        wslot = take(3 * P)
        bslot = take(3 * P)
        work_at = at[0]
        work = take(12 * P)
        mv = take(2 * NT)
        rstd = take(NT)
        nmr = take(NT)
        gamma, beta, bn_scale, bn_shift, b1col = [take(1) for _ in range(5)]
        bn_mv = take(2)
        ag = [work[:, i * P:(i + 1) * P] for i in (0, 1)]
        hb = [work[:, i * P:(i + 1) * P] for i in (2, 3)]
        hT = [work[:, i * P:(i + 1) * P] for i in (4, 5)]
        tmp = [work[:, i * P:(i + 1) * P] for i in (6, 7)]
        stat6 = work[:, 8 * P:8 * P + 6 * NT]
        assert NT * P <= 4 * W5 + 2 * PLACE and staged_end - NT * P <= work_at + 8 * P <= staged_end - 6 * NT
        gates_io = [work[:, 8 * P:10 * P], work[:, 10 * P:12 * P]]
        gates_g = ag
        stationary = [work[:, i * P:(i + 1) * P] for i in range(3)]
        rest_in = gates_io[1].bitcast(BF16)
        whh = big[:, 0:3 * P]
        bihh = big[:, 3 * P:9 * P]
        zeros = big[:, 9 * P:10 * P]
        w = [wslot[:, i * P:(i + 1) * P] for i in range(3)]
        b = [bslot[:, i * P:(i + 1) * P] for i in range(3)]

        agg = PS[:, 0:7 * BANK]
        misc = [PS[:, k * BANK:k * BANK + P] for k in range(8)]
        gates_out = [PS[:, k * BANK:k * BANK + 3 * P] for k in (4, 5)]
        gate_prod_out = PS[:, 6 * BANK:6 * BANK + 3 * P]

        def sem(name):
            return ctx.enter_context(nc.semaphore(name))

        def tile(buf, t, n=P):
            return buf[:, ds(t * P, n)] if not isinstance(t, int) else buf[:, t * P:t * P + n]

        def part(k, t):
            return cols(parts, (3 * t + k) * P, P)

        def col(buf, c):
            return buf[:, ds(c, 1)] if not isinstance(c, int) else buf[:, c:c + 1]

        def cols(buf, c, n):
            return buf[:, ds(c, n)] if not isinstance(c, int) else buf[:, c:c + n]

        class Mark:
            def __init__(self, s, base):
                self.sem, self.base = s, base

        stages = {}

        def stage(name, step=NT):
            if name not in stages:
                stages[name] = [sem(name), 2]
            s, base = stages[name]
            stages[name][1] += step
            return Mark(s, base)

        def finished(eng, m, t):
            eng.wait_ge(m.sem, m.base + t + 1)

        def one_back(eng, m, t):
            eng.wait_ge(m.sem, m.base + t)

        def two_back(eng, m, t):
            eng.wait_ge(m.sem, m.base + t - 1)

        counts = {}

        def mark(name, step):
            if name not in counts:
                counts[name] = [sem(name), 0]
            s, base = counts[name]
            counts[name][1] += step
            return Mark(s, base)

        TURN = 8

        def tiles(eng, body):
            skewed(eng, (0, body))

        def steps_of(*parts, ring=2):
            def step(s):
                for lag, body in parts:
                    if 0 <= s - lag < NT:
                        body(s - lag, (s - lag) % ring, LC if s - lag == NT - 1 else P)
            return step, max(lag for lag, _ in parts)

        def skewed(eng, *parts, turn=TURN, ring=2):
            step, most = steps_of(*parts, ring=ring)
            head, tail = -(-most // turn) * turn, NT // turn * turn
            if head >= tail:
                head = tail = NT
            for s in range(head):
                step(s)
            if head < tail:
                with eng.Fori(head // turn, tail // turn) as i:
                    for j in range(turn):
                        for lag, body in parts:
                            body(turn * i + (j - lag), (j - lag) % ring, P)
            for s in range(tail, NT + most):
                step(s)

        edges_in = sem("edges_in")
        firsts_in = sem("firsts_in")
        pool_const = sem("pool_const")
        dve_chain = sem("dve_chain")
        all_chain = sem("all_chain")
        firsts_ready = sem("firsts_ready")
        firsts_spread = sem("firsts_spread")
        rows_ready = sem("rows_ready")
        gather0 = sem("gather0")
        gather1 = sem("gather1")
        codes_ready = sem("codes_ready")
        tables_turned = sem("tables_turned")
        hits_summed = sem("hits_summed")
        flag_ready = sem("flag_ready")
        tables_ready = sem("tables_ready")
        list_in = sem("list_in")
        list_ready = sem("list_ready")
        hots_ready = sem("hots_ready")
        w1_ready = sem("w1_ready")
        scaled_ready = sem("scaled_ready")
        slots_used = sem("slots_used")
        row_ready = sem("row_ready")
        row_out = sem("row_out")
        pairs_out = stage("pairs_out").sem
        rest_out = sem("rest_out")
        rest_saved = sem("rest_saved")
        rest_free = sem("rest_free")
        shifted = sem("shifted")
        stage_saved = [sem("stage_saved0"), sem("stage_saved1")]
        tile_turned = stage("tile_turned").sem
        turned = stage("groups_turned").sem
        turned_out = sem("turned_out")
        piece_saved = [sem("piece_saved0"), sem("piece_saved1")]
        counted = sem("counted")
        build_over = sem("build_over")
        act_over = sem("act_over")
        root_ready = sem("root_ready")
        degrees_ready = sem("degrees_ready")

        def pairs_before(t):
            return t * NPT

        def pairs_in(t):
            return NPL if isinstance(t, int) and t == NT - 1 else NPT

        def build_tiles(eng, body):
            for t in range(3):
                body(t, t % 2)
            with eng.Fori(1, (NT - 3) // 2) as i:
                body(2 * i + 1, 1)
                body(2 * i + 2, 0)
            body(NT - 2, 1)
            body(NT - 1, 0)

        def pair_loop(eng, t, first, body):
            q0 = pairs_before(t)
            with eng.Fori(0, (pairs_in(t) - first) // 4) as i:
                for j in range(4):
                    body(q0 + first + 4 * i + j, j % 2)

        def pairs_and_groups(t, pair, group):
            pairs, before = pairs_in(t), not isinstance(t, int) or t >= 1
            for k in range(pairs):
                pair(pairs_before(t) + k, k)
                if before and 0 < k <= NG:
                    group(t - 1, k - 1)
            for g in range(pairs - 1, NG):
                if before:
                    group(t - 1, g)

        def list_batches(eng, body):
            with eng.Fori(0, NW) as win:
                with eng.Fori(0, NCB) as i:
                    for r in range(4):
                        body((4 * NCB) * win + 4 * i + r, r, 8 * i + 2 * r)

        def irregular_flag(eng):
            eng.wait_ge(flag_ready, 1)
            return eng.value_load(flag.bitcast(I32)[0:1, 0:1], min_val=0, max_val=1)

        x_in = sem("x_in")
        wload = {k: sem("w_" + k) for k in ("p0", "e0", "p1", "e1", "p2", "p3", "bias3", "e3", "e4", "e6a", "e6b", "small")}

        class Pass:
            def __init__(self, streamed):
                if streamed:
                    self.done = mark("agg_done", 1)
                    self.out = mark("agg_out", NB)
                    self.loaded = [mark(f"unit_loaded{i}", 16 * len(range(i, 2 * NT, 3))) for i in range(3)]
                    self.units = mark("units_used", 2 * NT)
                    self.stat = mark("stationary_ready", NT)
                else:
                    self.banks = mark("banks_done", 4 * NB)
                    self.rest_loaded = mark("rest_loaded", 16 * NT * NB)
                    self.rest_used = mark("rest_used", NT * NB)

        agg0, agg1, agg2 = Pass(True), Pass(True), Pass(True)
        agg3, agg4, agg5, agg6 = [Pass(False) for _ in range(4)]

        def norm_marks():
            return [mark("norm_" + k, 1) for k in ("var", "root", "ready")]

        n0, n1, n2, n4 = norm_marks(), norm_marks(), norm_marks(), norm_marks()
        p0 = [stage(k) for k in ("relu", "turned", "hT", "prod", "out", "kept")]
        e0 = [stage(k) for k in ("copied", "prod", "sum", "turned", "act_out")]
        bn_var, bn_root, bn_ready = sem("bn_var"), sem("bn_root"), sem("bn_ready")
        p1 = [stage(k) for k in ("relu", "prod", "out", "taken")]
        p1_x = sem("p1_x")
        h_cleared = sem("h_cleared")
        e1 = [stage(k) for k in ("copied", "prod", "out", "taken")]
        p2 = [stage(k) for k in ("relu", "turned", "hT", "prod", "out")]
        e2 = [stage(k) for k in ("copied", "turned", "out", "taken")]
        p3 = [stage(k) for k in ("relu", "turned", "hT", "gates", "biased", "acts", "cell", "tanh", "out")]
        gate_prod, gate_bias, gate_ready = sem("gate_prod"), sem("gate_bias"), sem("gate_ready")
        e3 = [stage(k) for k in ("copied", "prod", "out", "taken")]
        e4 = [stage(k) for k in ("copied", "prod", "sum", "turned", "act_hT", "prod3", "out", "taken")]
        p4 = [stage("relu")]
        e5 = [stage(k) for k in ("copied", "turned", "out", "taken")]
        e6 = [stage(k) for k in ("copied", "turned", "sum", "turned2", "act_hT", "prod3", "tT", "prod2", "out", "taken", "taken2")]
        split4, split5, split6 = [[stage("split_" + k) for k in ("high", "rest", "middle", "low")] for _ in range(3)]
        h_again = stage("h_again")
        out_saved = sem("out_saved")

        def evacuate(eng, copy, a, dest, first):
            agg_end(eng, a)
            for c, m in BANKS[first::2]:
                copy(dest[:, c:c + m], agg[:, c:c + m]).then_inc(a.out.sem, 1)

        def every_bank(eng, a):
            eng.wait_ge(a.banks.sem, a.banks.base + 4 * NB)

        def agg_end(eng, a):
            eng.wait_ge(a.done.sem, a.done.base + 1)

        block = ctx.enter_context(nc.Block())

        @block.sync
        def _(sp):
            for s, _ in stages.values():
                sp.sem_inc(s, 2)
            sp.sem_inc(slots_used, 4)
            sp.sem_inc(shifted, 1)
            sp.sem_inc(rest_free, 1)
            sp.sem_inc(agg0.units.sem, 6)
            sp.sem_inc(agg3.rest_used.sem, 1)
            for k, v in enumerate((src, dst, edge_weight.bitcast(I32))):
                sp.dma_start(edge_rows[0:LASTROW, k * ROW:(k + 1) * ROW],
                             bass.AP(v.tensor, 0, [[STEP, LASTROW], [1, ROW]])).then_inc(edges_in, 16)
                sp.dma_start(edge_rows[LASTROW:NROWS, k * ROW:(k + 1) * ROW],
                             bass.AP(v.tensor, E - ROW, [[ROW, 1], [1, ROW]])).then_inc(edges_in, 16)
            sp.dma_start(firsts_i[0:1, 0:NCH], bass.AP(dst.tensor, 0, [[1, 1], [P, NCH]]), allow_slow_non_contiguous=True).then_inc(firsts_in, 16)

            irregular = irregular_flag(sp)
            with sp.If(irregular != 0):
                n = NCH if E % P == 0 else NCH - 1
                dests = (list_i[:, NCP:2 * NCP], list_i[:, 0:NCP], list_w)
                sp.wait_ge(tables_ready, 1)
                for v, d in zip((src, dst, edge_weight), dests):
                    sp.dma_start(d[:, 0:n], bass.AP(v.tensor, 0, [[1, P], [P, n]]),
                                 allow_slow_non_contiguous=True).then_inc(list_in, 16)
                    if E % P:
                        sp.dma_start(d[0:E % P, n:n + 1], bass.AP(v.tensor, n * P, [[1, E % P], [1, 1]])).then_inc(list_in, 16)

            def save_rest(q, _):
                sp.wait_ge(rest_out, q + 1)
                sp.dma_start(count_rest[:, :, ds(q * 2 * V, 2 * V)].rearrange("a p d -> p a d"),
                             rest_stage.rearrange("p (a d) -> p a d", a=NT)).then_inc(rest_saved, 16)
                sp.wait_ge(rest_saved, 16 * (q + 1))
                sp.sem_inc(rest_free, 1)

            def save_group(t, g):
                n = LC if isinstance(t, int) and t == NT - 1 else P
                a_rows = A[ds(t, 1), 0:n, :] if not isinstance(t, int) else A[t:t + 1, 0:n, :]
                m = min(BANK, NT * P - g * BANK)
                sp.wait_ge(turned_out, NG * t + g + 1)
                sp.dma_start(a_rows[:, :, g * BANK:g * BANK + m].rearrange("a p s -> (a p) s"),
                             piece[g % 2][0:n, 0:m]).then_inc(piece_saved[g % 2], 16)

            def save_tile(t, p, rest):
                pairs_and_groups(t, save_rest if rest else lambda q, k: None, save_group)
                n = LC if isinstance(t, int) and t == NT - 1 else P
                sp.wait_ge(pairs_out, 2 + pairs_before(t) + pairs_in(t))
                at_cols = AT[:, :, ds(t * P, n)] if not isinstance(t, int) else AT[:, :, t * P:t * P + n]
                sp.dma_start(at_cols.rearrange("a p d -> p a d"),
                             staged[p].rearrange("p (a d) -> p a d", a=NT)[:, :, 0:n]).then_inc(stage_saved[p], 16)

            def save_last():
                for g in range(NG):
                    save_group(NT - 1, g)

            def load_x(s):
                sp.dma_start(X[:, 0:(NT - 1) * P].rearrange("p (t d) -> p t d", t=NT - 1),
                             x[0:(NT - 1) * P, :].rearrange("(t p) d -> p t d", p=P)).then_inc(s, 16)
                sp.dma_start(X[0:NR, (NT - 1) * P:NT * P], x[(NT - 1) * P:N, :]).then_inc(s, 16)

            with sp.If(irregular != 0):
                build_tiles(sp, lambda t, p: save_tile(t, p, True))
                save_last()
                sp.wait_ge(shifted, NW + NT + 1)
                sp.wait_ge(h_cleared, 1)
                load_x(x_in)
            with sp.Else():
                build_tiles(sp, lambda t, p: save_tile(t, p, False))
                sp.wait_ge(h_cleared, 1)
                load_x(x_in)
                save_last()
            sp.wait_ge(stage_saved[0], 16 * (NT // 2 + 1))
            sp.wait_ge(stage_saved[1], 16 * (NT // 2))
            sp.wait_ge(piece_saved[0], 16 * NT * ((NG + 1) // 2))
            sp.wait_ge(piece_saved[1], 16 * NT * (NG // 2))
            sp.wait_ge(counted, 1)
            sp.wait_ge(act_over, 1)
            sp.sem_inc(build_over, 1)

            def load_w(slot, names, s):
                i = weight_at[names[0]]
                sp.dma_start(wslot[:, slot * P:(slot + len(names)) * P], weights[:, i * P:(i + len(names)) * P]).then_inc(s, 16)

            def load_b(slot, name, s):
                i = bias_at[name]
                sp.dma_start(b[slot], bass.AP(biases.tensor, i * P, [[0, P], [1, P]])).then_inc(s, 16)

            load_w(0, ["W1r"], wload["p0"])
            load_b(0, "b1l", wload["p0"])
            load_w(1, ["W1l"], wload["e0"])
            load_w(2, ["W2r"], wload["p1"])
            load_b(1, "b2l", wload["p1"])
            load_b(2, "L1b", wload["p2"])
            for k, d in enumerate((gamma, beta, b1col)):
                sp.dma_start(d, columns[:, k:k + 1], allow_slow_non_contiguous=True).then_inc(wload["small"], 16)

            def stream_matrix(a, M):
                def unit(u, n, t):
                    c, m = HALVES[u % 2]
                    sp.wait_ge(a.units.sem, a.units.base + n + 4)
                    k = P
                    if isinstance(t, int) and t == NT - 1 and M is A:
                        k = LC
                    rows = M[ds(t, 1), 0:k, c:c + m] if not isinstance(t, int) else M[t:t + 1, 0:k, c:c + m]
                    sp.dma_start(stream[u % 3][0:k, 0:m], rows.rearrange("a p s -> (a p) s")).then_inc(a.loaded[u % 3].sem, 16)
                with sp.Fori(0, NT // 3) as i:
                    for u in range(6):
                        unit(u, 6 * i + u, 3 * i + u // 2)
                for u in range(2):
                    unit(u, 2 * (NT - 1) + u, NT - 1)

            stream_matrix(agg0, AT)
            finished(sp, e0[2], NT - 1)
            load_x(p1_x)
            load_w(0, ["W2l"], wload["e1"])
            load_w(1, ["L1W"], wload["p2"])
            finished(sp, p1[0], NT - 1)
            stream_matrix(agg1, AT)
            finished(sp, e1[2], NT - 1)
            stream_matrix(agg2, A)
            finished(sp, p2[4], NT - 1)
            load_w(0, ["Wih_i", "Wih_o", "Wih_g"], wload["p3"])
            agg_end(sp, agg2)
            i = weight_at["Whh_i"]
            sp.dma_start(whh, weights[:, i * P:(i + 3) * P]).then_inc(wload["bias3"], 16)
            i = bias_at["bih_i"]
            sp.dma_start(bihh, bass.AP(biases.tensor, i * P, [[0, P], [1, 6 * P]])).then_inc(wload["bias3"], 16)
            finished(sp, p3[8], NT - 1)
            load_w(0, ["W1"], wload["e3"])
            load_b(0, "b1", wload["e3"])
            load_w(1, ["W2", "W3"], wload["e4"])
            load_b(1, "b2", wload["e4"])
            load_b(2, "b3", wload["e4"])

            def stream_rest(a):
                with sp.If(irregular != 0):
                    for c, (c0, m) in enumerate(BANKS):
                        with sp.Fori(0, NT) as t:
                            sp.wait_ge(a.rest_used.sem, a.rest_used.base + c * NT + t + 1)
                            sp.dma_start(rest_in[:, 0:m], count_rest[ds(t, 1), :, c0:c0 + m].rearrange("a p s -> (a p) s"))\
                                .then_inc(a.rest_loaded.sem, 16)

            stream_rest(agg3)
            stream_rest(agg4)
            finished(sp, e4[6], NT - 1)
            load_w(0, ["w1", "w2"], wload["e6a"])
            load_b(0, "w2b", wload["e6b"])
            stream_rest(agg5)
            stream_rest(agg6)

            def save_out(t, p, n):
                finished(sp, e6[8], t)
                if n == P:
                    sp.dma_start(out[ds(t * P, P), :], tile(X, t)).then_inc(out_saved, 16)
                else:
                    sp.dma_start(out[(NT - 1) * P:N, :], X[0:NR, (NT - 1) * P:NT * P]).then_inc(out_saved, 16)
            tiles(sp, save_out)
            sp.wait_ge(out_saved, 16 * NT)

        @block.gpsimd
        def _(pool):
            nc.gpsimd.iota(iota[:, 0:max(CODE, P)], [[1, max(CODE, P)]], base=0, channel_multiplier=0,
                           allow_small_or_imprecise_dtypes=True).then_inc(pool_const, 1)
            nc.gpsimd.iota(theta_i, [[V * P, G]], base=0, channel_multiplier=V).then_inc(pool_const, 1)
            nc.gpsimd.iota(iota_w, [[1, P]], base=0, channel_multiplier=-1).then_inc(pool_const, 1)
            nc.gpsimd.memset(ones, 1.0).then_inc(pool_const, 1)
            nc.gpsimd.memset(onesb, 1.0).then_inc(pool_const, 1)
            nc.gpsimd.memset(onesrow, 1.0).then_inc(pool_const, 1)
            nc.gpsimd.memset(count, 0.0).then_inc(pool_const, 1)
            pool.wait_ge(edges_in, 96)
            for s, rows, done in ((1, row_i, gather0), (2, row1_i, gather1)):
                pool.wait_ge(rows_ready, s)
                for g in range(G):
                    nc.gpsimd.indirect_dma_start(
                        out=gathered[:, g * 3 * ROW:(g + 1) * 3 * ROW], out_offset=None, in_=edge_rows,
                        in_offset=bass.IndirectOffsetOnAxis(ap=rows[:, g:g + 1], axis=0)).then_inc(done, 16)
            def scale(n, place, w):
                pool.wait_ge(hots_ready, n + 1)
                each = hots[place].rearrange("p (s e) -> p s e", s=2)[:, :, None, :].to_broadcast([P, 2, 2, P])
                nc.gpsimd.tensor_tensor(hots_w23[place].rearrange("p (s k e) -> p s k e", s=2, k=2), each,
                                        w.to_broadcast([P, 2, 2, P]), ALU.mult).then_inc(scaled_ready, 1)

            irregular = irregular_flag(pool)
            pool.wait_ge(tables_ready, 1)
            with pool.If(irregular != 0):
                pool.wait_ge(list_ready, 1)
                list_batches(pool, lambda n, r, c: scale(n, r, l_w23[:, ds(c, 2), :][:, :, :, None]))
                pool.wait_ge(shifted, NW + NT + 1)
                pool.wait_ge(counted, 1)
            with pool.Else():
                def pair_scaled(q, j):
                    for v in range(2):
                        scale(2 * q + v, 2 * j + v, t_w23[:, :, :, ds(2 * q + v, 1)])
                build_tiles(pool, lambda t, p: pair_loop(pool, t, 0, pair_scaled))
                pool.wait_ge(pairs_out, 2 + NW // 2)
            nc.gpsimd.memset(X[:, (NT - 1) * P:NT * P], 0.0).then_inc(h_cleared, 1)

            def keep(t, p, n):
                finished(pool, p0[0], t)
                nc.gpsimd.tensor_copy(tile(H, t), hb[p]).then_inc(p0[5].sem, 1)
            tiles(pool, keep)

            def feed(a, before):
                finished(pool, before, NT - 1)

                def one(t, j):
                    pool.wait_ge(a.units.sem, a.units.base + 2 * t + 2)
                    nc.gpsimd.tensor_copy(stationary[j], tile(H, t)).then_inc(a.stat.sem, 1)
                with pool.Fori(0, NT // 3) as i:
                    for j in range(3):
                        one(3 * i + j, j)
                one(NT - 1, 0)
            finished(pool, p0[5], NT - 1)
            feed(agg0, p0[4])
            finished(pool, e0[2], NT - 1)
            nc.gpsimd.memset(H[:, (NT - 1) * P:NT * P], 0.0).then_inc(h_cleared, 1)
            feed(agg1, p1[2])
            feed(agg2, p2[4])

        @block.scalar
        def _(act):
            irregular = irregular_flag(act)

            def scale_second(n, place, w1):
                act.wait_ge(hots_ready, n + 1)
                nc.scalar.activation(hot_w[place][1][0], hot[place][1], ACT.Copy, scale=w1).then_inc(w1_ready, 1)

            def scale_pair(q, j):
                for v in range(2):
                    scale_second(2 * q + v, 2 * j + v, col(t_w1, NW + 2 * q + v))

            def scale_pair_all(q):
                for v in range(2):
                    with act.Fori(0, NCB) as i:
                        for r in range(4):
                            scale_second((2 * q + v) * NCB * 4 + 4 * i + r, r, col(l_w1, 8 * i + 2 * r + 1))

            def evacuate_pair(slots, t, p, q, j, place):
                act.wait_ge(slots_used, 4 + slots * (q + 1))
                src_w = PS[:, 2 * j * BANK:2 * (j + 1) * BANK].rearrange("p (v c) -> p v c", v=2)
                d = staged[p].rearrange("p (a d) -> p a d", a=NT)[:, :, place:place + 2 * V]
                nc.scalar.copy(d.rearrange("p a (v d) -> p v a d", v=2),
                               src_w[:, :, 0:CODE].rearrange("p v (d a) -> p v a d", d=V))
                c = C.rearrange("p (a d) -> p a d", a=NT)[:, :, ds(q * 2 * V, 2 * V)]
                nc.scalar.copy(c.rearrange("p a (v d) -> p v a d", v=2),
                               src_w[:, :, CODE:2 * CODE].rearrange("p v (d a) -> p v a d", d=V)).then_inc(pairs_out, 1)

            def group_out(t, g, with_counts):
                n = LC if isinstance(t, int) and t == NT - 1 else P
                if g == 0 and with_counts:
                    act.wait_ge(row_ready, t + 1)
                    nc.scalar.copy(degree_row[0:1, 0:n], PS[0:1, 7 * BANK:7 * BANK + n]).then_inc(row_out, 1)
                m = min(BANK, NT * P - g * BANK)
                before = (NG + 1) // 2 * t + g // 2 if g % 2 == 0 else NG // 2 * t + g // 2
                act.wait_ge(turned, 3 + NG * t + g)
                if not isinstance(t, int) or before > 0:
                    act.wait_ge(piece_saved[g % 2], 16 * before)
                nc.scalar.copy(piece[g % 2][0:n, 0:m], PS[0:n, (4 + g % 2) * BANK:(4 + g % 2) * BANK + m])\
                    .then_inc(turned_out, 1)

            def build_tile(per_pair, t, p, with_counts):
                def pair_out(q, k):
                    if k == 0 and (not isinstance(t, int) or t >= 2):
                        act.wait_ge(stage_saved[p], (t - p) * 8)
                        act.wait_ge(tile_turned, 2 + t - 1)
                    if not with_counts:
                        scale_pair_all(q)
                    elif not (isinstance(t, int) and t == NT - 1 and k == NPL - 1):
                        scale_pair(q + 1, (k + 1) % 2)
                    evacuate_pair(per_pair, t, p, q, k % 2, k * 2 * V)
                pairs_and_groups(t, pair_out, lambda t, g: group_out(t, g, with_counts))

            with act.If(irregular != 0):
                act.wait_ge(list_ready, 1)
                build_tiles(act, lambda t, p: build_tile(2 * (4 * NCB + 1), t, p, False))
                for g in range(NG):
                    group_out(NT - 1, g, False)
            with act.Else():
                act.wait_ge(tables_ready, 1)
                scale_pair(0, 0)
                build_tiles(act, lambda t, p: build_tile(2, t, p, True))
                for g in range(NG):
                    group_out(NT - 1, g, True)
            act.wait_ge(counted, 1)
            act.wait_ge(pool_const, 7)
            nc.scalar.copy(count[:, 0:NT - 1], PS[:, 6 * BANK:6 * BANK + NT - 1])
            nc.scalar.copy(count[0:LC, NT - 1:NT], PS[0:LC, 6 * BANK + NT - 1:6 * BANK + NT]).then_inc(act_over, 1)
            act.wait_ge(act_over, 1)
            act.wait_ge(build_over, 1)
            nc.scalar.activation(dinv, count, ACT.Sqrt, bias=1.0, scale=1.0).then_inc(root_ready, 1)

            def root(s, d):
                finished(act, s[0], 0)
                nc.scalar.activation(d, d, ACT.Sqrt).then_inc(s[1].sem, 1)

            def relu_norm(t, dest, done):
                nc.scalar.activation(dest, tile(X, t), ACT.Relu, bias=col(nmr, t), scale=col(rstd, t)).then_inc(done.sem, 1)

            def copy_agg(s, a, used, source=H):
                evacuate(act, nc.scalar.copy, a, source, 0)
                finished(act, a.out, len(BANKS) - 1)

                def one(t, p, n):
                    two_back(act, used, t)
                    nc.scalar.copy(ag[p][:, 0:n], cols(source, t * P, n)).then_inc(s.sem, 1)
                return one

            root(n0, rstd)
            finished(act, n0[2], 0)

            def f(t, p, n):
                two_back(act, p0[1], t)
                two_back(act, p0[5], t)
                relu_norm(t, hb[p], p0[0])
            tiles(act, f)

            one = copy_agg(e0[0], agg0, e0[1])

            def turn(t, p, n):
                finished(act, e0[3], t)
                m = n if n == P else NR
                nc.scalar.copy(cols(bn_in, t * P, m), misc[2 + p][:, 0:m]).then_inc(e0[4].sem, 1)
            skewed(act, (0, one), (3, turn))
            act.wait_ge(bn_var, 1)
            nc.scalar.activation(bn_scale, bn_scale, ACT.Sqrt).then_inc(bn_root, 1)
            act.wait_ge(bn_ready, 1)

            def f(t, p, n):
                two_back(act, p1[1], t)
                m = n if n == P else NR
                nc.scalar.activation(hT[p][:, 0:m], cols(bn_in, t * P, m), ACT.Relu, bias=bn_shift, scale=bn_scale)\
                    .then_inc(p1[0].sem, 1)
            tiles(act, f)
            tiles(act, copy_agg(e1[0], agg1, e1[1]))
            root(n1, rstd)
            finished(act, n1[2], 0)

            def f(t, p, n):
                two_back(act, p2[1], t)
                relu_norm(t, hb[p], p2[0])
            tiles(act, f)
            tiles(act, copy_agg(e2[0], agg2, e2[1]))
            root(n2, rstd)
            finished(act, n2[2], 0)

            def h(t, p, n):
                two_back(act, p3[1], t)
                relu_norm(t, hb[p], p3[0])

            def gates(t, p, n):
                finished(act, p3[4], t)
                nc.scalar.activation(gates_io[p], gates_io[p], ACT.Sigmoid)
                nc.scalar.activation(gates_g[p], gates_g[p], ACT.Tanh).then_inc(p3[5].sem, 1)

            def of_cell(t, p, n):
                finished(act, p3[6], t)
                nc.scalar.activation(tmp[p], tmp[p], ACT.Tanh).then_inc(p3[7].sem, 1)
            skewed(act, (4, of_cell), (0, h), (3, gates))
            def copy_bank(s, a, used):
                def f(t, r, n):
                    act.wait_ge(a.banks.sem, a.banks.base + t - r % 4 + 4)
                    two_back(act, used, t)
                    nc.scalar.copy(ag[r % 2][:, 0:n], PS[:, r * P:r * P + n]).then_inc(s.sem, 1)
                return f
            skewed(act, (0, copy_bank(e3[0], agg3, e3[1])), turn=8, ring=8)

            def turned_back(t, r, n):
                finished(act, e4[3], t)
                two_back(act, e4[5], t)
                nc.scalar.copy(hT[r % 2][:, 0:n], misc[4 + r % 2][:, 0:n]).then_inc(e4[4].sem, 1)
            skewed(act, (0, copy_bank(e4[0], agg4, e4[1])), (2, turned_back), turn=8, ring=8)
            root(n4, rstd)
            finished(act, n4[2], 0)

            def f(t, p, n):
                relu_norm(t, tile(H, t), p4[0])
            tiles(act, f)
            skewed(act, (0, copy_bank(e5[0], agg5, e5[1])), turn=8, ring=8)

            def f(t, p, n):
                finished(act, split6[3], t)
                relu_norm(t, tile(H, t), h_again)
            tiles(act, f)
            act.wait_ge(wload["small"], 48)

            def hidden_T(t, r, n):
                finished(act, e6[3], t)
                two_back(act, e6[5], t)
                nc.scalar.copy(hT[r % 2][:, 0:n], misc[4 + r % 2][:, 0:n]).then_inc(e6[4].sem, 1)

            def middle_T(t, r, n):
                finished(act, e6[5], t)
                two_back(act, e6[7], t)
                nc.scalar.activation(tmp[r % 2][:, 0:n], misc[6][:, 0:n], ACT.Identity, bias=b1col, scale=1.0).then_inc(e6[6].sem, 1)
            skewed(act, (0, copy_bank(e6[0], agg6, e6[1])), (2, hidden_T), (4, middle_T), turn=8, ring=8)

        @block.vector
        def _(dve):
            def chain(s):
                done = [0]

                def step(ins):
                    done[0] += 1
                    ins.then_inc(s, 1)
                    dve.wait_ge(s, done[0])
                return step
            link = chain(dve_chain)

            def links(per_tile):
                m = mark("tile_links", per_tile * NT)
                return m.sem, lambda t, k: dve.wait_ge(m.sem, m.base + per_tile * t + k)

            dve.wait_ge(pool_const, 7)
            link(nc.vector.tensor_scalar(ident, iota_w, 0.0, None, ALU.is_equal))
            link(nc.vector.tensor_copy(identb, ident))
            link(nc.vector.tensor_copy(theta, theta_i))
            link(nc.vector.tensor_scalar(theta_nt, theta, float(NT), None, ALU.mult))
            dve.wait_ge(firsts_in, 16)
            nc.vector.tensor_copy(firsts[0:1, 0:NCH], firsts_i[0:1, 0:NCH]).then_inc(firsts_ready, 1)
            dve.wait_ge(firsts_spread, 1)
            link(nc.vector.tensor_copy(firsts_all[:, 0:NCH], PS[:, 7 * BANK:7 * BANK + NCH]))
            for g in range(G):
                link(nc.vector.tensor_scalar(below[:, 0:NCH], firsts_all[:, 0:NCH], theta[:, g:g + 1], 0.0,
                                             ALU.is_lt, ALU.add, accum_out=chunks_below[:, g:g + 1]))
            link(nc.vector.tensor_scalar(row0, chunks_below, float(P // STEP), -float(P // STEP), ALU.mult, ALU.add))
            link(nc.vector.tensor_scalar(row0, row0, 0.0, float(LASTROW), ALU.max, ALU.min))
            nc.vector.tensor_copy(row_i, row0).then_inc(rows_ready, 1)
            link(nc.vector.tensor_scalar(base0, row0, float(STEP), float(E - ROW), ALU.mult, ALU.min))
            dve.wait_ge(gather0, 16 * G)
            gv = gathered.rearrange("p (g k r) -> p g k r", g=G, k=3)
            d3 = dstf.rearrange("p (g r) -> p g r", g=G)
            link(nc.vector.tensor_copy(d3, gv[:, :, 1, :]))
            for g in range(G):
                link(nc.vector.tensor_scalar(below[:, 0:ROW], dstf[:, g * ROW:(g + 1) * ROW], theta[:, g:g + 1], 0.0,
                                             ALU.is_lt, ALU.add, accum_out=fine[:, g:g + 1]))
            link(nc.vector.tensor_tensor(start, base0, fine, ALU.add))
            link(nc.vector.tensor_copy(start_i, start))
            link(nc.vector.tensor_scalar(start_i, start_i, STEP.bit_length() - 1, None, ALU.arith_shift_right))
            link(nc.vector.tensor_copy(row1, start_i))
            link(nc.vector.tensor_scalar(last_or, start, float(E - ROW), float(LASTROW), ALU.is_ge, ALU.mult))
            link(nc.vector.tensor_tensor(row1, row1, last_or, ALU.max))
            link(nc.vector.tensor_scalar(row1, row1, float(LASTROW), None, ALU.min))
            nc.vector.tensor_copy(row1_i, row1).then_inc(rows_ready, 1)
            dve.wait_ge(gather1, 16 * G)
            t3, l3 = tile_i.rearrange("p (g r) -> p g r", g=G), low_i.rearrange("p (g r) -> p g r", g=G)
            link(nc.vector.tensor_copy(d3, gv[:, :, 1, :]))
            link(nc.vector.tensor_scalar(t3, gv[:, :, 0, :], 7, None, ALU.arith_shift_right))
            link(nc.vector.tensor_scalar(l3, gv[:, :, 0, :], P - 1, None, ALU.bitwise_and))
            link(nc.vector.tensor_copy(tilef, tile_i))
            link(nc.vector.tensor_copy(lowf, low_i))
            link(nc.vector.scalar_tensor_tensor(out=codef, in0=dstf, scalar=float(NT), in1=tilef, op0=ALU.mult, op1=ALU.add))
            for g in range(G):
                link(nc.vector.tensor_scalar(codef[:, g * ROW:(g + 1) * ROW], codef[:, g * ROW:(g + 1) * ROW],
                                             theta_nt[:, g:g + 1], None, ALU.subtract))
            link(nc.vector.tensor_scalar(inside, codef, 0.0, None, ALU.is_ge))
            link(nc.vector.scalar_tensor_tensor(out=inside2, in0=codef, scalar=float(CODE), in1=inside, op0=ALU.is_lt, op1=ALU.mult))
            nc.vector.reduce_sum(hits, inside2, mybir.AxisListType.X).then_inc(codes_ready, 1)
            dve.wait_ge(hits_summed, 1)
            nc.vector.tensor_scalar(flag.bitcast(I32)[0:1, :], PS[0:1, 6 * BANK:6 * BANK + 1], float(E), None, ALU.not_equal)\
                .then_inc(flag_ready, 1)
            dve.wait_ge(tables_turned, 1)
            for q, tab in enumerate((t_code, t_src, w_left)):
                for k in range(2):
                    link(nc.vector.tensor_copy(tab[:, k * NW:(k + 1) * NW], PS[:, (2 * q + k) * BANK:(2 * q + k) * BANK + NW]))

            def split_weights(link, parts, left):
                w1, w2, w3 = parts
                link(nc.vector.tensor_copy(w2, left))
                link(nc.vector.tensor_copy(w1, w2))
                link(nc.vector.tensor_tensor(left, left, w1, ALU.subtract))
                link(nc.vector.tensor_copy(w2, left))
                link(nc.vector.tensor_tensor(left, left, w2, ALU.subtract))
                link(nc.vector.tensor_copy(w3, left))
            halves = [m.rearrange("p (h v) -> p h v", h=2) for m in (w_left, t_w1)]
            split_weights(link, [halves[1], t_w23[:, :, 0], t_w23[:, :, 1]], halves[0])

            def place_hots(place, n, code, low, w1):
                dve.wait_ge(slots_used, n + 1)
                for s in range(2):
                    nc.vector.tensor_scalar(hot[place][s], iota[:, 0:P], low[s], None, ALU.is_equal)
                    if s == 0:
                        nc.vector.tensor_scalar(hot_w[place][s][0], iota[:, 0:P], low[s], w1[s], ALU.is_equal, ALU.mult)
                    last = nc.vector.tensor_scalar(code_hot[place][s], iota[:, 0:CODE], code[s], None, ALU.is_equal)
                return last.then_inc(hots_ready, 1)

            def pair_hots(q, j):
                for v in range(2):
                    place_hots(2 * j + v, 2 * q + v, *[[col(tab, s * NW + 2 * q + v) for s in (0, 1)]
                                                     for tab in (t_code, t_src, t_w1)])

            irregular = irregular_flag(dve)
            with dve.If(irregular != 0):
                lks = chain(all_chain)
                lks(nc.vector.memset(zerosb, 0.0))
                lks(nc.vector.memset(list_i, -1))
                lks(nc.vector.memset(list_w, 0.0))
                nc.vector.memset(hits, 0.0).then_inc(tables_ready, 1)
                dve.wait_ge(list_in, 16 * 3 * (2 if E % P else 1))
                lks(nc.vector.tensor_copy(l_dst, list_i[:, 0:NCP]))
                lks(nc.vector.tensor_scalar(list_t, list_i[:, NCP:2 * NCP], 7, None, ALU.arith_shift_right))
                lks(nc.vector.tensor_copy(l_src, list_t))
                lks(nc.vector.scalar_tensor_tensor(out=l_code, in0=l_dst, scalar=float(NT), in1=l_src, op0=ALU.mult, op1=ALU.add))
                lks(nc.vector.tensor_scalar(list_t, list_i[:, NCP:2 * NCP], P - 1, None, ALU.bitwise_and))
                lks(nc.vector.tensor_copy(l_src, list_t))
                split_weights(lks, [l_w1, l_w23[:, :, 0], l_w23[:, :, 1]], list_w)
                nc.vector.memset(rest_stage, 0.0).then_inc(list_ready, 1)

                def pair_of_all(q, j):
                    for v in range(2):
                        win = 2 * q + v
                        with dve.Fori(0, NCB) as i:
                            dve.wait_ge(shifted, win + 1)
                            for r in range(4):
                                place_hots(r, (4 * NCB) * win + 4 * i + r + win,
                                           *[[col(tab, 8 * i + 2 * r + s) for s in (0, 1)] for tab in (l_code, l_src, l_w1)])
                        dve.wait_ge(hots_ready, 4 * NCB * (win + 1))
                        nc.vector.tensor_scalar(l_code, l_code, float(CODE), None, ALU.subtract).then_inc(shifted, 1)
                    dve.wait_ge(pairs_out, 2 + q + 1)
                    dve.wait_ge(rest_free, q + 1)
                    r = rest_stage.rearrange("p (a v d) -> p v a d", a=NT, v=2)
                    full = PS[:, 2 * j * BANK:2 * (j + 1) * BANK].rearrange("p (v c) -> p v c", v=2)[:, :, CODE:2 * CODE]
                    kept = C.rearrange("p (a d) -> p a d", a=NT)[:, :, ds(q * 2 * V, 2 * V)]
                    for v in range(2):
                        last = nc.vector.tensor_tensor(r[:, v], full[:, v].rearrange("p (d a) -> p a d", d=V),
                                                       kept[:, :, v * V:(v + 1) * V], ALU.subtract)
                    last.then_inc(rest_out, 1)
                build_tiles(dve, lambda t, p: pair_loop(dve, t, 0, pair_of_all))
                with dve.Fori(0, NT) as t:
                    with dve.Fori(0, NCB) as i:
                        dve.wait_ge(shifted, NW + t + 1)
                        for r in range(4):
                            dve.wait_ge(slots_used, (NW + t) * (4 * NCB + 1) + 4 * i + r + 1)
                            for s in range(2):
                                last = nc.vector.tensor_scalar(hot[r][s], iota[:, 0:P], col(l_dst, 8 * i + 2 * r + s), None, ALU.is_equal)
                            last.then_inc(hots_ready, 1)
                    dve.wait_ge(hots_ready, 4 * NCB * (NW + t + 1))
                    nc.vector.tensor_scalar(l_dst, l_dst, float(P), None, ALU.subtract).then_inc(shifted, 1)
            with dve.Else():
                nc.vector.memset(zerosb, 0.0).then_inc(tables_ready, 1)
                build_tiles(dve, lambda t, p: pair_loop(dve, t, 0, pair_hots))

            def tile_stats(t):
                return nc.vector.bn_stats(cols(stat6, 6 * t, 6), tile(X, t))

            dve.wait_ge(stage_saved[1], 16 * (NT // 2))
            dve.wait_ge(tile_turned, 2 + NT - 1)
            s0, linked0 = links(1)
            dve.wait_ge(x_in, 32)
            tiles(dve, lambda t, p, n: tile_stats(t).then_inc(s0, 1))

            dve.wait_ge(root_ready, 1)

            link(nc.vector.tensor_scalar(rcount, count, 1.0, None, ALU.max))
            link(nc.vector.reciprocal(rcount, rcount))
            link(nc.vector.reciprocal(dinv, dinv))
            link(nc.vector.tensor_scalar(half_dinv, dinv, 0.5, None, ALU.mult))

            def norm_params(s):
                st = stat6.rearrange("p (t k) -> p t k", k=6)
                mean, var = mv[:, 0:NT], mv[:, NT:2 * NT]
                link(nc.vector.tensor_tensor(nmr, st[:, :, 1], st[:, :, 4], ALU.subtract))
                link(nc.vector.tensor_tensor(mean, st[:, :, 1], st[:, :, 4], ALU.add))
                link(nc.vector.tensor_tensor(var, st[:, :, 2], st[:, :, 5], ALU.add))
                link(nc.vector.scalar_tensor_tensor(out=nmr, in0=nmr, scalar=0.25, in1=nmr, op0=ALU.mult, op1=ALU.mult))
                link(nc.vector.scalar_tensor_tensor(out=var, in0=var, scalar=1.0 / D, in1=nmr, op0=ALU.mult, op1=ALU.add))
                nc.vector.tensor_scalar(rstd, var, EPS, None, ALU.add).then_inc(s[0].sem, 1)
                finished(dve, s[1], 0)
                link(nc.vector.reciprocal(rstd, rstd))
                nc.vector.scalar_tensor_tensor(out=nmr, in0=mean, scalar=-0.5, in1=rstd, op0=ALU.mult, op1=ALU.mult)\
                    .then_inc(s[2].sem, 1)

            linked0(NT - 1, 1)
            norm_params(n0)
            dve.wait_ge(wload["p0"], 32)

            def hT_of(s, bank=0):
                def f(t, p, n):
                    finished(dve, s[0], t)
                    two_back(dve, s[2], t)
                    nc.vector.tensor_copy(hT[p], misc[bank + p]).then_inc(s[1].sem, 1)
                return f

            def f(t, p, n):
                finished(dve, p0[3], t)
                nc.vector.tensor_tensor(tile(X, t), misc[2 + p], b[0], ALU.add).then_inc(p0[4].sem, 1)
            skewed(dve, (1, hT_of(p0[1:4])), (3, f))

            evacuate(dve, nc.vector.tensor_copy, agg0, H, 1)

            def f(t, p, n):
                finished(dve, e0[1], t)
                two_back(dve, e0[3], t)
                nc.vector.scalar_tensor_tensor(out=hb[p][0:n], in0=misc[p][0:n], scalar=col(rcount, t)[0:n],
                                               in1=tile(X, t)[0:n], op0=ALU.mult, op1=ALU.add).then_inc(e0[2].sem, 1)
            tiles(dve, f)
            finished(dve, e0[4], NT - 1)
            pieces = [(c, min(BANK, N - c)) for c in range(0, N, BANK)]
            for i, (c, m) in enumerate(pieces):
                ins = nc.vector.bn_stats(stat6[:, 6 * i:6 * i + 6], bn_in[:, c:c + m])
            link(ins)
            link(nc.vector.bn_aggr(bn_mv, stat6[:, 0:6 * len(pieces)]))
            nc.vector.tensor_scalar(bn_scale, bn_mv[:, 1:2], EPS, None, ALU.add).then_inc(bn_var, 1)
            dve.wait_ge(bn_root, 1)
            dve.wait_ge(wload["small"], 48)
            link(nc.vector.reciprocal(bn_scale, bn_scale))
            link(nc.vector.tensor_tensor(bn_scale, bn_scale, gamma, ALU.mult))
            link(nc.vector.tensor_tensor(bn_shift, bn_mv[:, 0:1], bn_scale, ALU.mult))
            nc.vector.tensor_tensor(bn_shift, beta, bn_shift, ALU.subtract).then_inc(bn_ready, 1)
            dve.wait_ge(p1_x, 32)
            dve.wait_ge(wload["p1"], 32)
            dve.wait_ge(h_cleared, 2)

            def f(t, p, n):
                m = n if n == P else NR
                finished(dve, p1[1], t)
                nc.vector.tensor_copy(tile(H, t)[0:m], misc[p][0:m])
                nc.vector.tensor_tensor(tile(X, t)[0:m], misc[2 + p][0:m], tile(X, t)[0:m], ALU.add).then_inc(p1[3].sem, 1)

            def biased(t, p, n):
                finished(dve, p1[3], t)
                nc.vector.tensor_tensor(tile(X, t), tile(X, t), b[1], ALU.add).then_inc(p1[2].sem, 1)
            skewed(dve, (0, f), (1, biased))

            evacuate(dve, nc.vector.tensor_copy, agg1, H, 1)

            def stats_of(s):
                def f(t, p, n):
                    finished(dve, s[0], t)
                    tile_stats(t).then_inc(s[1].sem, 1)
                return f

            def f(t, p, n):
                finished(dve, e1[1], t)
                nc.vector.scalar_tensor_tensor(out=tile(X, t)[0:n], in0=misc[p][0:n], scalar=col(rcount, t)[0:n],
                                               in1=tile(X, t)[0:n], op0=ALU.mult, op1=ALU.add).then_inc(e1[3].sem, 1)
            skewed(dve, (0, f), (1, stats_of([e1[3], e1[2]])))
            finished(dve, e1[2], NT - 1)
            norm_params(n1)
            dve.wait_ge(wload["p2"], 32)

            def f(t, p, n):
                finished(dve, p2[3], t)
                nc.vector.tensor_tensor(tile(H, t), misc[2 + p], b[2], ALU.add).then_inc(p2[4].sem, 1)
            skewed(dve, (1, hT_of(p2[1:4])), (3, f))

            evacuate(dve, nc.vector.tensor_copy, agg2, H, 1)

            def f(t, p, n):
                finished(dve, e2[1], t)
                nc.vector.tensor_tensor(tile(X, t)[0:n], misc[p][0:n], tile(X, t)[0:n], ALU.add).then_inc(e2[3].sem, 1)
            skewed(dve, (0, f), (1, stats_of([e2[3], e2[2]])))
            finished(dve, e2[2], NT - 1)
            norm_params(n2)
            agg_end(dve, agg2)
            nc.vector.memset(zeros, 0.0).then_inc(gate_bias, 1)
            dve.wait_ge(wload["bias3"], 32)
            nc.vector.tensor_tensor(bslot, bihh[:, 0:3 * P], bihh[:, 3 * P:6 * P], ALU.add).then_inc(gate_bias, 1)
            dve.wait_ge(gate_bias, 2)
            dve.wait_ge(gate_prod, 1)
            nc.vector.tensor_tensor(bslot, bslot, gate_prod_out, ALU.add).then_inc(gate_ready, 1)
            dve.wait_ge(gate_ready, 1)

            def split_high(u, t):
                return nc.vector.tensor_copy(part(0, t), u)

            def split_rest(u, t):
                return nc.vector.tensor_tensor(u, u, part(0, t), ALU.subtract)

            def split_middle(u, t):
                return nc.vector.tensor_copy(part(1, t), u)

            def split_low(u, t):
                return nc.vector.tensor_tensor(part(2, t), u, part(1, t), ALU.subtract)

            s3, linked3 = links(4)

            def gate_io(t, p, n):
                finished(dve, p3[3], t)
                nc.vector.tensor_tensor(gates_io[p], gates_out[p][:, 0:2 * P], bslot[:, 0:2 * P], ALU.add)

            def gate_g(t, p, n):
                nc.vector.tensor_tensor(gates_g[p], gates_out[p][:, 2 * P:3 * P], bslot[:, 2 * P:3 * P], ALU.add)\
                    .then_inc(p3[4].sem, 1)

            def cell(t, p, n):
                finished(dve, p3[5], t)
                two_back(dve, p3[8], t)
                nc.vector.tensor_tensor(tmp[p], gates_io[p][:, 0:P], gates_g[p], ALU.mult).then_inc(p3[6].sem, 1)

            def hidden(t, p, n):
                finished(dve, p3[7], t)
                nc.vector.scalar_tensor_tensor(out=tmp[p], in0=tmp[p], scalar=col(dinv, t), in1=gates_io[p][:, P:2 * P],
                                               op0=ALU.mult, op1=ALU.mult).then_inc(s3, 1)

            def high(t, p, n):
                linked3(t, 1)
                split_high(tmp[p], t).then_inc(s3, 1)

            def rest(t, p, n):
                linked3(t, 2)
                split_rest(tmp[p], t).then_inc(s3, 1)

            def middle(t, p, n):
                linked3(t, 3)
                split_middle(tmp[p], t).then_inc(s3, 1)

            def low(t, p, n):
                linked3(t, 4)
                split_low(tmp[p], t).then_inc(p3[8].sem, 1)
            skewed(dve, (4, cell), (5, hidden), (1, hT_of(p3[1:4], 2)), (5, high), (3, gate_io), (3, gate_g), (5, rest),
                   (5, middle), (5, low))

            dve.wait_ge(wload["e3"], 32)

            def f(t, p, n):
                finished(dve, e3[1], t)
                two_back(dve, e3[2], t)
                nc.vector.scalar_tensor_tensor(out=tmp[p][0:n], in0=misc[2 + p][0:n], scalar=col(dinv, t)[0:n],
                                               in1=b[0][0:n], op0=ALU.mult, op1=ALU.add).then_inc(e3[3].sem, 1)

            def next_operand(t, p, n):
                finished(dve, e3[3], t)
                nc.vector.tensor_scalar(tile(H, t), tmp[p], 0.0, col(dinv, t), ALU.max, ALU.mult).then_inc(e3[2].sem, 1)
            skewed(dve, (0, f), (1, next_operand))

            def split_H(a, high, rest, middle, low, ready=None, scaled=False):
                every_bank(dve, a)

                def f_high(t, p, n):
                    if ready:
                        finished(dve, ready, t)
                    if scaled:
                        nc.vector.tensor_scalar(part(0, t), tile(H, t), col(dinv, t), None, ALU.mult).then_inc(high.sem, 1)
                    else:
                        split_high(tile(H, t), t).then_inc(high.sem, 1)

                def f_rest(t, p, n):
                    finished(dve, high, t)
                    two_back(dve, low, t)
                    if scaled:
                        nc.vector.scalar_tensor_tensor(out=tmp[p], in0=tile(H, t), scalar=col(dinv, t), in1=part(0, t),
                                                       op0=ALU.mult, op1=ALU.subtract).then_inc(rest.sem, 1)
                    else:
                        nc.vector.tensor_tensor(tmp[p], tile(H, t), part(0, t), ALU.subtract).then_inc(rest.sem, 1)

                def f_middle(t, p, n):
                    finished(dve, rest, t)
                    split_middle(tmp[p], t).then_inc(middle.sem, 1)

                def f_low(t, p, n):
                    finished(dve, middle, t)
                    split_low(tmp[p], t).then_inc(low.sem, 1)
                skewed(dve, (1, f_rest), (2, f_low), (0, f_high), (1, f_middle))
                finished(dve, low, NT - 1)
            finished(dve, e3[2], NT - 1)
            split_H(agg3, *split4)

            dve.wait_ge(wload["e4"], 48)

            s, linked = links(1)

            def f(t, p, n):
                finished(dve, e4[1], t)
                two_back(dve, e4[3], t)
                nc.vector.scalar_tensor_tensor(out=hb[p][0:n], in0=misc[2 + p][0:n], scalar=col(dinv, t)[0:n], in1=b[1][0:n],
                                               op0=ALU.mult, op1=ALU.add).then_inc(e4[2].sem, 1)

            def biased(t, p, n):
                finished(dve, e4[5], t)
                nc.vector.tensor_tensor(tmp[p][0:n], misc[6 + p][0:n], b[2][0:n], ALU.add).then_inc(e4[7].sem, 1)

            def added(t, p, n, s=s):
                finished(dve, e4[7], t)
                nc.vector.scalar_tensor_tensor(out=tile(X, t)[0:n], in0=tmp[p][0:n], scalar=0.0, in1=tile(X, t)[0:n],
                                               op0=ALU.max, op1=ALU.add).then_inc(s, 1)

            def stats(t, p, n, linked=linked):
                linked(t, 1)
                tile_stats(t).then_inc(e4[6].sem, 1)
            skewed(dve, (0, f), (4, added), (3, biased), (4, stats))
            finished(dve, e4[6], NT - 1)
            norm_params(n4)

            split_H(agg4, *split5, ready=p4[0], scaled=True)

            def f(t, p, n):
                finished(dve, e5[1], t)
                two_back(dve, e5[2], t)
                nc.vector.scalar_tensor_tensor(out=tmp[p][0:n], in0=misc[2 + p][0:n], scalar=col(dinv, t)[0:n],
                                               in1=tile(H, t)[0:n], op0=ALU.mult, op1=ALU.add).then_inc(e5[3].sem, 1)

            def next_operand(t, p, n):
                finished(dve, e5[3], t)
                nc.vector.tensor_scalar(tile(H, t), tmp[p], col(half_dinv, t), None, ALU.mult).then_inc(e5[2].sem, 1)
            skewed(dve, (0, f), (1, next_operand))
            finished(dve, e5[2], NT - 1)
            split_H(agg5, *split6)

            dve.wait_ge(wload["e6b"], 16)

            def mixed(t, p, n):
                finished(dve, e6[1], t)
                finished(dve, h_again, t)
                two_back(dve, e6[3], t)
                nc.vector.scalar_tensor_tensor(out=hb[p][0:n], in0=misc[2 + p][0:n], scalar=col(dinv, t)[0:n], in1=tile(H, t)[0:n],
                                               op0=ALU.mult, op1=ALU.add).then_inc(e6[9].sem, 1)

            def relu_half(t, p, n):
                finished(dve, e6[9], t)
                nc.vector.tensor_scalar(hb[p][0:n], hb[p][0:n], 0.5, 0.0, ALU.mult, ALU.max).then_inc(e6[2].sem, 1)

            def added(t, p, n):
                finished(dve, e6[7], t)
                nc.vector.tensor_tensor(tile(X, t)[0:n], misc[7][0:n], tile(X, t)[0:n], ALU.add).then_inc(e6[10].sem, 1)

            def biased(t, p, n):
                finished(dve, e6[10], t)
                nc.vector.tensor_tensor(tile(X, t)[0:n], tile(X, t)[0:n], b[0][0:n], ALU.add).then_inc(e6[8].sem, 1)
            skewed(dve, (1, relu_half), (6, added), (7, biased), (0, mixed))

        @block.tensor
        def _(pe):
            mm = nc.tensor.matmul
            pe.wait_ge(firsts_ready, 1)
            mm(PS[:, 7 * BANK:7 * BANK + NCH], onesrow[0:1, :], firsts[0:1, 0:NCH], start=True, stop=True).then_inc(firsts_spread, 1)
            pe.wait_ge(codes_ready, 1)
            mm(PS[:, 6 * BANK:6 * BANK + 1], onesrow, hits, start=True, stop=True).then_inc(hits_summed, 1)
            wg = gathered.bitcast(F32)
            for g in range(G):
                for k in range(2):
                    for q, s in enumerate((codef, lowf, wg)):
                        c = g * ROW + k * P if q < 2 else g * 3 * ROW + 2 * ROW + k * P
                        last = nc.tensor.transpose(PS[:, (2 * q + k) * BANK + g * P:(2 * q + k) * BANK + (g + 1) * P],
                                                   s[:, c:c + P], ident)
            last.then_inc(tables_turned, 1)
            irregular = irregular_flag(pe)
            pe.wait_ge(tables_ready, 1)

            def bank_of(j, v):
                return PS[:, (2 * j + v) * BANK:(2 * j + v) * BANK + 2 * CODE]

            def add_place(place, n, out, alone):
                pe.wait_ge(hots_ready, n + 1)
                for s in range(2):
                    mm(out[:, CODE:2 * CODE], hot[place][s], code_hot[place][s], start=alone and s == 0,
                       stop=alone and s == 1)
                for s, k in ((0, 0), (1, 0), (0, 1), (0, 2), (1, 1), (1, 2)):
                    if (s, k) == (1, 0):
                        pe.wait_ge(w1_ready, n + 1)
                    if (s, k) == (0, 1):
                        pe.wait_ge(scaled_ready, n + 1)
                    last = mm(out[:, 0:CODE], hot_w[place][s][k], code_hot[place][s], start=False,
                              stop=alone and (s, k) == (1, 2), skip_group_check=True)
                return last.then_inc(slots_used, 1)

            def pair(q, j):
                pe.wait_ge(pairs_out, q + 1)
                for v in range(2):
                    add_place(2 * j + v, 2 * q + v, bank_of(j, v), True)

            def pair_all(q, j):
                pe.wait_ge(pairs_out, q + 1)
                for v in range(2):
                    mm(bank_of(j, v), zerosb[:, 0:P], zerosb[:, 0:2 * CODE], start=True, stop=False)
                    base = (2 * q + v) * NCB * 4
                    with pe.Fori(0, NCB) as i:
                        for r in range(4):
                            add_place(r, base + 4 * i + r, bank_of(j, v), False)
                    mm(bank_of(j, v), zerosb[:, 0:P], zerosb[:, 0:2 * CODE], start=False, stop=True).then_inc(slots_used, 1)
                pe.wait_ge(rest_out, q + 1)

            def turn_group(t, p, g, with_counts):
                n = LC if isinstance(t, int) and t == NT - 1 else P
                if g == 0:
                    pe.wait_ge(pairs_out, 2 + pairs_before(t) + pairs_in(t))
                    if with_counts:
                        for a in range(NT):
                            last = mm(PS[0:1, 7 * BANK:7 * BANK + n], onesb[:, 0:1], cols(C, a * NC + t * P, n),
                                      start=(a == 0), stop=(a == NT - 1))
                        last.then_inc(row_ready, 1)
                before = NG * t + max(g - 1, 0)
                if not isinstance(t, int) or before > 0:
                    pe.wait_ge(turned_out, before)
                for a in range(4 * g, min(4 * g + 4, NT)):
                    last = nc.tensor.transpose(PS[0:n, (4 + g % 2) * BANK + (a % 4) * P:(4 + g % 2) * BANK + (a % 4 + 1) * P],
                                               staged[p][:, a * P:a * P + n], ident)
                last.then_inc(turned, 1)
                if g == NG - 1 and with_counts:
                    pe.wait_ge(row_out, t + 1)
                    mm(col(PS, 6 * BANK + t)[0:n], degree_row[0:1, 0:n], ones[0:1, 0:1], start=True, stop=True)\
                        .then_inc(tile_turned, 1)
                elif g == NG - 1:
                    mm(PS[:, 7 * BANK:7 * BANK + 1], zerosb[:, 0:P], zerosb[:, 0:1], start=True, stop=True).then_inc(tile_turned, 1)

            def build_tile(t, p, pair_body, with_counts):
                pairs_and_groups(t, lambda q, k: pair_body(q, k % 2), lambda t, g: turn_group(t, 1 - p, g, with_counts))

            with pe.If(irregular != 0):
                build_tiles(pe, lambda t, p: build_tile(t, p, pair_all, False))
                for g in range(NG):
                    turn_group(NT - 1, 0, g, False)
                with pe.Fori(0, NT) as t:
                    mm(col(PS, 6 * BANK + t), zerosb[:, 0:P], zerosb[:, 0:1], start=True, stop=False)
                    with pe.Fori(0, NCB) as i:
                        for r in range(4):
                            pe.wait_ge(hots_ready, (NW + t) * NCB * 4 + 4 * i + r + 1)
                            for s in range(2):
                                last = mm(col(PS, 6 * BANK + t), hot[r][s], onesb[:, 0:1], start=False, stop=False)
                            last.then_inc(slots_used, 1)
                    mm(col(PS, 6 * BANK + t), zerosb[:, 0:P], zerosb[:, 0:1], start=False, stop=True).then_inc(slots_used, 1)
                mm(PS[:, 7 * BANK:7 * BANK + 1], zerosb[:, 0:P], zerosb[:, 0:1], start=True, stop=True).then_inc(counted, 1)
            with pe.Else():
                build_tiles(pe, lambda t, p: build_tile(t, p, pair, True))
                for g in range(NG):
                    turn_group(NT - 1, 0, g, True)
                mm(PS[:, 7 * BANK:7 * BANK + 1], ident, ones, start=True, stop=True).then_inc(counted, 1)

            def run_fp32(a, k_last, before):
                for s in before:
                    finished(pe, s, NT - 1)

                def one(t, turn, j, start, stop, k):
                    finished(pe, a.stat, t)
                    for h, (c, m) in enumerate(HALVES):
                        u = 2 * j + h
                        pe.wait_ge(a.loaded[u % 3].sem, a.loaded[u % 3].base + 16 * (2 * turn + u // 3 + 1))
                        for c1 in range(0, m, BANK):
                            w_ = min(BANK, m - c1)
                            last = mm(agg[:, c + c1:c + c1 + w_], stationary[j][0:k], stream[u % 3][0:k, c1:c1 + w_],
                                      start=start, stop=stop)
                        last.then_inc(a.units.sem, 1)
                for j in range(3):
                    one(j, 0, j, j == 0, False, P)
                with pe.Fori(1, NT // 3) as i:
                    for j in range(3):
                        one(3 * i + j, i, j, False, False, P)
                one(NT - 1, NT // 3, 0, False, True, k_last)
                mm(misc[7][:, 0:1], ident, ones, start=True, stop=True).then_inc(a.done.sem, 1)

            def counts_of_tile(t, c, ready):
                c0, m = BANKS[c]
                if c == 0:
                    finished(pe, ready, t)
                for k in range(3):
                    mm(PS[:, c % 2 * BANK:c % 2 * BANK + m], part(k, t), cols(C, t * NC + c0, m),
                       start=isinstance(t, int) and t == 0 and k == 0, stop=False)

            def run_counts(a, ready, copied, steps):
                step, most = steps
                fourths = [NT * j // 4 for j in range(5)]
                for c, (c0, m) in enumerate(BANKS):
                    out = PS[:, c % 2 * BANK:c % 2 * BANK + m]
                    if c >= 2:
                        finished(pe, copied, 4 * (c - 2) + 3)

                    for j in range(4):
                        if c >= 1 or ready:
                            for t in range(fourths[j], fourths[j + 1]):
                                counts_of_tile(t, c, ready)
                        if c >= 1:
                            step(4 * (c - 1) + j)
                    with pe.If(irregular != 0):
                        with pe.Fori(0, NT) as t:
                            pe.wait_ge(a.rest_loaded.sem, a.rest_loaded.base + 16 * (c * NT + t + 1))
                            for k in range(3):
                                last = mm(out, part(k, t), rest_in[:, 0:m], start=False, stop=False)
                            last.then_inc(a.rest_used.sem, 1)
                    for t in range(4 * c, min(4 * c + 4, NT)):
                        n = LC if t == NT - 1 else P
                        for k in range(3):
                            last = mm(out[:, t % 4 * P:t % 4 * P + n], part(k, t), identb[:, 0:n], start=False,
                                      stop=k == 2 and (t % 4 == 3 or t == NT - 1))
                    last.then_inc(a.banks.sem, 4)
                for s in range(4 * (NB - 1), NT + most):
                    step(s)

            def product(t, p, n, operand, operand_done, weight, dest, done, free):
                finished(pe, operand_done, t)
                two_back(pe, free, t)
                mm(misc[dest + p][0:n], operand[p][:, 0:n], weight, start=True, stop=True).then_inc(done.sem, 1)

            def turn(t, p, n, operand, operand_done, dest, done, free):
                finished(pe, operand_done, t)
                two_back(pe, free, t)
                nc.tensor.transpose(misc[dest + p][:, 0:n], operand[p][0:n, :], ident[0:n, 0:n]).then_inc(done.sem, 1)

            def turn_back(t, p, n, operand, operand_done, dest, done, free):
                finished(pe, operand_done, t)
                two_back(pe, free, t)
                nc.tensor.transpose(misc[dest + p][0:n, :], operand[p][:, 0:n], ident).then_inc(done.sem, 1)

            pe.wait_ge(wload["p0"], 32)

            def norm_product(s, weight):
                skewed(pe, (0, lambda t, p, n: turn(t, p, P, hb, s[0], 0, s[1], s[2])),
                       (2, lambda t, p, n: product(t, p, P, hT, s[2], weight, 2, s[3], s[4])))
            norm_product(p0, w[0])
            run_fp32(agg0, P, [p0[4]])
            pe.wait_ge(wload["e0"], 16)

            skewed(pe, (0, lambda t, p, n: product(t, p, n, ag, e0[0], w[1], 0, e0[1], e0[2])),
                   (2, lambda t, p, n: turn(t, p, n, hb, e0[2], 2, e0[3], e0[4])))
            pe.wait_ge(wload["p1"], 32)

            def f(t, p, n):
                m = n if n == P else NR
                finished(pe, p1[0], t)
                two_back(pe, p1[3], t)
                nc.tensor.transpose(misc[p][0:m, :], hT[p][:, 0:m], ident)
                mm(misc[2 + p][0:m], hT[p][:, 0:m], w[2], start=True, stop=True).then_inc(p1[1].sem, 1)
            tiles(pe, f)
            run_fp32(agg1, P, [p1[2]])
            pe.wait_ge(wload["e1"], 16)
            tiles(pe, lambda t, p, n: product(t, p, n, ag, e1[0], w[0], 0, e1[1], e1[3]))
            pe.wait_ge(wload["p2"], 32)

            norm_product(p2, w[1])
            run_fp32(agg2, LC, [p2[4]])
            tiles(pe, lambda t, p, n: turn_back(t, p, n, ag, e2[0], 0, e2[1], e2[3]))
            pe.wait_ge(gate_bias, 2)
            mm(gate_prod_out, zeros, whh, start=True, stop=True).then_inc(gate_prod, 1)
            pe.wait_ge(wload["p3"], 16)

            def f(t, p, n):
                finished(pe, p3[2], t)
                two_back(pe, p3[4], t)
                mm(gates_out[p], hT[p], wslot, start=True, stop=True).then_inc(p3[3].sem, 1)
            skewed(pe, (0, lambda t, p, n: turn(t, p, P, hb, p3[0], 2, p3[1], p3[2])), (2, f),
                   (7, lambda t, p, n: counts_of_tile(t, 0, p3[8])))
            pe.wait_ge(wload["e3"], 32)
            run_counts(agg3, None, e3[0], steps_of((0, lambda t, p, n: product(t, p, n, ag, e3[0], w[0], 2, e3[1], e3[3]))))
            pe.wait_ge(wload["e4"], 48)
            run_counts(agg4, split4[3], e4[0], steps_of(
                (0, lambda t, p, n: product(t, p, n, ag, e4[0], w[1], 2, e4[1], e4[2])),
                (1, lambda t, p, n: turn(t, p, n, hb, e4[2], 4, e4[3], e4[4])),
                (3, lambda t, p, n: product(t, p, n, hT, e4[4], w[2], 6, e4[5], e4[7]))))
            run_counts(agg5, split5[3], e5[0], steps_of((0, lambda t, p, n: turn_back(t, p, n, ag, e5[0], 2, e5[1], e5[3]))))
            pe.wait_ge(wload["e6a"], 16)

            def middle(t, p, n):
                finished(pe, e6[4], t)
                one_back(pe, e6[6], t)
                mm(misc[6][:, 0:n], w[0], hT[p][:, 0:n], start=True, stop=True).then_inc(e6[5].sem, 1)

            def last_product(t, p, n):
                finished(pe, e6[6], t)
                one_back(pe, e6[10], t)
                mm(misc[7][0:n], tmp[p][:, 0:n], w[1], start=True, stop=True).then_inc(e6[7].sem, 1)
            run_counts(agg6, split6[3], e6[0], steps_of(
                (0, lambda t, p, n: turn_back(t, p, n, ag, e6[0], 2, e6[1], e6[9])),
                (1, lambda t, p, n: turn(t, p, n, hb, e6[2], 4, e6[3], e6[4])), (3, middle), (5, last_product)))


_W = ["W1r", "W1l", "W2r", "W2l", "L1W", "Wih_i", "Wih_o", "Wih_g", "Whh_i", "Whh_o", "Whh_g", "W1", "W2", "W3", "w1", "w2"]
_B = ["b1l", "b2l", "L1b", "bih_i", "bih_o", "bih_g", "bhh_i", "bhh_o", "bhh_g", "b1", "b2", "b3", "w2b"]


def kernel(x, src, dst, edge_weight, L0_gnn_W1l, L0_gnn_b1l, L0_gnn_W1r, L0_gnn_bn_gamma, L0_gnn_bn_beta, L0_gnn_W2l,
           L0_gnn_b2l, L0_gnn_W2r, L1_gnn_W, L1_gnn_b, L2_gnn_W_ih, L2_gnn_W_hh, L2_gnn_b_ih, L2_gnn_b_hh, L2_gnn_W1,
           L2_gnn_b1, L2_gnn_W2, L2_gnn_b2, L2_gnn_W3, L2_gnn_b3, L3_gnn_w1, L3_gnn_b1, L3_gnn_w2, L3_gnn_b2):
    import numpy as _np
    import concourse.bacc as _bacc
    from concourse.bass_utils import run_bass_kernel_spmd as _run

    D = x.shape[1]

    def gate(a, k):
        return _np.asarray(a)[k * D:(k + 1) * D]

    by_name = {"W1r": _np.asarray(L0_gnn_W1r).T, "W1l": _np.asarray(L0_gnn_W1l).T, "W2r": _np.asarray(L0_gnn_W2r).T,
               "W2l": _np.asarray(L0_gnn_W2l).T, "L1W": _np.asarray(L1_gnn_W), "W1": _np.asarray(L2_gnn_W1),
               "W2": _np.asarray(L2_gnn_W2), "W3": _np.asarray(L2_gnn_W3).T, "w1": _np.asarray(L3_gnn_w1).T,
               "w2": _np.asarray(L3_gnn_w2).T}
    rows = {"b1l": L0_gnn_b1l, "b2l": L0_gnn_b2l, "L1b": L1_gnn_b, "b1": L2_gnn_b1, "b2": L2_gnn_b2, "b3": L2_gnn_b3,
            "w2b": L3_gnn_b2}
    for name, k in (("i", 0), ("g", 2), ("o", 3)):
        by_name["Wih_" + name] = gate(L2_gnn_W_ih, k).T
        by_name["Whh_" + name] = gate(L2_gnn_W_hh, k).T
        rows["bih_" + name] = gate(L2_gnn_b_ih, k)
        rows["bhh_" + name] = gate(L2_gnn_b_hh, k)
    arrays = {
        "in_x": _np.ascontiguousarray(x),
        "in_src": _np.ascontiguousarray(src),
        "in_dst": _np.ascontiguousarray(dst),
        "in_edge_weight": _np.ascontiguousarray(edge_weight),
        "in_weights": _np.ascontiguousarray(_np.concatenate([by_name[n] for n in _W], axis=1)),
        "in_biases": _np.ascontiguousarray(_np.stack([_np.asarray(rows[n]) for n in _B])),
        "in_columns": _np.ascontiguousarray(_np.stack([_np.asarray(a) for a in (L0_gnn_bn_gamma, L0_gnn_bn_beta, L3_gnn_b1)], axis=1)),
    }
    nc = _bacc.Bacc("TRN2", target_bir_lowering=False, num_devices=1)
    t = {k: nc.dram_tensor(k, a.shape, mybir.dt.from_np(a.dtype), kind="ExternalInput").ap() for k, a in arrays.items()}
    out = nc.dram_tensor("out", x.shape, F32, kind="ExternalOutput").ap()
    gnn_blocks(nc, t["in_x"], t["in_src"], t["in_dst"], t["in_edge_weight"], t["in_weights"],
               {n: i for i, n in enumerate(_W)}, t["in_biases"], {n: i for i, n in enumerate(_B)}, t["in_columns"], out)
    r = _run(nc, [arrays], core_ids=[0])
    return r.results[0]["out"]
```
